# Optimizing a Trainium2 kernel written in Bass

```python
import numpy as np
import jax
import jax.numpy as jnp

def _softmax(x, axis=-1):
    return jax.nn.softmax(x, axis=axis)

def _gelu(x):
    return jax.nn.gelu(x, approximate=True)

def _silu(x):
    return jax.nn.silu(x)

def _sigmoid(x):
    return jax.nn.sigmoid(x)

def _layernorm(x, axis=-1, eps=1e-05):
    m = jnp.mean(x, axis=axis, keepdims=True)
    v = jnp.var(x, axis=axis, keepdims=True)
    return (x - m) / jnp.sqrt(v + eps)

def _scatter_add(tgt, idx, src, axis=0):
    return tgt.at[idx].add(src)

def _segment_sum(src, seg, n):
    return jax.ops.segment_sum(src, seg, n)
kernel_name = 'mk_flamingo_gated_d4_seqx_r8_9b8439'

def setup_inputs(seed: int=0):
    np.random.seed(seed)
    _w = jnp.asarray

    def _rec_inputs():
        import jax
        import jax.numpy as jnp
        _rk = jax.random.key(seed)
        x = -0.0002928 + 1 * jax.random.normal(jax.random.fold_in(_rk, 1), (4, 256, 128), jnp.float32)
        _lenS = 256 - jax.random.randint(jax.random.fold_in(_rk, 7), (4,), 0, max(1, 256 // 4) + 1, jnp.int32)
        _lenS2 = 256 - jax.random.randint(jax.random.fold_in(_rk, 8), (4,), 0, max(1, 256 // 4) + 1, jnp.int32)
        _ctx_1024P = jax.random.normal(jax.random.fold_in(_rk, 11), (4, 16, 128), jnp.float32)
        _ctx_1024c = jax.random.dirichlet(jax.random.fold_in(_rk, 511), 0.3 * jnp.ones((16,), jnp.float32), (4, 256))
        _ctx_1024t = jnp.einsum('bsk,bkd->bsd', _ctx_1024c, _ctx_1024P)
        _ctx_1024t = _ctx_1024t * jax.lax.rsqrt(jnp.mean(jnp.square(_ctx_1024t)) + 1e-12) * 0.953939
        ctx_1024 = -1.39393e-06 + 0.999914 * (_ctx_1024t + 0.3 * jax.random.normal(jax.random.fold_in(_rk, 611), (4, 256, 128), jnp.float32))
        _g = jax.random.normal(jax.random.fold_in(_rk, 9001), (2, 4), jnp.float32)
        _g = jnp.sign(_g) * jnp.maximum(jnp.abs(_g), 1.0) + (_g == 0) * 1.0
        g_xattn = _g[0]
        g_ffn = _g[1]
        return (x, ctx_1024, g_xattn, g_ffn)
    x, ctx_1024, g_xattn, g_ffn = _rec_inputs()

    def _L0_xattn_setup():
        import jax, jax.numpy as jnp
        import numpy as np
        import math
        D_MODEL = 128
        NUM_HEADS = 16
        MAX_LEN = 256
        D_HEAD = D_MODEL // NUM_HEADS
        BATCH = 2
        SEQ = 256

        def _skew(QEr):
            B, H, R, C = QEr.shape
            padded = jnp.pad(QEr, ((0, 0), (0, 0), (0, 0), (1, 0)))
            reshaped = padded.reshape(B, H, C + 1, R)
            return reshaped[:, :, 1:, :]
        root = jax.random.key(seed)
        ks = jax.random.split(root, 10)
        s = 1.0 / math.sqrt(D_MODEL)
        return {'query': jax.random.normal(ks[0], (BATCH, SEQ, D_MODEL), jnp.float32), 'key': jax.random.normal(ks[1], (BATCH, SEQ, D_MODEL), jnp.float32), 'value': jax.random.normal(ks[2], (BATCH, SEQ, D_MODEL), jnp.float32), 'Wq': jax.random.normal(ks[3], (D_MODEL, D_MODEL), jnp.float32) * s, 'bq': jax.random.normal(ks[4], (D_MODEL,), jnp.float32) * s, 'Wk': jax.random.normal(ks[5], (D_MODEL, D_MODEL), jnp.float32) * s, 'bk': jax.random.normal(ks[6], (D_MODEL,), jnp.float32) * s, 'Wv': jax.random.normal(ks[7], (D_MODEL, D_MODEL), jnp.float32) * s, 'bv': jax.random.normal(ks[8], (D_MODEL,), jnp.float32) * s, 'Er': jax.random.normal(ks[9], (MAX_LEN, D_HEAD), jnp.float32)}
    _L0_xattn_all = _L0_xattn_setup()
    _L0_xattn_in = {k: v for k, v in _L0_xattn_all.items() if k in ('Wq', 'bq', 'Wk', 'bk', 'Wv', 'bv', 'Er')}
    del _L0_xattn_all

    def _L0_ffn_setup():
        import jax, jax.numpy as jnp
        import numpy as np
        D_MODEL = 128
        HIDDEN = 512
        N_ROUTING = 2
        key = jax.random.key(seed)
        ks = jax.random.split(key, 10)
        s = 0.02
        x = jax.random.normal(ks[0], (4, 512, D_MODEL), dtype=jnp.float32)
        gate_w = jax.random.normal(ks[1], (N_ROUTING, D_MODEL), dtype=jnp.float32) * s
        w1 = jax.random.normal(ks[2], (N_ROUTING, D_MODEL, HIDDEN), dtype=jnp.float32) * s
        b1 = jax.random.normal(ks[3], (N_ROUTING, HIDDEN), dtype=jnp.float32) * s
        w2 = jax.random.normal(ks[4], (N_ROUTING, HIDDEN, D_MODEL), dtype=jnp.float32) * s
        b2 = jax.random.normal(ks[5], (N_ROUTING, D_MODEL), dtype=jnp.float32) * s
        sw1 = jax.random.normal(ks[6], (D_MODEL, HIDDEN), dtype=jnp.float32) * s
        sb1 = jax.random.normal(ks[7], (HIDDEN,), dtype=jnp.float32) * s
        sw2 = jax.random.normal(ks[8], (HIDDEN, D_MODEL), dtype=jnp.float32) * s
        sb2 = jax.random.normal(ks[9], (D_MODEL,), dtype=jnp.float32) * s
        return {'x': x, 'gate_w': gate_w, 'w1': w1, 'b1': b1, 'w2': w2, 'b2': b2, 'sw1': sw1, 'sb1': sb1, 'sw2': sw2, 'sb2': sb2}
    _L0_ffn_all = _L0_ffn_setup()
    _L0_ffn_in = {k: v for k, v in _L0_ffn_all.items() if k in ('gate_w', 'w1', 'b1', 'w2', 'b2', 'sw1', 'sb1', 'sw2', 'sb2')}
    del _L0_ffn_all

    def _L1_xattn_setup():
        import jax, jax.numpy as jnp
        import numpy as np
        import math
        NHEADS = 16
        CAUSAL = True
        NEG_INF = -1e+18
        key = jax.random.key(seed)
        kq, kk, kv = jax.random.split(key, 3)
        B, S, D = (4, 1024, 128)
        q = jax.random.normal(kq, (B, S, D), dtype=jnp.float32)
        k = jax.random.normal(kk, (B, S, D), dtype=jnp.float32)
        v = jax.random.normal(kv, (B, S, D), dtype=jnp.float32)
        return {'q': q, 'k': k, 'v': v}
    _L1_xattn_all = _L1_xattn_setup()
    _L1_xattn_in = {k: v for k, v in _L1_xattn_all.items() if k in ()}
    del _L1_xattn_all

    def _L1_ffn_setup():
        import jax, jax.numpy as jnp
        import numpy as np
        DIM = 128
        MOE_INTER = 128
        SHARED_INTER = 128
        N_EXPERTS = 6
        TOP_K = 2
        ROUTE_SCALE = 1.0
        B, S = (8, 512)
        STD = 0.02 / np.sqrt(DIM)
        STD_I = 0.02 / np.sqrt(MOE_INTER)
        key = jax.random.key(seed)
        ks = jax.random.split(key, 10)
        inp = {'x': jax.random.normal(ks[0], (B, S, DIM), dtype=jnp.float32), 'gate_w': jax.random.normal(ks[1], (N_EXPERTS, DIM), dtype=jnp.float32) * STD, 'gate_b': jnp.zeros((N_EXPERTS,), dtype=jnp.float32), 'ew1': jax.random.normal(ks[2], (N_EXPERTS, MOE_INTER, DIM), dtype=jnp.float32) * STD, 'ew2': jax.random.normal(ks[3], (N_EXPERTS, DIM, MOE_INTER), dtype=jnp.float32) * STD_I, 'ew3': jax.random.normal(ks[4], (N_EXPERTS, MOE_INTER, DIM), dtype=jnp.float32) * STD, 'fc1': jax.random.normal(ks[5], (SHARED_INTER, DIM), dtype=jnp.float32) * STD, 'fc2': jax.random.normal(ks[6], (SHARED_INTER, DIM), dtype=jnp.float32) * STD, 'fc3': jax.random.normal(ks[7], (DIM, SHARED_INTER), dtype=jnp.float32) * STD_I}
        return inp
    _L1_ffn_all = _L1_ffn_setup()
    _L1_ffn_in = {k: v for k, v in _L1_ffn_all.items() if k in ('gate_w', 'gate_b', 'ew1', 'ew2', 'ew3', 'fc1', 'fc2', 'fc3')}
    del _L1_ffn_all

    def _L2_xattn_setup():
        import jax, jax.numpy as jnp
        import numpy as np
        B, S, E, NH = (2, 256, 128, 4)
        HD = E // NH

        def _mlstm_head(q, k, v, ig, fg, eps=1e-06):
            s, dh = q.shape
            log_f = jax.nn.log_sigmoid(fg)
            cs = jnp.concatenate([jnp.zeros((1, 1), log_f.dtype), jnp.cumsum(log_f, axis=0)], axis=0)
            neg = jnp.asarray(-0.7 * jnp.finfo(cs.dtype).max, cs.dtype)
            log_d = jnp.where(jnp.tri(s, dtype=bool), (cs - cs.T)[1:, 1:] + ig.T, neg)
            m = jnp.max(log_d, axis=-1, keepdims=True)
            d = jnp.exp(log_d - m)
            c = q @ (k.T / jnp.sqrt(dh)) * d
            n = jnp.maximum(jnp.sum(c, axis=-1, keepdims=True), jnp.exp(-m))
            return c / (n + eps) @ v
        key = jax.random.key(seed)
        ks = jax.random.split(key, 8)
        return {'q': jax.random.normal(ks[0], (B, S, E), jnp.float32), 'k': jax.random.normal(ks[1], (B, S, E), jnp.float32), 'v': jax.random.normal(ks[2], (B, S, E), jnp.float32), 'igate_kernel': jax.random.normal(ks[3], (3 * E, NH), jnp.float32) * 0.02, 'igate_bias': jax.random.normal(ks[4], (NH,), jnp.float32) * 0.1, 'fgate_kernel': jax.random.normal(ks[5], (3 * E, NH), jnp.float32) * 0.02, 'fgate_bias': jnp.linspace(3.0, 6.0, NH, dtype=jnp.float32), 'rms_scale': jax.random.normal(ks[6], (HD,), jnp.float32) * 0.02}
    _L2_xattn_all = _L2_xattn_setup()
    _L2_xattn_in = {k: v for k, v in _L2_xattn_all.items() if k in ('igate_kernel', 'igate_bias', 'fgate_kernel', 'fgate_bias', 'rms_scale')}
    del _L2_xattn_all

    def _L2_ffn_setup():
        import jax, jax.numpy as jnp
        import numpy as np
        TOP_K = 2
        key = jax.random.key(seed)
        k0, k1, k2, k3, k4 = jax.random.split(key, 5)
        B, S, H, I, E = (1, 512, 128, 256, 8)
        hidden_states = jax.random.normal(k0, (B, S, H), dtype=jnp.float32)
        wg = jax.random.normal(k1, (E, H), dtype=jnp.float32) * 0.02
        w1 = jax.random.normal(k2, (E, I, H), dtype=jnp.float32) * 0.02
        w3 = jax.random.normal(k3, (E, I, H), dtype=jnp.float32) * 0.02
        w2 = jax.random.normal(k4, (E, H, I), dtype=jnp.float32) * 0.02
        return {'hidden_states': hidden_states, 'wg': wg, 'w1': w1, 'w3': w3, 'w2': w2}
    _L2_ffn_all = _L2_ffn_setup()
    _L2_ffn_in = {k: v for k, v in _L2_ffn_all.items() if k in ('wg', 'w1', 'w3', 'w2')}
    del _L2_ffn_all

    def _L3_xattn_setup():
        import jax, jax.numpy as jnp
        import numpy as np
        SCALE_BASE = 512.0
        GN_EPS = 1e-05

        def _xpos(x, downscale):
            L, D = (x.shape[-2], x.shape[-1])
            half = D // 2
            base = (jnp.arange(0, D, 2, dtype=jnp.float32) + 0.4 * D) / (1.4 * D)
            min_pos = -(L // 2)
            power = (jnp.arange(min_pos, min_pos + L, dtype=jnp.float32) / SCALE_BASE)[:, None]
            scale = base[None, :] ** power
            inv_freq = 1.0 / 10000.0 ** (jnp.arange(half, dtype=jnp.float32) / half)
            ang = jnp.arange(L, dtype=jnp.float32)[:, None] * inv_freq[None, :]
            sin, cos = (jnp.sin(ang), jnp.cos(ang))
            if downscale:
                scale = 1.0 / scale
            sin_s = jnp.repeat(sin * scale, 2, axis=-1)
            cos_s = jnp.repeat(cos * scale, 2, axis=-1)
            x1, x2 = (x[..., ::2], x[..., 1::2])
            rot = jnp.stack((-x2, x1), axis=-1).reshape(x.shape)
            return x * cos_s + rot * sin_s

        def _decay_mask(L, H):
            gammas = 1.0 - jnp.exp(jnp.linspace(np.log(1.0 / 32.0), np.log(1.0 / 512.0), H)).astype(jnp.float32)
            idx = jnp.arange(L)
            dist = idx[:, None] - idx[None, :]
            causal = dist >= 0
            d = jnp.maximum(dist, 0).astype(jnp.float32)
            return jnp.where(causal[None], gammas[:, None, None] ** d[None], 0.0)
        key = jax.random.key(seed)
        ks = jax.random.split(key, 9)
        B, L, D, H = (2, 256, 128, 16)
        hd = D // H
        return {'query': jax.random.normal(ks[0], (B, L, D), jnp.float32), 'key': jax.random.normal(ks[1], (B, L, D), jnp.float32), 'value': jax.random.normal(ks[2], (B, L, D), jnp.float32), 'W_Q': jax.random.normal(ks[3], (H, D, hd), jnp.float32) / D, 'W_K': jax.random.normal(ks[4], (H, D, hd), jnp.float32) / D, 'W_V': jax.random.normal(ks[5], (H, D, hd), jnp.float32) / D, 'g_w': jax.random.normal(ks[6], (D, D), jnp.float32) * (2.0 / (D + D)) ** 0.5, 'g_b': jnp.zeros((D,), jnp.float32), 'out_w': jax.random.normal(ks[7], (D, D), jnp.float32) * (2.0 / (D + D)) ** 0.5, 'out_b': jnp.zeros((D,), jnp.float32)}
    _L3_xattn_all = _L3_xattn_setup()
    _L3_xattn_in = {k: v for k, v in _L3_xattn_all.items() if k in ('W_Q', 'W_K', 'W_V', 'g_w', 'g_b', 'out_w', 'out_b')}
    del _L3_xattn_all

    def _L3_ffn_setup():
        import jax, jax.numpy as jnp
        import numpy as np
        L, E, H, F, K = (4, 4, 128, 512, 2)
        B, S = (4, 256)
        EPS = 1e-05

        def _moe_layer(x, rw, rb, g, b, w1, b1, w2, b2):
            logits = jnp.einsum('bsh,he->bse', x, rw) + rb
            probs = jax.nn.softmax(logits, axis=-1)
            vals, idx = jax.lax.top_k(probs, K)
            vals = vals / vals.sum(axis=-1, keepdims=True)
            mu = x.mean(axis=-1, keepdims=True)
            xc = x - mu
            xhat = xc * jax.lax.rsqrt((xc * xc).mean(axis=-1, keepdims=True) + EPS)
            xe = xhat[None] * g[:, None, None, :] + b[:, None, None, :]
            h = jax.nn.gelu(jnp.einsum('ebsh,ehf->ebsf', xe, w1) + b1[:, None, None, :], approximate=False)
            y = jnp.einsum('ebsf,efh->ebsh', h, w2) + b2[:, None, None, :]
            expert_out = x[None] + y
            comb = jnp.einsum('bsk,bske->bse', vals, jax.nn.one_hot(idx, E, dtype=x.dtype))
            return jnp.einsum('bse,ebsh->bsh', comb, expert_out)
        key = jax.random.key(seed)
        ks = jax.random.split(key, 4)
        return {'hidden_states': jax.random.normal(ks[0], (B, S, H), jnp.float32), 'router_w': 0.02 * jax.random.normal(ks[1], (L, H, E), jnp.float32), 'router_b': jnp.zeros((L, E), jnp.float32), 'ln_g': jnp.ones((L, E, H), jnp.float32), 'ln_b': jnp.zeros((L, E, H), jnp.float32), 'w1': 0.02 * jax.random.normal(ks[2], (L, E, H, F), jnp.float32), 'b1': jnp.zeros((L, E, F), jnp.float32), 'w2': 0.02 * jax.random.normal(ks[3], (L, E, F, H), jnp.float32), 'b2': jnp.zeros((L, E, H), jnp.float32)}
    _L3_ffn_all = _L3_ffn_setup()
    _L3_ffn_in = {k: v for k, v in _L3_ffn_all.items() if k in ('router_w', 'router_b', 'ln_g', 'ln_b', 'w1', 'b1', 'w2', 'b2')}
    del _L3_ffn_all
    return {'x': x, 'ctx_1024': ctx_1024, 'g_xattn': g_xattn, 'g_ffn': g_ffn, 'L0_xattn_Wq': _L0_xattn_in['Wq'], 'L0_xattn_bq': _L0_xattn_in['bq'], 'L0_xattn_Wk': _L0_xattn_in['Wk'], 'L0_xattn_bk': _L0_xattn_in['bk'], 'L0_xattn_Wv': _L0_xattn_in['Wv'], 'L0_xattn_bv': _L0_xattn_in['bv'], 'L0_xattn_Er': _L0_xattn_in['Er'], 'L0_ffn_gate_w': _L0_ffn_in['gate_w'], 'L0_ffn_w1': _L0_ffn_in['w1'], 'L0_ffn_b1': _L0_ffn_in['b1'], 'L0_ffn_w2': _L0_ffn_in['w2'], 'L0_ffn_b2': _L0_ffn_in['b2'], 'L0_ffn_sw1': _L0_ffn_in['sw1'], 'L0_ffn_sb1': _L0_ffn_in['sb1'], 'L0_ffn_sw2': _L0_ffn_in['sw2'], 'L0_ffn_sb2': _L0_ffn_in['sb2'], 'L1_ffn_gate_w': _L1_ffn_in['gate_w'], 'L1_ffn_gate_b': _L1_ffn_in['gate_b'], 'L1_ffn_ew1': _L1_ffn_in['ew1'], 'L1_ffn_ew2': _L1_ffn_in['ew2'], 'L1_ffn_ew3': _L1_ffn_in['ew3'], 'L1_ffn_fc1': _L1_ffn_in['fc1'], 'L1_ffn_fc2': _L1_ffn_in['fc2'], 'L1_ffn_fc3': _L1_ffn_in['fc3'], 'L2_xattn_igate_kernel': _L2_xattn_in['igate_kernel'], 'L2_xattn_igate_bias': _L2_xattn_in['igate_bias'], 'L2_xattn_fgate_kernel': _L2_xattn_in['fgate_kernel'], 'L2_xattn_fgate_bias': _L2_xattn_in['fgate_bias'], 'L2_xattn_rms_scale': _L2_xattn_in['rms_scale'], 'L2_ffn_wg': _L2_ffn_in['wg'], 'L2_ffn_w1': _L2_ffn_in['w1'], 'L2_ffn_w3': _L2_ffn_in['w3'], 'L2_ffn_w2': _L2_ffn_in['w2'], 'L3_xattn_W_Q': _L3_xattn_in['W_Q'], 'L3_xattn_W_K': _L3_xattn_in['W_K'], 'L3_xattn_W_V': _L3_xattn_in['W_V'], 'L3_xattn_g_w': _L3_xattn_in['g_w'], 'L3_xattn_g_b': _L3_xattn_in['g_b'], 'L3_xattn_out_w': _L3_xattn_in['out_w'], 'L3_xattn_out_b': _L3_xattn_in['out_b'], 'L3_ffn_router_w': _L3_ffn_in['router_w'], 'L3_ffn_router_b': _L3_ffn_in['router_b'], 'L3_ffn_ln_g': _L3_ffn_in['ln_g'], 'L3_ffn_ln_b': _L3_ffn_in['ln_b'], 'L3_ffn_w1': _L3_ffn_in['w1'], 'L3_ffn_b1': _L3_ffn_in['b1'], 'L3_ffn_w2': _L3_ffn_in['w2'], 'L3_ffn_b2': _L3_ffn_in['b2']}

def reference(x, ctx_1024, g_xattn, g_ffn, L0_xattn_Wq, L0_xattn_bq, L0_xattn_Wk, L0_xattn_bk, L0_xattn_Wv, L0_xattn_bv, L0_xattn_Er, L0_ffn_gate_w, L0_ffn_w1, L0_ffn_b1, L0_ffn_w2, L0_ffn_b2, L0_ffn_sw1, L0_ffn_sb1, L0_ffn_sw2, L0_ffn_sb2, L1_ffn_gate_w, L1_ffn_gate_b, L1_ffn_ew1, L1_ffn_ew2, L1_ffn_ew3, L1_ffn_fc1, L1_ffn_fc2, L1_ffn_fc3, L2_xattn_igate_kernel, L2_xattn_igate_bias, L2_xattn_fgate_kernel, L2_xattn_fgate_bias, L2_xattn_rms_scale, L2_ffn_wg, L2_ffn_w1, L2_ffn_w3, L2_ffn_w2, L3_xattn_W_Q, L3_xattn_W_K, L3_xattn_W_V, L3_xattn_g_w, L3_xattn_g_b, L3_xattn_out_w, L3_xattn_out_b, L3_ffn_router_w, L3_ffn_router_b, L3_ffn_ln_g, L3_ffn_ln_b, L3_ffn_w1, L3_ffn_b1, L3_ffn_w2, L3_ffn_b2):
    import jax
    import jax.numpy as jnp

    def _L0_xattn_ref(query, key, value, Wq, bq, Wk, bk, Wv, bv, Er):
        import jax, jax.numpy as jnp
        import numpy as np
        import math
        D_MODEL = 128
        NUM_HEADS = 16
        MAX_LEN = 256
        D_HEAD = D_MODEL // NUM_HEADS
        BATCH = 2
        SEQ = 256

        def _skew(QEr):
            B, H, R, C = QEr.shape
            padded = jnp.pad(QEr, ((0, 0), (0, 0), (0, 0), (1, 0)))
            reshaped = padded.reshape(B, H, C + 1, R)
            return reshaped[:, :, 1:, :]
        B, S, D = query.shape
        H, dh = (NUM_HEADS, D_HEAD)
        q = (jnp.einsum('bsd,ed->bse', query, Wq) + bq).reshape(B, S, H, dh).transpose(0, 2, 1, 3)
        k = (jnp.einsum('bsd,ed->bse', key, Wk) + bk).reshape(B, S, H, dh).transpose(0, 2, 1, 3)
        v = (jnp.einsum('bsd,ed->bse', value, Wv) + bv).reshape(B, S, H, dh).transpose(0, 2, 1, 3)
        start = MAX_LEN - S
        Er_s = Er[start:, :]
        QEr = jnp.einsum('bhsd,ld->bhsl', q, Er_s)
        Srel = _skew(QEr)
        QK = jnp.einsum('bhsd,bhtd->bhst', q, k)
        attn = (QK + Srel) / math.sqrt(dh)
        causal = jnp.tril(jnp.ones((S, S), dtype=bool))
        attn = jnp.where(causal[None, None], attn, -jnp.inf)
        attn = jax.nn.softmax(attn, axis=-1)
        out = jnp.einsum('bhst,bhtd->bhsd', attn, v)
        out = out.transpose(0, 2, 1, 3).reshape(B, S, D)
        return out

    def _L0_ffn_ref(x, gate_w, w1, b1, w2, b2, sw1, sb1, sw2, sb2):
        import jax, jax.numpy as jnp
        import numpy as np
        D_MODEL = 128
        HIDDEN = 512
        N_ROUTING = 2
        B, S, D = x.shape
        xf = x.reshape(-1, D)
        gate_scores = xf @ gate_w.T
        gate_probs = jax.nn.softmax(gate_scores, axis=-1)
        top1 = jnp.argmax(gate_probs, axis=-1)
        one_hot = jax.nn.one_hot(top1, N_ROUTING, dtype=xf.dtype)
        masked = xf[None, :, :] * one_hot.T[:, :, None]
        h = jax.nn.relu(jnp.einsum('end,edh->enh', masked, w1) + b1[:, None, :])
        expert_out = jnp.einsum('enh,ehd->end', h, w2) + b2[:, None, :]
        routing_output = expert_out.sum(axis=0)
        shared = jax.nn.relu(xf @ sw1 + sb1) @ sw2 + sb2
        return (routing_output + shared).reshape(B, S, D)

    def _L1_xattn_ref(q, k, v):
        import jax, jax.numpy as jnp
        import numpy as np
        import math
        NHEADS = 16
        CAUSAL = True
        NEG_INF = -1e+18
        B, S, D = q.shape
        hd = D // NHEADS
        qh = q.reshape(B, S, NHEADS, hd)
        kh = k.reshape(B, S, NHEADS, hd)
        vh = v.reshape(B, S, NHEADS, hd)
        scores = jnp.einsum('bsqd,bskd->bsqk', qh, kh) / math.sqrt(hd)
        if CAUSAL:
            mask = jnp.tril(jnp.ones((NHEADS, NHEADS), dtype=bool))
            scores = jnp.where(mask, scores, jnp.asarray(NEG_INF, scores.dtype))
        attn = jax.nn.softmax(scores, axis=-1)
        out = jnp.einsum('bsqk,bskd->bsqd', attn, vh)
        return out.reshape(B, S, D)

    def _L1_ffn_ref(x, gate_w, gate_b, ew1, ew2, ew3, fc1, fc2, fc3):
        import jax, jax.numpy as jnp
        import numpy as np
        DIM = 128
        MOE_INTER = 128
        SHARED_INTER = 128
        N_EXPERTS = 6
        TOP_K = 2
        ROUTE_SCALE = 1.0
        B, S = (8, 512)
        STD = 0.02 / np.sqrt(DIM)
        STD_I = 0.02 / np.sqrt(MOE_INTER)
        orig_shape = x.shape
        xt = x.reshape(-1, DIM)
        logits = xt @ gate_w.T + gate_b
        probs = jax.nn.sigmoid(logits)
        w, idx = jax.lax.top_k(probs, TOP_K)
        w = w / (jnp.sum(w, axis=-1, keepdims=True) + 1e-08)
        w = w * ROUTE_SCALE
        ge = jnp.sum(jax.nn.one_hot(idx, N_EXPERTS, dtype=w.dtype) * w[..., None], axis=1)
        y = jnp.zeros_like(xt)
        for e in range(N_EXPERTS):
            h = jax.nn.silu(xt @ ew1[e].T) * (xt @ ew3[e].T)
            y = y + ge[:, e:e + 1] * (h @ ew2[e].T)
        z = jax.nn.silu(xt @ fc1.T) * (xt @ fc2.T) @ fc3.T
        return (y + z).reshape(orig_shape)

    def _L2_xattn_ref(q, k, v, igate_kernel, igate_bias, fgate_kernel, fgate_bias, rms_scale):
        import jax, jax.numpy as jnp
        import numpy as np
        B, S, E, NH = (2, 256, 128, 4)
        HD = E // NH

        def _mlstm_head(q, k, v, ig, fg, eps=1e-06):
            s, dh = q.shape
            log_f = jax.nn.log_sigmoid(fg)
            cs = jnp.concatenate([jnp.zeros((1, 1), log_f.dtype), jnp.cumsum(log_f, axis=0)], axis=0)
            neg = jnp.asarray(-0.7 * jnp.finfo(cs.dtype).max, cs.dtype)
            log_d = jnp.where(jnp.tri(s, dtype=bool), (cs - cs.T)[1:, 1:] + ig.T, neg)
            m = jnp.max(log_d, axis=-1, keepdims=True)
            d = jnp.exp(log_d - m)
            c = q @ (k.T / jnp.sqrt(dh)) * d
            n = jnp.maximum(jnp.sum(c, axis=-1, keepdims=True), jnp.exp(-m))
            return c / (n + eps) @ v
        b, s, e = q.shape
        nh = igate_kernel.shape[1]
        hd = e // nh
        gate_in = jnp.concatenate((q, k, v), axis=-1)
        ig = (gate_in @ igate_kernel + igate_bias).swapaxes(-1, -2)[..., None]
        fg = (gate_in @ fgate_kernel + fgate_bias).swapaxes(-1, -2)[..., None]
        qh = q.reshape(b, s, nh, hd).swapaxes(1, 2)
        kh = k.reshape(b, s, nh, hd).swapaxes(1, 2)
        vh = v.reshape(b, s, nh, hd).swapaxes(1, 2)
        h = jax.vmap(jax.vmap(_mlstm_head))(qh, kh, vh, ig, fg)
        var = jnp.mean(jnp.square(h.astype(jnp.float32)), axis=-1, keepdims=True)
        h = (h * jax.lax.rsqrt(var + 1e-06)).astype(h.dtype) * (1.0 + rms_scale)
        return h.swapaxes(1, 2).reshape(b, s, e)

    def _L2_ffn_ref(hidden_states, wg, w1, w3, w2):
        import jax, jax.numpy as jnp
        import numpy as np
        TOP_K = 2
        orig_shape = hidden_states.shape
        H = orig_shape[-1]
        E = wg.shape[0]
        x = hidden_states.reshape(-1, H)
        router_logits = x @ wg.T
        probs = jax.nn.softmax(router_logits, axis=-1)
        topk_w, topk_idx = jax.lax.top_k(probs, TOP_K)
        topk_w = topk_w / jnp.sum(topk_w, axis=-1, keepdims=True)
        expert_w = jnp.sum(jax.nn.one_hot(topk_idx, E, dtype=x.dtype) * topk_w[..., None], axis=1)
        h1 = jnp.einsum('th,eih->tei', x, w1)
        h3 = jnp.einsum('th,eih->tei', x, w3)
        y = jnp.einsum('tei,ehi->teh', jax.nn.silu(h1) * h3, w2)
        out = jnp.einsum('te,teh->th', expert_w, y)
        return out.reshape(orig_shape)

    def _L3_xattn_ref(query, key, value, W_Q, W_K, W_V, g_w, g_b, out_w, out_b):
        import jax, jax.numpy as jnp
        import numpy as np
        SCALE_BASE = 512.0
        GN_EPS = 1e-05

        def _xpos(x, downscale):
            L, D = (x.shape[-2], x.shape[-1])
            half = D // 2
            base = (jnp.arange(0, D, 2, dtype=jnp.float32) + 0.4 * D) / (1.4 * D)
            min_pos = -(L // 2)
            power = (jnp.arange(min_pos, min_pos + L, dtype=jnp.float32) / SCALE_BASE)[:, None]
            scale = base[None, :] ** power
            inv_freq = 1.0 / 10000.0 ** (jnp.arange(half, dtype=jnp.float32) / half)
            ang = jnp.arange(L, dtype=jnp.float32)[:, None] * inv_freq[None, :]
            sin, cos = (jnp.sin(ang), jnp.cos(ang))
            if downscale:
                scale = 1.0 / scale
            sin_s = jnp.repeat(sin * scale, 2, axis=-1)
            cos_s = jnp.repeat(cos * scale, 2, axis=-1)
            x1, x2 = (x[..., ::2], x[..., 1::2])
            rot = jnp.stack((-x2, x1), axis=-1).reshape(x.shape)
            return x * cos_s + rot * sin_s

        def _decay_mask(L, H):
            gammas = 1.0 - jnp.exp(jnp.linspace(np.log(1.0 / 32.0), np.log(1.0 / 512.0), H)).astype(jnp.float32)
            idx = jnp.arange(L)
            dist = idx[:, None] - idx[None, :]
            causal = dist >= 0
            d = jnp.maximum(dist, 0).astype(jnp.float32)
            return jnp.where(causal[None], gammas[:, None, None] ** d[None], 0.0)
        B, L, D = query.shape
        H = W_Q.shape[0]
        q = jnp.einsum('bld,hde->bhle', query, W_Q)
        k = jnp.einsum('bld,hde->bhle', key, W_K)
        v = jnp.einsum('bld,hde->bhle', value, W_V)
        q = _xpos(q, downscale=False)
        k = _xpos(k, downscale=True)
        sim = jnp.einsum('bhnd,bhsd->bhns', q, k) * _decay_mask(L, H)[None]
        ret = jnp.einsum('bhns,bhsd->bhnd', sim, v)
        mu = ret.mean(axis=-1, keepdims=True)
        var = ret.var(axis=-1, keepdims=True)
        ret = (ret - mu) / jnp.sqrt(var + GN_EPS)
        ret = ret.transpose(0, 2, 1, 3).reshape(B, L, D)
        gate = jax.nn.silu(query @ g_w.T + g_b)
        return ret * gate @ out_w.T + out_b

    def _L3_ffn_ref(hidden_states, router_w, router_b, ln_g, ln_b, w1, b1, w2, b2):
        import jax, jax.numpy as jnp
        import numpy as np
        L, E, H, F, K = (4, 4, 128, 512, 2)
        B, S = (4, 256)
        EPS = 1e-05

        def _moe_layer(x, rw, rb, g, b, w1, b1, w2, b2):
            logits = jnp.einsum('bsh,he->bse', x, rw) + rb
            probs = jax.nn.softmax(logits, axis=-1)
            vals, idx = jax.lax.top_k(probs, K)
            vals = vals / vals.sum(axis=-1, keepdims=True)
            mu = x.mean(axis=-1, keepdims=True)
            xc = x - mu
            xhat = xc * jax.lax.rsqrt((xc * xc).mean(axis=-1, keepdims=True) + EPS)
            xe = xhat[None] * g[:, None, None, :] + b[:, None, None, :]
            h = jax.nn.gelu(jnp.einsum('ebsh,ehf->ebsf', xe, w1) + b1[:, None, None, :], approximate=False)
            y = jnp.einsum('ebsf,efh->ebsh', h, w2) + b2[:, None, None, :]
            expert_out = x[None] + y
            comb = jnp.einsum('bsk,bske->bse', vals, jax.nn.one_hot(idx, E, dtype=x.dtype))
            return jnp.einsum('bse,ebsh->bsh', comb, expert_out)
        x = hidden_states
        for l in range(L):
            x = _moe_layer(x, router_w[l], router_b[l], ln_g[l], ln_b[l], w1[l], b1[l], w2[l], b2[l])
        return x
    x = x + jnp.tanh(g_xattn[0]) * _L0_xattn_ref(_layernorm(x, axis=-1), ctx_1024, ctx_1024, L0_xattn_Wq, L0_xattn_bq, L0_xattn_Wk, L0_xattn_bk, L0_xattn_Wv, L0_xattn_bv, L0_xattn_Er)
    x = x + jnp.tanh(g_ffn[0]) * _L0_ffn_ref(_layernorm(x, axis=-1), L0_ffn_gate_w, L0_ffn_w1, L0_ffn_b1, L0_ffn_w2, L0_ffn_b2, L0_ffn_sw1, L0_ffn_sb1, L0_ffn_sw2, L0_ffn_sb2)
    x = x + jnp.tanh(g_xattn[1]) * _L1_xattn_ref(_layernorm(x, axis=-1), ctx_1024, ctx_1024)
    x = x + jnp.tanh(g_ffn[1]) * _L1_ffn_ref(_layernorm(x, axis=-1), L1_ffn_gate_w, L1_ffn_gate_b, L1_ffn_ew1, L1_ffn_ew2, L1_ffn_ew3, L1_ffn_fc1, L1_ffn_fc2, L1_ffn_fc3)
    x = x + jnp.tanh(g_xattn[2]) * _L2_xattn_ref(_layernorm(x, axis=-1), ctx_1024, ctx_1024, L2_xattn_igate_kernel, L2_xattn_igate_bias, L2_xattn_fgate_kernel, L2_xattn_fgate_bias, L2_xattn_rms_scale)
    x = x + jnp.tanh(g_ffn[2]) * _L2_ffn_ref(_layernorm(x, axis=-1), L2_ffn_wg, L2_ffn_w1, L2_ffn_w3, L2_ffn_w2)
    x = x + jnp.tanh(g_xattn[3]) * _L3_xattn_ref(_layernorm(x, axis=-1), ctx_1024, ctx_1024, L3_xattn_W_Q, L3_xattn_W_K, L3_xattn_W_V, L3_xattn_g_w, L3_xattn_g_b, L3_xattn_out_w, L3_xattn_out_b)
    x = x + jnp.tanh(g_ffn[3]) * _L3_ffn_ref(_layernorm(x, axis=-1), L3_ffn_router_w, L3_ffn_router_b, L3_ffn_ln_g, L3_ffn_ln_b, L3_ffn_w1, L3_ffn_b1, L3_ffn_w2, L3_ffn_b2)
    return x

_drawn_inputs = setup_inputs


def setup_inputs(seed=0):
    import zlib

    import numpy as np

    out = dict(_drawn_inputs(seed))
    spreads = {'L1_ffn_gate_b': (0.0, 2.0),
     'L3_xattn_g_b': (0.0, 0.666),
     'L3_xattn_out_b': (0.0, 0.462),
     'L3_ffn_router_b': (0.0, 0.315),
     'L3_ffn_ln_g': (1.0, 0.6),
     'L3_ffn_ln_b': (0.0, 2.0),
     'L3_ffn_b1': (0.0, 0.448),
     'L3_ffn_b2': (0.0, 0.283)}
    factors = {'g_ffn': 23.24,
     'L0_xattn_bk': 64.0,
     'L0_ffn_b1': 7.226,
     'L0_ffn_sb1': 8.0,
     'L0_ffn_sb2': 2.836,
     'L1_ffn_gate_w': 53.274,
     'L1_ffn_ew1': 50.326,
     'L1_ffn_ew2': 50.616,
     'L1_ffn_ew3': 50.136,
     'L1_ffn_fc1': 31.502,
     'L1_ffn_fc2': 34.45,
     'L1_ffn_fc3': 41.108,
     'L2_xattn_igate_bias': 64.0,
     'L2_ffn_wg': 8.0,
     'L2_ffn_w1': 8.0,
     'L2_ffn_w3': 8.0,
     'L2_ffn_w2': 8.0}
    for name, (base, spread) in spreads.items():
        noise = np.random.default_rng([zlib.crc32(name.encode()), seed]).standard_normal(out[name].shape)
        drawn = base * np.exp(spread * noise) if base else spread * noise
        out[name] = jnp.asarray(drawn.astype(out[name].dtype))
    for name, factor in factors.items():
        out[name] = (out[name] * factor).astype(out[name].dtype)
    return out
```

```python
from contextlib import ExitStack

import numpy as np

import concourse.bass as bass
from concourse import mybir

F32 = mybir.dt.float32
BF16 = mybir.dt.bfloat16
ALU = mybir.AluOpType
ACT = mybir.ActivationFunctionType
AX = mybir.AxisListType.X

P = 128
D = 128
S = 256
T = 4
HALF = T * P
NB = HALF // S
H = 16
HD = D // H
MH = 4
MD = D // MH
NEG = -1e30
F0 = 512 // P
E1, E2, E3, L3 = 6, 8, 4, 4
I2 = 256 // P
PARTS_A = (0, 0, 1, 0, 2, 1)
PARTS_B = (0, 1, 0, 2, 0, 1)
NSTACK = HD * len(PARTS_A)

ORDER = [("att0", 0), ("att0", 1), ("ffn0", 0), ("att1", 0), ("ffn0", 1), ("ffn1", 0), ("att1", 1),
         ("ffn1", 1), ("att2", 0), ("att2", 1), ("ffn2", 0), ("ffn2", 1), ("att3", 0), ("att3", 1)]
ORDER += [(f"moe{l}", hf) for l in range(L3) for hf in range(2)]

def _columns(parts):
    at, n = {}, 0
    for name, w in parts:
        at[name] = (n, w)
        n += w
    return at, n


SMALL, NSMALL = _columns([
    ("wq", D), ("wk", D), ("wv", D), ("bq", 1), ("bk", 1), ("gates", 8), ("bv", D), ("er", 384),
    ("ident", P), ("addmask", 2 * P), ("ones", P),
    ("low", 64), ("g0w", 2), ("g1w", E1), ("g1b", E1), ("g2w", E2), ("g3w", L3 * E3), ("g3b", L3 * E3),
    ("s0b1", 3 * F0), ("b2s", D), ("rms", MD), ("mgw", 3 * 64), ("mgb", 1),
    ("b2", L3 * D), ("lng", L3 * E3), ("lnb", L3 * E3), ("b1", L3 * E3 * F0),
    ("rwq", D), ("rwqs", D), ("rwk", D), ("rwks", D), ("rwv", D), ("rgw", D), ("rgb", D), ("row", D), ("rob", D),
    ("keep", P), ("sel", MH * P),
    ("qcos", S), ("qsin", S), ("kcos", S), ("ksin", S)])
W0, NW0 = _columns([("w1", 3 * F0 * P), ("w2", 3 * F0 * D)])
W1, NW1 = _columns([("w1", 7 * P), ("w3", 7 * P), ("w2", 7 * D)])
W2, NW2 = _columns([("w1", E2 * I2 * P), ("w3", E2 * I2 * P), ("w2", E2 * I2 * D)])
W3, NW3 = _columns([("w1", E3 * F0 * P), ("w2", E3 * F0 * D)])


class Tally:

    def __init__(self):
        self.n = {}

    def __call__(self, sem, by=1):
        self.n[sem.name] = self.n.get(sem.name, 0) + by
        return self.n[sem.name]


class Turn:

    def __init__(self, bank, n, banks):
        self.bank, self.filled, self.drained, self.free = bank, n, n, max(n - banks, 0)


def plan(order):
    rings = {"a": [0, 1], "d": [2, 3], "s": [4, 5], "o": [6, 7]}
    count = {r: 0 for r in rings}
    turns = {}

    def use(name, hf, ring, *label):
        banks = rings[ring]
        turns[(name, hf, ring) + label] = Turn(banks[count[ring] % len(banks)], count[ring] + 1, len(banks))
        count[ring] += 1

    for name, hf in order:
        if name == "att0":
            use(name, hf, "d", "k")
            use(name, hf, "d", "v")
            use(name, hf, "a", "xt")
            use(name, hf, "d", "q")
            for c in range(16):
                use(name, hf, "d", "rel", c)
                if c % 2:
                    use(name, hf, "a", "rel", c // 2)
            for n in range(NB * H):
                use(name, hf, "s", "scores", n)
                use(name, hf, "d", "probs", n)
            for b in range(NB):
                use(name, hf, "o", "out", b)
        if name == "ffn0":
            use(name, hf, "a", "xt")
            use(name, hf, "d", "logits")
            use(name, hf, "o", "out")
            for k, e in enumerate(FFN0_ORDER):
                for c in range(F0):
                    use(name, hf, "a", "h", e, c)
                if k == 0:
                    for m in range(2):
                        use(name, hf, "a", "masked", m)
        if name == "att1":
            use(name, hf, "o", "out")
        if name in ("ffn1", "ffn2"):
            use(name, hf, "a", "xt")
            use(name, hf, "d", "logits")
            for e in range(EXPERTS[name]):
                for c in range(CHUNKS[name]):
                    use(name, hf, "a", "gate", e, c)
                    use(name, hf, "d", "up", e, c)
                use(name, hf, "o", "y", e)
        if name == "att2":
            use(name, hf, "a", "xt")
            use(name, hf, "d", "gates")
            use(name, hf, "d", "cols")
            for b in range(NB):
                use(name, hf, "o", "out", b)
            for h in range(MH):
                use(name, hf, "d", "rows", h)
                for b in range(NB):
                    use(name, hf, "d", "scores", h, b)
        if name == "att3":
            for w in ("k", "ks"):
                use(name, hf, "d", w)
            use(name, hf, "a", "v")
            use(name, hf, "a", "xt")
            for w in ("q", "qs", "gate"):
                use(name, hf, "d", w)
            for b in range(NB):
                use(name, hf, "o", "out", b)
                for p in range(H // 2):
                    if p % 2 == 0:
                        use(name, hf, "a", "off", b, p // 2)
                    use(name, hf, "d", "diag", b, p)
            use(name, hf, "a", "yt")
            use(name, hf, "d", "proj")
        if name[:3] == "moe":
            use(name, hf, "a", "xt")
            use(name, hf, "a", "xh")
            use(name, hf, "d", "logits")
            use(name, hf, "d", "combT")
            use(name, hf, "d", "bias")
            for e in range(E3):
                for c in range(F0):
                    use(name, hf, "a", "h", e, c)
                use(name, hf, "o", "y", e)
    return turns


FFN0_ORDER = (2, 0, 1)
EXPERTS = {"ffn1": E1 + 1, "ffn2": E2}
CHUNKS = {"ffn1": 1, "ffn2": I2}
FFN1_ORDER = (6, 0, 1, 2, 3, 4, 5)


def build(nc, x_in, ctx_in, ctxT_in, small_in, w0_in, w1_in, w2_in, w3_in, out, order=ORDER, debug_x=False):
    with ExitStack() as stack:
        def sb(name, shape, dt=F32):
            return stack.enter_context(nc.sbuf_tensor(name, shape, dt))

        def sem(name):
            return stack.enter_context(nc.semaphore(name))

        X = sb("X", [P, 2, T, D])
        XN = sb("XN", [P, 2, T, D])
        XT = sb("XT", [P, 2, HALF])
        CT = sb("CT", [P, 2, HALF])
        CX = sb("CX", [P, 2, T, D])
        V9 = sb("V9", [P, T, H, HD + 1])
        V33 = sb("V33", [P, 2, T, MH, MD + 1])
        V3 = V9[:, :, :, :].rearrange("p t h e -> p (t h e)")[:, 0:T * D].rearrange("p (t d) -> p t d", t=T)
        XH = V33[:, :, :, :, :].rearrange("p a t h e -> p (a t h e)")[:, 0:2 * T * D]\
            .rearrange("p (a t d) -> p a t d", a=2, t=T)
        small = sb("small", [P, NSMALL])
        W = sb("W", [P, max(NW0 + NW1, NW2)])
        arena = sb("arena", [P, 3 * 32 * P])
        hidden = sb("hidden", [P, 2, F0, HALF])
        q6 = sb("q6", [NSTACK, H, HALF], BF16)
        k6 = sb("k6", [NSTACK, H, HALF], BF16)
        er6 = sb("er6", [NSTACK, 384], BF16)
        erp = sb("erp", [HD, 3, 384], BF16)
        erf = sb("erf", [HD, 384])
        gated = sb("gated", [P, 2, HALF])
        turned = sb("turned", [P, 2, HALF])
        scratch = sb("scratch", [P, 24 * 256])
        TG = sb("TG", [P, 8])
        st6 = sb("st6", [P, T, 6])
        mv = sb("mv", [P, T, 2])
        VE = sb("VE", [P, 64])
        RS = sb("RS", [P, 64])
        mhalf = sb("mhalf", [P, 64])
        negmax = sb("negmax", [P, 4, 2])
        sums = sb("sums", [P, 64])
        rms1 = sb("rms1", [P, MD])
        rt = sb("rt", [P, 2 * T * 64])
        lg = sb("lg", [P, T * 8])
        pr = sb("pr", [P, T * 8])
        comb = sb("comb", [P, T * 8])
        rs4 = sb("rs4", [P, T * 2])
        combT = rt[0:E3, 0:HALF]
        ps = [stack.enter_context(nc.psum_tensor(f"bank{i}", [P, 512], F32)) for i in range(8)]

        def sm(name, rows=P):
            a, w = SMALL[name]
            return small[0:rows, a:a + w]

        def scr(at, *shape):
            n = int(np.prod(shape))
            v = scratch[:, at:at + n]
            if len(shape) == 1:
                return v
            names = "abcd"[:len(shape)]
            return v.rearrange(f"p ({' '.join(names)}) -> p {' '.join(names)}",
                               **{c: s for c, s in zip(names[1:], shape[1:])})

        ident = sm("ident")
        addmask = sm("addmask")
        w0, w1, w2 = W[:, 0:NW0], W[:, NW0:NW0 + NW1], W[:, 0:NW2]
        relD = arena[:, 0:2 * 32 * P].rearrange("p (c i) -> p c i", i=P)
        relO = arena[:, 2 * 32 * P:3 * 32 * P].rearrange("p (c i) -> p c i", i=P)
        w3 = [arena[:, s * NW3:(s + 1) * NW3] for s in range(2)]
        flat = hidden[:, :, :, :].rearrange("p a b c -> p (a b c)")
        probs = [flat[:, 3 * P * s:3 * P * (s + 1)] for s in range(3)]
        probsT = [flat[:, 2048 + 3 * P * s:2048 + 3 * P * (s + 1)] for s in range(3)]

        fval = scr(0, HALF)
        ftmp = scr(512, HALF)
        parts = [scratch[:, 1024 + 768 * s:1024 + 768 * (s + 1)].bitcast(BF16).rearrange("p (c t) -> p c t", c=3)
                 for s in range(2)]
        pad = scr(2560, T, D)
        sc1 = scr(0, T, H, H)
        prod1 = [scr(1024 + 512 * s, T, D) for s in range(3)]
        grow = scratch[0:64, 0:512]
        row = [scratch[0:MH, 512 * (1 + s):512 * (2 + s)] for s in range(5)]
        decay = [scr(3072 + 768 * s, NB, 3 * P) for s in range(2)]
        cmat = [scr(4608 + 384 * s, 3 * P) for s in range(2)]
        mout = scr(3072, T, MH, MD)
        msq = scr(3584, T, MH, MD)
        ae = [sb("a_tok", [P, T, MH]), sb("em_tok", [P, T, MH])]
        diag = [scr(2560 + 512 * s, 2, 2, P) for s in range(2)]
        gate3 = scr(3584, T, D)
        ret = scr(4096, T, H, HD)
        retsq = scr(4608, T, H, HD)
        Z = [[scr(512 * (2 * s + hf), T, D) for hf in range(2)] for s in range(2)]
        xe = [scr(2048 + 512 * s, HALF) for s in range(2)]
        msk = [scr(512 * s, T, D) for s in range(2)]
        acc = scr(1024, T, D)

        stage = {(k, hf): nc.dram_tensor(f"parts_{k}_{hf}", (P, 3 * HALF), BF16, kind="Internal").ap()
                 for k in ("k0", "q0", "k3", "q3") for hf in range(2)}

        small_loaded, ctx_loaded = sem("small_loaded"), sem("ctx_loaded")
        ctxT_loaded = [sem(f"ctxT_loaded{h}") for h in range(2)]
        rest_loaded = sem("rest_loaded")
        x_loaded = [sem(f"x_loaded{h}") for h in range(2)]
        w0_loaded, w1_loaded, w2_loaded = sem("w0_loaded"), sem("w1_loaded"), sem("w2_loaded")
        w3_loaded = [sem(f"w3_loaded{s}") for s in range(2)]
        consts_done = sem("consts_done")
        v33_done = sem("v33_done")
        tanh_done = sem("tanh_done")
        er_parts = sem("er_parts")
        er_stacked = sem("er_stacked")
        parts_ready = sem("parts_ready")
        parts_out = [sem(f"parts_out{s}") for s in range(2)]
        stacked_k = sem("stacked_k")
        stacked_q = sem("stacked_q")
        norm_done = [sem(f"norm_done{h}") for h in range(2)]
        var_ready = sem("var_ready")
        rstd_ready = sem("rstd_ready")
        act_filled, act_drained = sem("act_filled"), sem("act_drained")
        dve_filled, dve_drained = sem("dve_filled"), sem("dve_drained")
        score_filled, score_drained = sem("score_filled"), sem("score_drained")
        out_filled, out_drained = sem("out_filled"), sem("out_drained")
        negmax_ready = sem("negmax_ready")
        masked_ready = sem("masked_ready")
        logits_ready = sem("logits_ready")
        weights_ready = sem("weights_ready")
        shifted1, expd1 = sem("shifted1"), sem("expd1")
        av1_ready, av1_used = sem("av1_ready"), sem("av1_used")
        flog_ready = sem("flog_ready")
        emarg_ready, em_ready = sem("emarg_ready"), sem("em_ready")
        rows_ready = sem("rows_ready")
        dexp_in, dexp_ready = sem("dexp_in"), sem("dexp_ready")
        gate3_in, gate3_ready = sem("gate3_in"), sem("gate3_ready")
        y3_ready = sem("y3_ready")
        comb_ready = sem("comb_ready")
        xe_ready = sem("xe_ready")
        step = sem("dve_step")
        astep = sem("act_step")
        x_done = [sem(f"x_done{h}") for h in range(2)]
        out_stored = sem("out_stored")

        NORM = {"att0": 1, "ffn0": 2, "att1": 3, "ffn1": 4, "att2": 5, "ffn2": 6, "att3": 7,
                "moe0": 8, "moe1": 9, "moe2": 10, "moe3": 11}
        GATE = {"att0": 0, "att1": 1, "att2": 2, "att3": 3, "ffn0": 4, "ffn1": 5, "ffn2": 6, "moe3": 7}
        turns = plan(order)
        BANK = [p_[:, :] for p_ in ps]

        block = stack.enter_context(nc.Block())

        @block.sync
        def _(sp):
            seen = Tally()
            cut = SMALL["rms"][0]
            sp.dma_start(small[:, 0:cut], small_in[:, 0:cut]).then_inc(small_loaded, 16)
            xv = x_in.rearrange("(h t p) d -> h p t d", h=2, p=P)
            cv = ctx_in.rearrange("(h t p) d -> h p t d", h=2, p=P)
            for hf in range(2):
                sp.dma_start(CT[:, hf, :], ctxT_in[:, hf * HALF:(hf + 1) * HALF]).then_inc(ctxT_loaded[hf], 16)
                sp.dma_start(X[:, hf, :, :], xv[hf]).then_inc(x_loaded[hf], 16)
            sp.wait_ge(er_parts, 1)
            for r, c in enumerate(PARTS_B):
                sp.dma_start(er6[HD * r:HD * (r + 1), :], erp[:, c, :]).then_inc(er_stacked, 16)
            n_parts = 0

            def restack(kind, hf, dst, rows, loaded):
                nonlocal n_parts
                buf = n_parts % 2
                n_parts += 1
                sp.wait_ge(parts_ready, n_parts)
                sp.dma_start(stage[kind, hf], parts[buf].rearrange("p c t -> p (c t)")).then_inc(parts_out[buf], 16)
                sp.wait_ge(parts_out[buf], seen(parts_out[buf], 16))
                src = stage[kind, hf].rearrange("(h e) (c t) -> e c h t", e=HD, c=3)
                for r, c in enumerate(rows):
                    sp.dma_start(dst[HD * r:HD * (r + 1), :, :], src[:, c, :, :]).then_inc(loaded, 16)

            for name, hf in order:
                if name == "att0":
                    if hf == 1:
                        sp.wait_ge(norm_done[0], NORM[name] + 1)
                    restack("k0", hf, k6, PARTS_B, stacked_k)
                    restack("q0", hf, q6, PARTS_A, stacked_q)
                    if hf == 0:
                        sp.dma_start(small[:, cut:], small_in[:, cut:]).then_inc(rest_loaded, 16)
                        sp.dma_start(w0, w0_in).then_inc(w0_loaded, 16)
                        for h2 in range(2):
                            sp.dma_start(CX[:, h2, :, :], cv[h2]).then_inc(ctx_loaded, 16)
                        sp.dma_start(w1, w1_in).then_inc(w1_loaded, 16)
                    else:
                        sp.wait_ge(norm_done[1], NORM[name] + 1)
                        for l in range(2):
                            sp.dma_start(w3[l], w3_in[l]).then_inc(w3_loaded[l], 16)
                if name == "ffn1" and hf == 1:
                    sp.wait_ge(norm_done[0], NORM[name] + 1)
                    sp.wait_ge(norm_done[1], NORM[name] + 1)
                    sp.dma_start(w2, w2_in).then_inc(w2_loaded, 16)
                if name == "att3":
                    if hf == 1:
                        sp.wait_ge(norm_done[0], NORM[name] + 1)
                    restack("k3", hf, k6, PARTS_B, stacked_k)
                    restack("q3", hf, q6, PARTS_A, stacked_q)
                if name in ("moe0", "moe1") and hf == 1:
                    l = int(name[3])
                    sp.wait_ge(norm_done[0], NORM[name] + 1)
                    sp.wait_ge(norm_done[1], NORM[name] + 1)
                    sp.dma_start(w3[l], w3_in[l + 2]).then_inc(w3_loaded[l], 16)
            ov = out.rearrange("(h t p) d -> h p t d", h=2, p=P)
            for hf in range(2):
                sp.wait_ge(x_done[hf], 1)
                sp.dma_start(ov[hf], X[:, hf, :, :]).then_inc(out_stored, 16)
            sp.wait_ge(out_stored, 32)

        @block.gpsimd
        def _(pool):
            seen = Tally()
            pool.memset(mhalf[:, :], -0.5)
            pool.memset(V9[:, :, :, HD:HD + 1], 1.0)
            pool.memset(V33[:, :, :, :, MD:MD + 1], 1.0).then_inc(consts_done, 1)
            pool.wait_ge(consts_done, 1)

            def rsqrt(n):
                pool.wait_ge(var_ready, seen(var_ready))
                pool.tensor_tensor(RS[:, 0:n], VE[:, 0:n], mhalf[:, 0:n], ALU.pow).then_inc(rstd_ready, 1)

            for hf in range(2):
                rsqrt(T)
            for name, hf in order:
                if name == "att2":
                    rsqrt(T * MH)
                if name == "att3":
                    rsqrt(T * H)
                    rsqrt(T)
                if name != "moe3":
                    rsqrt(T)
                if name == "att0" and hf == 0:
                    pool.wait_ge(ctx_loaded, 32)
                    for h2 in range(2):
                        for h in range(MH):
                            last = pool.tensor_copy(V33[:, h2, :, h, 0:MD], CX[:, h2, :, MD * h:MD * (h + 1)])
                    last.then_inc(v33_done, 1)

        @block.scalar
        def _(act):
            seen = Tally()
            act.wait_ge(small_loaded, 16)
            act.activation(TG[:, :], sm("gates"), ACT.Tanh).then_inc(tanh_done, 1)

            def drain(turn, dst, func=ACT.Copy, **kw):
                act.wait_ge(act_filled, turn.filled)
                src = BANK[turn.bank]
                if len(dst.shape) == 3:
                    src = src.rearrange("p (a b) -> p a b", a=dst.shape[1])
                act.activation(dst, src, func, **kw).then_inc(act_drained, 1)

            for name, hf in order:
                at = {k[2:]: v for k, v in turns.items() if k[:2] == (name, hf)}
                if ("a", "v") in at:
                    drain(at["a", "v"], V3[:, :, :])
                if ("a", "xt") in at:
                    drain(at["a", "xt"], XT[:, hf, :])

                if name == "att0":
                    for c in range(8):
                        turn = at["a", "rel", c]
                        act.wait_ge(act_filled, turn.filled)
                        act.activation(relO[:, :, 16 * c:16 * (c + 1)],
                                       BANK[turn.bank].rearrange("p (u c) -> p c u", c=NB * H), ACT.Copy)\
                           .then_inc(act_drained, 1)
                    for n in range(NB * H):
                        turn = at["s", "scores", n]
                        act.wait_ge(negmax_ready, seen(negmax_ready))
                        pr_ = probs[n % 3]
                        act.activation(pr_[:, 0:P], BANK[turn.bank][:, 0:P], ACT.Exp, bias=negmax[:, n % 4, 0:1])
                        act.activation(pr_[:, P:3 * P], BANK[turn.bank][:, P:3 * P], ACT.Exp,
                                       bias=negmax[:, n % 4, 1:2]).then_inc(score_drained, 1)

                if name == "ffn0":
                    for k, e in enumerate(FFN0_ORDER):
                        for c in range(F0):
                            if hf == 0 and k == 0 and c == 0:
                                act.wait_ge(rest_loaded, 16)
                            drain(at["a", "h", e, c], hidden[:, k % 2, c, :], ACT.Relu,
                                  bias=sm("s0b1")[:, e * F0 + c:e * F0 + c + 1])
                        if k == 0:
                            for m in range(2):
                                drain(at["a", "masked", m], turned[:, m, :])

                if name == "att1":
                    act.wait_ge(shifted1, seen(shifted1))
                    act.activation(sc1, sc1, ACT.Exp, scale=HD ** -0.5).then_inc(expd1, 1)

                if name in ("ffn1", "ffn2"):
                    act.wait_ge(logits_ready, seen(logits_ready))
                    n = T * (E1 if name == "ffn1" else E2)
                    act.activation(pr[:, 0:n], lg[:, 0:n], ACT.Sigmoid if name == "ffn1" else ACT.Exp)\
                       .then_inc(weights_ready, 1)
                    chunks = [(e, c) for e in range(EXPERTS[name]) for c in range(CHUNKS[name])]
                    for k, (e, c) in enumerate(chunks):
                        if k >= 2:
                            act.wait_ge(dve_drained, at[("d", "up") + chunks[k - 2]].drained)
                        drain(at["a", "gate", e, c], gated[:, k % 2, :], ACT.Silu)

                if name == "att2":
                    act.wait_ge(dve_drained, at["d", "gates"].drained)
                    act.activation(row[1], grow[32:32 + MH, :], ACT.Abs).then_inc(astep, 1)
                    act.wait_ge(astep, seen(astep))
                    act.activation(row[1], row[1], ACT.Exp, scale=-1.0).then_inc(astep, 1)
                    act.wait_ge(astep, seen(astep))
                    act.activation(row[1], row[1], ACT.Ln, bias=sm("ones", MH)[:, 0:1]).then_inc(flog_ready, 1)
                    act.wait_ge(emarg_ready, seen(emarg_ready))
                    act.activation(row[0], row[0], ACT.Exp, scale=-1.0).then_inc(em_ready, 1)
                    for h in range(MH):
                        act.wait_ge(dexp_in, seen(dexp_in))
                        act.activation(decay[h % 2], decay[h % 2], ACT.Exp).then_inc(dexp_ready, 1)

                if name == "att3":
                    act.wait_ge(gate3_in, seen(gate3_in))
                    act.activation(gate3, gate3, ACT.Silu).then_inc(gate3_ready, 1)
                    for b in range(NB):
                        for g in range(H // 4):
                            drain(at["a", "off", b, g], gated[:, g % 2, :])
                    drain(at["a", "yt"], turned[:, 0, :])

                if name[:3] == "moe":
                    l = int(name[3])
                    drain(at["a", "xh"], turned[:, hf, :])
                    act.wait_ge(logits_ready, seen(logits_ready))
                    act.activation(pr[:, 0:T * E3], lg[:, 0:T * E3], ACT.Exp).then_inc(weights_ready, 1)
                    for e in range(E3):
                        for c in range(F0):
                            k = (l * E3 + e) * F0 + c
                            drain(at["a", "h", e, c], hidden[:, e % 2, c, :], ACT.Gelu, bias=sm("b1")[:, k:k + 1])

        @block.tensor
        def _(pe):
            seen = Tally()

            def mm(dst, lhsT, rhs, start, stop=False, turn=False):
                return pe.matmul(dst, lhsT, rhs, start=start, stop=stop, is_transpose=turn or None,
                                 skip_group_check=True)

            def bank(turn, drained):
                if turn.free:
                    pe.wait_ge(drained, turn.free)
                return BANK[turn.bank]

            def turn_tiles(turn, src):
                b_ = bank(turn, act_drained)
                for t in range(T):
                    last = mm(b_[:, t * P:(t + 1) * P], src[:, t, :], ident, start=(t == 0), stop=True, turn=True)
                last.then_inc(act_filled, 1)

            def tokens(turn, lhsT, rhs, n, ring=(dve_drained, dve_filled)):
                b_ = bank(turn, ring[0])
                for t in range(T):
                    last = mm(b_[:, t * n:(t + 1) * n], lhsT[:, t * P:(t + 1) * P], rhs, start=True, stop=True)
                last.then_inc(ring[1], 1)

            def feats(turn, w, rhs, drained, filled):
                mm(bank(turn, drained), w, rhs, start=True, stop=True).then_inc(filled, 1)

            def inputs(name, hf, at):
                pe.wait_ge(norm_done[hf], NORM[name])
                turn_tiles(at["a", "xt"], XN[:, hf, :, :])

            def second(turn, n, w2_, slot, ready, count, first=True, close=True):
                b_ = BANK[turn.bank] if not first else bank(turn, out_drained)
                pe.wait_ge(ready, count)
                for t in range(T):
                    for c in range(n):
                        last = mm(b_[:, t * P:(t + 1) * P], hidden[:, slot, c, t * P:(t + 1) * P], w2_(c),
                                  start=(first and t == 0 and c == 0), stop=(c == n - 1))
                if close:
                    last.then_inc(out_filled, 1)

            pe.wait_ge(small_loaded, 16)
            for name, hf in order:
                at = {k[2:]: v for k, v in turns.items() if k[:2] == (name, hf)}

                if name == "att0":
                    pe.wait_ge(ctxT_loaded[hf], 16)
                    feats(at["d", "k"], sm("wk"), CT[:, hf, :], dve_drained, dve_filled)
                    tokens(at["d", "v"], CT[:, hf, :], sm("wv"), D)
                    inputs(name, hf, at)
                    pe.wait_ge(act_drained, at["a", "xt"].drained)
                    feats(at["d", "q"], sm("wq"), XT[:, hf, :], dve_drained, dve_filled)
                    pe.wait_ge(er_stacked, 16 * len(PARTS_B))
                    pe.wait_ge(stacked_q, seen(stacked_q, 16 * len(PARTS_A)))
                    qv = q6[:, :, :].rearrange("k h (c i) -> k c h i", i=P)
                    for c in range(16):
                        b_ = bank(at["d", "rel", c], dve_drained)
                        for u in range(8):
                            i = 8 * c + u
                            last = mm(b_[:, u * 64:(u + 1) * 64], er6[:, S - 1 - i:S - 1 - i + P], qv[:, :, :, i],
                                      start=True, stop=True)
                        last.then_inc(dve_filled, 1)
                        if c % 2:
                            b_ = bank(at["a", "rel", c // 2], act_drained)
                            for u in range(16):
                                i = 16 * (c // 2) + u
                                last = mm(b_[:, u * 32:(u + 1) * 32], er6[:, P - 1 - i:2 * P - 1 - i],
                                          qv[:, 1::2, :, i], start=True, stop=True)
                            last.then_inc(act_filled, 1)
                    pe.wait_ge(stacked_k, seen(stacked_k, 16 * len(PARTS_B)))
                    pe.wait_ge(dve_drained, at["d", "rel", 15].drained)
                    pe.wait_ge(act_drained, at["a", "rel", 7].drained)
                    for i in range(NB * H + 3):
                        if i < NB * H:
                            b, h = divmod(i, H)
                            s_ = bank(at["s", "scores", i], score_drained)
                            q0 = b * S
                            mm(s_[:, 0:P], relD[:, 2 * b * H + h, :], ident, start=True, turn=True)
                            mm(s_[:, P:2 * P], relO[:, b * H + h, :], ident, start=False, turn=True)
                            mm(s_[:, 2 * P:3 * P], relD[:, (2 * b + 1) * H + h, :], ident, start=False, turn=True)
                            mm(s_[:, 0:P], q6[:, h, q0:q0 + P], k6[:, h, q0:q0 + P], start=False)
                            mm(s_[:, P:3 * P], q6[:, h, q0 + P:q0 + S], k6[:, h, q0:q0 + S], start=False, stop=True)\
                                .then_inc(score_filled, 1)
                        if 2 <= i < NB * H + 2:
                            n = i - 2
                            pt = bank(at["d", "probs", n], dve_drained)
                            pe.wait_ge(score_drained, at["s", "scores", n].drained)
                            for k in range(3):
                                last = mm(pt[:, k * P:(k + 1) * P], probs[n % 3][:, k * P:(k + 1) * P], ident,
                                          start=(k == 0), stop=True, turn=True)
                            last.then_inc(dve_filled, 1)
                        if i >= 3:
                            n = i - 3
                            b, h = divmod(n, H)
                            if h == 0:
                                o_ = bank(at["o", "out", b], out_drained)[:, 0:2 * H * (HD + 1)]\
                                    .rearrange("p (a h e) -> p a h e", a=2, h=H)
                            if n == 0:
                                pe.wait_ge(dve_drained, at["d", "v"].drained)
                                pe.wait_ge(consts_done, 1)
                            pe.wait_ge(dve_drained, at["d", "probs", n].drained)
                            pt = probsT[n % 3]
                            mm(o_[:, 0, h, :], pt[:, 0:P], V9[:, 2 * b, h, :], start=(h == 0))
                            mm(o_[:, 1, h, :], pt[:, P:2 * P], V9[:, 2 * b, h, :], start=False)
                            last = mm(o_[:, 1, h, :], pt[:, 2 * P:3 * P], V9[:, 2 * b + 1, h, :], start=False, stop=True)
                            if h == H - 1:
                                last.then_inc(out_filled, 1)

                if name == "ffn0":
                    inputs(name, hf, at)
                    if hf == 0:
                        pe.wait_ge(rest_loaded, 16)
                    pe.wait_ge(act_drained, at["a", "xt"].drained)
                    tokens(at["d", "logits"], XT[:, hf, :], sm("g0w"), 2)
                    w1_ = w0[:, W0["w1"][0]:].rearrange("p (e c f) -> p e c f", e=6, c=F0)
                    w2_ = w0[:, W0["w2"][0]:].rearrange("p (e c d) -> p e c d", e=3, c=F0)
                    o_ = bank(at["o", "out"], out_drained)
                    for t in range(T):
                        mm(o_[:, t * P:(t + 1) * P], sm("ones", 3), sm("b2s", 3), start=(t == 0))
                    if hf == 0:
                        pe.wait_ge(w0_loaded, 16)

                    def first(e, rhs):
                        for c in range(F0):
                            feats(at["a", "h", e, c], w1_[:, e, c, :], rhs, act_drained, act_filled)

                    def then(k):
                        e = FFN0_ORDER[k]
                        second(at["o", "out"], F0, lambda c: w2_[:, e, c, :], k % 2, act_drained,
                               at["a", "h", e, F0 - 1].drained, first=False, close=(k == 2))

                    first(2, XT[:, hf, :])
                    for m in range(2):
                        pe.wait_ge(masked_ready, seen(masked_ready))
                        turn_tiles(at["a", "masked", m], msk[m])
                    pe.wait_ge(act_drained, at["a", "masked", 0].drained)
                    first(0, turned[:, 0, :])
                    then(0)
                    pe.wait_ge(act_drained, at["a", "masked", 1].drained)
                    first(1, turned[:, 1, :])
                    then(1)
                    then(2)

                if name == "att1":
                    o_ = bank(at["o", "out"], out_drained).rearrange("p (t d) -> p t d", t=T)
                    for dl in range(H):
                        pe.wait_ge(av1_ready, seen(av1_ready))
                        w = D - HD * dl
                        last = mm(o_[:, :, HD * dl:D], ident, prod1[dl % 3][:, :, 0:w], start=(dl == 0), stop=(dl == H - 1))
                        last.then_inc(av1_used if dl < H - 1 else out_filled, 1)

                if name in ("ffn1", "ffn2"):
                    E, C = EXPERTS[name], CHUNKS[name]
                    inputs(name, hf, at)
                    pe.wait_ge(act_drained, at["a", "xt"].drained)
                    if name == "ffn1":
                        tokens(at["d", "logits"], XT[:, hf, :], sm("g1w"), E1)
                        cols, w_ = W1, w1
                    else:
                        tokens(at["d", "logits"], XT[:, hf, :], sm("g2w"), E2)
                        cols, w_ = W2, w2
                    if hf == 0:
                        pe.wait_ge(w1_loaded if name == "ffn1" else w2_loaded, 16)
                    wg, wu, wd = [w_[:, cols[k][0]:cols[k][0] + cols[k][1]].rearrange("p (e c f) -> p e c f", e=E, c=C)
                                  for k in ("w1", "w3", "w2")]

                    def down(e):
                        g = e if name == "ffn2" else FFN1_ORDER[e]
                        second(at["o", "y", e], C, lambda c: wd[:, g, c, :], e % 2, dve_drained,
                               at["d", "up", e, C - 1].drained)

                    for e in range(E):
                        g = e if name == "ffn2" else FFN1_ORDER[e]
                        for c in range(C):
                            feats(at["a", "gate", e, c], wg[:, g, c, :], XT[:, hf, :], act_drained, act_filled)
                            feats(at["d", "up", e, c], wu[:, g, c, :], XT[:, hf, :], dve_drained, dve_filled)
                        if e:
                            down(e - 1)
                    down(E - 1)

                if name == "att2":
                    inputs(name, hf, at)
                    pe.wait_ge(act_drained, at["a", "xt"].drained)
                    gw = sm("mgw").rearrange("p (k m) -> p k m", k=3)
                    b_ = bank(at["d", "gates"], dve_drained)
                    mm(b_[0:64, :], gw[:, 0, :], XT[:, hf, :], start=True)
                    mm(b_[0:64, :], gw[:, 1, :], CT[:, hf, :], start=False)
                    mm(b_[0:64, :], gw[:, 2, :], CT[:, hf, :], start=False, stop=True).then_inc(dve_filled, 1)
                    b_ = bank(at["d", "cols"], dve_drained)
                    pe.wait_ge(rows_ready, seen(rows_ready))
                    pe.wait_ge(em_ready, seen(em_ready))
                    for k, src in enumerate((row[2], row[0])):
                        for t in range(T):
                            last = mm(b_[:, (k * T + t) * MH:(k * T + t + 1) * MH], src[:, t * P:(t + 1) * P],
                                      ident[0:MH, 0:MH], start=True, stop=True)
                    last.then_inc(dve_filled, 1)
                    outs = [bank(at["o", "out", b], out_drained)[:, 0:2 * MH * (MD + 1)]
                            .rearrange("p (a h e) -> p a h e", a=2, h=MH) for b in range(NB)]
                    if hf == 0:
                        pe.wait_ge(v33_done, 1)
                    sel = sm("sel", MH).rearrange("p (h m) -> p h m", h=MH)

                    def values(k):
                        h, b = divmod(k, NB)
                        pe.wait_ge(dve_drained, at["d", "scores", h, b].drained)
                        c_ = cmat[k % 2]
                        o_ = outs[b]
                        mm(o_[:, 0, h, :], c_[:, 0:P], V33[:, hf, 2 * b, h, :], start=(h == 0))
                        mm(o_[:, 1, h, :], c_[:, P:2 * P], V33[:, hf, 2 * b, h, :], start=False)
                        last = mm(o_[:, 1, h, :], c_[:, 2 * P:3 * P], V33[:, hf, 2 * b + 1, h, :], start=False, stop=True)
                        if h == MH - 1:
                            last.then_inc(out_filled, 1)

                    for h in range(MH):
                        mm(bank(at["d", "rows", h], dve_drained), sel[:, h, :], row[3], start=True, stop=True)\
                            .then_inc(dve_filled, 1)
                        hs = slice(MD * h, MD * (h + 1))
                        for b in range(NB):
                            b_ = bank(at["d", "scores", h, b], dve_drained)
                            k0, k1, k2 = b * S, b * S + P, (b + 1) * S
                            mm(b_[:, 0:S], CT[hs, hf, k0:k1], XT[hs, hf, k0:k2], start=True, stop=True)
                            mm(b_[:, S:S + P], CT[hs, hf, k1:k2], XT[hs, hf, k1:k2], start=True, stop=True)\
                                .then_inc(dve_filled, 1)
                            k = NB * h + b
                            if k:
                                values(k - 1)
                    values(NB * MH - 1)

                if name == "att3":
                    feats(at["d", "k"], sm("rwk"), CT[:, hf, :], dve_drained, dve_filled)
                    feats(at["d", "ks"], sm("rwks"), CT[:, hf, :], dve_drained, dve_filled)
                    tokens(at["a", "v"], CT[:, hf, :], sm("rwv"), D, (act_drained, act_filled))
                    inputs(name, hf, at)
                    pe.wait_ge(act_drained, at["a", "xt"].drained)
                    feats(at["d", "q"], sm("rwq"), XT[:, hf, :], dve_drained, dve_filled)
                    feats(at["d", "qs"], sm("rwqs"), XT[:, hf, :], dve_drained, dve_filled)
                    tokens(at["d", "gate"], XT[:, hf, :], sm("rgw"), D)
                    pe.wait_ge(stacked_k, seen(stacked_k, 16 * len(PARTS_B)))
                    pe.wait_ge(stacked_q, seen(stacked_q, 16 * len(PARTS_A)))

                    def retained(b, p_):
                        pe.wait_ge(dve_drained, at["d", "diag", b, p_].drained)
                        pe.wait_ge(act_drained, at["a", "off", b, p_ // 2].drained)
                        for k in range(2):
                            h = 2 * p_ + k
                            off = gated[:, (p_ // 2) % 2, :].rearrange("p (h i) -> p h i", h=4)[:, h % 4, :]
                            d_ = diag[p_ % 2]
                            hs = slice(HD * h, HD * (h + 1))
                            mm(o_[:, 0, hs], d_[:, k, 0, :], V3[:, 2 * b, hs], start=(h == 0))
                            mm(o_[:, 1, hs], off, V3[:, 2 * b, hs], start=False)
                            last = mm(o_[:, 1, hs], d_[:, k, 1, :], V3[:, 2 * b + 1, hs], start=False, stop=True)
                        if p_ == H // 2 - 1:
                            last.then_inc(out_filled, 1)

                    for b in range(NB):
                        o_ = bank(at["o", "out", b], out_drained)[:, 0:2 * D].rearrange("p (a d) -> p a d", a=2)
                        k0, k1, k2 = b * S, b * S + P, (b + 1) * S
                        for p_ in range(H // 2):
                            if p_ % 2 == 0:
                                b_ = bank(at["a", "off", b, p_ // 2], act_drained)
                                for k in range(4):
                                    h = 2 * p_ + k
                                    last = mm(b_[:, k * P:(k + 1) * P], k6[:, h, k0:k1], q6[:, h, k1:k2], start=True, stop=True)
                                last.then_inc(act_filled, 1)
                            b_ = bank(at["d", "diag", b, p_], dve_drained)
                            for k in range(2):
                                h = 2 * p_ + k
                                mm(b_[:, 2 * k * P:(2 * k + 1) * P], k6[:, h, k0:k1], q6[:, h, k0:k1], start=True, stop=True)
                                last = mm(b_[:, (2 * k + 1) * P:(2 * k + 2) * P], k6[:, h, k1:k2], q6[:, h, k1:k2],
                                          start=True, stop=True)
                            last.then_inc(dve_filled, 1)
                            if p_:
                                retained(b, p_ - 1)
                        retained(b, H // 2 - 1)
                    pe.wait_ge(y3_ready, seen(y3_ready))
                    turn_tiles(at["a", "yt"], fval.rearrange("p (t d) -> p t d", t=T))
                    pe.wait_ge(act_drained, at["a", "yt"].drained)
                    tokens(at["d", "proj"], turned[:, 0, :], sm("row"), D)

                if name[:3] == "moe":
                    l = int(name[3])
                    w_ = w3[l % 2]
                    wa = w_[:, 0:W3["w1"][1]].rearrange("p (e c f) -> p e c f", e=E3, c=F0)
                    wb = w_[:, W3["w2"][0]:].rearrange("p (e c d) -> p e c d", e=E3, c=F0)
                    pe.wait_ge(norm_done[hf], NORM[name])
                    turn_tiles(at["a", "xt"], XN[:, hf, :, :] if l == 0 else Z[l % 2][hf])
                    turn_tiles(at["a", "xh"], XH[:, hf, :, :])
                    pe.wait_ge(act_drained, at["a", "xt"].drained)
                    tokens(at["d", "logits"], XT[:, hf, :], sm("g3w")[:, l * E3:(l + 1) * E3], E3)
                    if hf == 0:
                        pe.wait_ge(w3_loaded[l % 2], 16 * (l // 2 + 1))

                    def down(e):
                        second(at["o", "y", e], F0, lambda c: wb[:, e, c, :], e % 2, act_drained,
                               at["a", "h", e, F0 - 1].drained)

                    for e in range(E3):
                        pe.wait_ge(xe_ready, seen(xe_ready))
                        for c in range(F0):
                            feats(at["a", "h", e, c], wa[:, e, c, :], xe[e % 2], act_drained, act_filled)
                        if e == 0:
                            b_ = bank(at["d", "combT"], dve_drained)
                            pe.wait_ge(comb_ready, seen(comb_ready))
                            for t in range(T):
                                last = mm(b_[0:E3, t * P:(t + 1) * P], comb[:, t * E3:(t + 1) * E3], ident, start=True, stop=True)
                            last.then_inc(dve_filled, 1)
                            pe.wait_ge(dve_drained, at["d", "combT"].drained)
                            tokens(at["d", "bias"], combT[:, :], sm("b2", E3)[:, l * D:(l + 1) * D], D)
                        else:
                            down(e - 1)
                    down(E3 - 1)

        @block.vector
        def _(dve):
            seen = Tally()

            def settle(last):
                last.then_inc(step, 1)
                dve.wait_ge(step, seen(step))

            def rsqrt(last):
                last.then_inc(var_ready, 1)
                dve.wait_ge(rstd_ready, seen(rstd_ready))

            def layernorm(src, dst):
                for t in range(T):
                    last = dve.bn_stats(st6[:, t, :], src[:, t, :])
                settle(last)
                for t in range(T):
                    last = dve.bn_aggr(mv[:, t, :], st6[:, t, :])
                settle(last)
                rsqrt(dve.tensor_scalar(VE[:, 0:T], mv[:, :, 1], 1e-5, None, ALU.add))
                for t in range(T):
                    last = dve.tensor_scalar(dst[:, t, :], src[:, t, :], mv[:, t, 0:1], RS[:, t:t + 1],
                                             ALU.subtract, ALU.mult)
                return last

            n_parts = 0

            def split(src, out_sem):
                nonlocal n_parts
                buf = n_parts % 2
                if n_parts >= 2:
                    dve.wait_ge(parts_out[buf], 16 * (n_parts // 2))
                n_parts += 1
                part = parts[buf]
                settle(dve.tensor_copy(part[:, 0, :], src))
                settle(dve.tensor_tensor(ftmp, src, part[:, 0, :], ALU.subtract))
                settle(dve.tensor_copy(part[:, 1, :], ftmp))
                dve.tensor_tensor(part[:, 2, :], ftmp, part[:, 1, :], ALU.subtract).then_inc(out_sem, 1)

            def bc(ap, shape, axis):
                return ap.unsqueeze(axis).broadcast_to(shape)

            def take(turn):
                dve.wait_ge(dve_filled, turn.filled)
                return BANK[turn.bank]

            def drained(last, turn):
                last.then_inc(dve_drained, 1)
                dve.wait_ge(dve_drained, turn.drained)

            def top2(E, keys, vals, eps):
                K = keys.rearrange("p (t e) -> p t e", t=T)
                n = T * E * E
                gt = rt[:, 0:n].rearrange("p (t e f) -> p t e f", t=T, e=E)
                eq = rt[:, T * 64:T * 64 + n].rearrange("p (t e f) -> p t e f", t=T, e=E)
                mine = bc(K, [P, T, E, E], 3)
                other = bc(K, [P, T, E, E], 2)
                low = bc(sm("low").rearrange("p (e f) -> p e f", e=8)[:, 0:E, 0:E], [P, T, E, E], 1)
                dve.tensor_tensor(gt, other, mine, ALU.is_gt)
                settle(dve.tensor_tensor(eq, other, mine, ALU.is_equal))
                settle(dve.tensor_tensor(eq, eq, low, ALU.mult))
                settle(dve.tensor_tensor(gt, gt, eq, ALU.add))
                C = comb[:, 0:T * E].rearrange("p (t e) -> p t e", t=T)
                settle(dve.tensor_reduce(C, gt, AX, ALU.add))
                dve.wait_ge(weights_ready, seen(weights_ready))
                settle(dve.scalar_tensor_tensor(comb[:, 0:T * E], comb[:, 0:T * E], 1.5, vals, ALU.is_lt, ALU.mult))
                settle(dve.tensor_reduce(rs4[:, 0:T], C, AX, ALU.add))
                if eps:
                    settle(dve.tensor_scalar(rs4[:, 0:T], rs4[:, 0:T], eps, None, ALU.add))
                settle(dve.reciprocal(rs4[:, T:2 * T], rs4[:, 0:T]))
                return dve.tensor_tensor(C, C, bc(rs4[:, T:2 * T], [P, T, E], 2), ALU.mult)

            def softmax_keys(E):
                K = lg[:, 0:T * E].rearrange("p (t e) -> p t e", t=T)
                settle(dve.tensor_reduce(rs4[:, 0:T], K, AX, ALU.max))
                dve.tensor_tensor(K, K, bc(rs4[:, 0:T], [P, T, E], 2), ALU.subtract).then_inc(logits_ready, 1)
                dve.wait_ge(logits_ready, seen(logits_ready))

            def residual(name, hf, src, tiles=slice(0, T)):
                g = GATE[name]
                return dve.scalar_tensor_tensor(X[:, hf, tiles, :], src, TG[:, g:g + 1], X[:, hf, tiles, :],
                                                ALU.mult, ALU.add)

            dve.wait_ge(small_loaded, 16)
            er = sm("er", HD)
            settle(dve.tensor_copy(erp[:, 0, :], er))
            settle(dve.tensor_tensor(erf[:, :], er, erp[:, 0, :], ALU.subtract))
            settle(dve.tensor_copy(erp[:, 1, :], erf[:, :]))
            dve.tensor_tensor(erp[:, 2, :], erf[:, :], erp[:, 1, :], ALU.subtract).then_inc(er_parts, 1)
            for hf in range(2):
                dve.wait_ge(x_loaded[hf], 16)
                layernorm(X[:, hf, :, :], XN[:, hf, :, :]).then_inc(norm_done[hf], 1)
            dve.wait_ge(tanh_done, 1)

            for name, hf in order:
                at = {k[2:]: v for k, v in turns.items() if k[:2] == (name, hf)}

                if name == "att0":
                    turn = at["d", "k"]
                    drained(dve.tensor_scalar(fval, take(turn), sm("bk"), None, ALU.add), turn)
                    split(fval, parts_ready)
                    turn = at["d", "v"]
                    drained(dve.tensor_tensor(V9[:, :, :, 0:HD],
                                              take(turn).rearrange("p (t h e) -> p t h e", t=T, h=H),
                                              bc(sm("bv").rearrange("p (h e) -> p h e", h=H), [P, T, H, HD], 1),
                                              ALU.add), turn)
                    turn = at["d", "q"]
                    drained(dve.tensor_scalar(fval, take(turn), sm("bq"), HD ** -0.5, ALU.add, ALU.mult), turn)
                    split(fval, parts_ready)
                    for c in range(16):
                        turn = at["d", "rel", c]
                        dve.tensor_tensor(relD[:, :, 8 * c:8 * (c + 1)],
                                          take(turn).rearrange("p (u c) -> p c u", c=64),
                                          bc(addmask[:, 8 * c:8 * (c + 1)], [P, 64, 8], 1), ALU.add)\
                           .then_inc(dve_drained, 1)

                    def finish(b):
                        turn = at["o", "out", b]
                        dve.wait_ge(out_filled, turn.filled)
                        o_ = BANK[turn.bank][:, 0:2 * H * (HD + 1)].rearrange("p (a h e) -> p a h e", a=2, h=H)
                        inv = sums[:, 0:2 * H].rearrange("p (a h) -> p a h", a=2)
                        settle(dve.reciprocal(inv, o_[:, :, :, HD]))
                        dst = pad[:, 0:2, :].rearrange("p a (h e) -> p a h e", h=H)
                        dve.tensor_tensor(dst, o_[:, :, :, 0:HD], bc(inv, [P, 2, H, HD], 3), ALU.mult)\
                           .then_inc(out_drained, 1)
                        dve.wait_ge(out_drained, turn.drained)
                        return residual(name, hf, pad[:, 0:2, :], slice(2 * b, 2 * b + 2))

                    for i in range(NB * H + 2):
                        if i < NB * H:
                            turn = at["s", "scores", i]
                            dve.wait_ge(score_filled, turn.filled)
                            dve.tensor_reduce(negmax[:, i % 4, 0:1], BANK[turn.bank][:, 0:P], AX, ALU.max, negate=True)
                            dve.tensor_reduce(negmax[:, i % 4, 1:2], BANK[turn.bank][:, P:3 * P], AX, ALU.max,
                                              negate=True).then_inc(negmax_ready, 1)
                        if i >= 2:
                            turn = at["d", "probs", i - 2]
                            dve.tensor_copy(probsT[(i - 2) % 3], take(turn)[:, 0:3 * P]).then_inc(dve_drained, 1)
                        if i == H + 4:
                            finish(0)
                    settle(finish(1))

                if name == "ffn0":
                    turn = at["d", "logits"]
                    b_ = take(turn)[:, 0:2 * T].rearrange("p (t e) -> p t e", e=2)
                    settle(dve.tensor_copy(lg[:, 0:T], b_[:, :, 1]))
                    drained(dve.tensor_tensor(comb[:, 0:T], b_[:, :, 0], lg[:, 0:T], ALU.is_ge), turn)
                    for t in range(T):
                        last = dve.tensor_scalar(msk[0][:, t, :], XN[:, hf, t, :], comb[:, t:t + 1], None, ALU.mult)
                    last.then_inc(masked_ready, 1)
                    dve.wait_ge(masked_ready, seen(masked_ready))
                    dve.tensor_tensor(msk[1], XN[:, hf, :, :], msk[0], ALU.subtract).then_inc(masked_ready, 1)
                    seen(masked_ready)
                    turn = at["o", "out"]
                    dve.wait_ge(out_filled, turn.filled)
                    residual(name, hf, BANK[turn.bank].rearrange("p (t d) -> p t d", t=T)).then_inc(out_drained, 1)
                    dve.wait_ge(out_drained, turn.drained)

                if name == "att1":
                    xn, cx = XN[:, hf, :, :], CX[:, hf, :, :]
                    if hf == 0:
                        dve.wait_ge(ctx_loaded, 32)
                    settle(dve.memset(sc1, NEG))
                    for dl in range(H):
                        w = D - HD * dl
                        pb = prod1[dl % 3][:, :, 0:w]
                        settle(dve.tensor_tensor(pb, xn[:, :, HD * dl:D], cx[:, :, 0:w], ALU.mult))
                        last = dve.tensor_reduce(sc1[:, :, dl:H, dl], pb.rearrange("p t (h e) -> p t h e", e=HD), AX, ALU.add)
                    settle(last)
                    mx = sums[:, 0:T * H].rearrange("p (t h) -> p t h", t=T)
                    settle(dve.tensor_reduce(mx, sc1, AX, ALU.max))
                    dve.tensor_tensor(sc1, sc1, bc(mx, [P, T, H, H], 3), ALU.subtract).then_inc(shifted1, 1)
                    dve.wait_ge(expd1, seen(expd1))
                    settle(dve.tensor_reduce(mx, sc1, AX, ALU.add))
                    settle(dve.reciprocal(mx, mx))
                    settle(dve.tensor_tensor(sc1, sc1, bc(mx, [P, T, H, H], 3), ALU.mult))
                    for dl in range(H):
                        w = D - HD * dl
                        if dl >= 3:
                            dve.wait_ge(av1_used, (H - 1) * hf + dl - 2)
                        for t in range(T):
                            last = dve.tensor_tensor(prod1[dl % 3][:, t, 0:w].rearrange("p (h e) -> p h e", e=HD),
                                                     cx[:, t, 0:w].rearrange("p (h e) -> p h e", e=HD),
                                                     bc(sc1[:, t, dl:H, dl], [P, H - dl, HD], 2), ALU.mult)
                        last.then_inc(av1_ready, 1)
                    turn = at["o", "out"]
                    dve.wait_ge(out_filled, turn.filled)
                    residual(name, hf, BANK[turn.bank].rearrange("p (t d) -> p t d", t=T)).then_inc(out_drained, 1)
                    dve.wait_ge(out_drained, turn.drained)

                if name in ("ffn1", "ffn2"):
                    E, C = EXPERTS[name], CHUNKS[name]
                    R = E1 if name == "ffn1" else E2
                    turn = at["d", "logits"]
                    K = lg[:, 0:T * R].rearrange("p (t e) -> p t e", t=T)
                    src = take(turn)[:, 0:T * R].rearrange("p (t e) -> p t e", t=T)
                    if name == "ffn1":
                        dve.tensor_tensor(K, src, bc(sm("g1b"), [P, T, R], 1), ALU.add).then_inc(dve_drained, 1)
                        dve.wait_ge(dve_drained, turn.drained)
                        dve.tensor_scalar(K, K, 17.0, -87.0, ALU.min, ALU.max).then_inc(logits_ready, 1)
                        dve.wait_ge(logits_ready, seen(logits_ready))
                    else:
                        drained(dve.tensor_copy(K, src), turn)
                        softmax_keys(R)

                    def product(e):
                        for c in range(C):
                            u, g = at["d", "up", e, c], at["a", "gate", e, c]
                            k = e * C + c
                            b_ = take(u)
                            dve.wait_ge(act_drained, g.drained)
                            dve.tensor_tensor(hidden[:, e % 2, c, :], b_, gated[:, k % 2, :], ALU.mult)\
                               .then_inc(dve_drained, 1)

                    def gather(e):
                        turn = at["o", "y", e]
                        dve.wait_ge(out_filled, turn.filled)
                        y = BANK[turn.bank].rearrange("p (t d) -> p t d", t=T)
                        g = e if name == "ffn2" else FFN1_ORDER[e]
                        if g == E1 and name == "ffn1":
                            last = dve.tensor_copy(acc, y)
                        else:
                            for t in range(T):
                                w = comb[:, t * R + g:t * R + g + 1]
                                if e == 0:
                                    last = dve.tensor_scalar(acc[:, t, :], y[:, t, :], w, None, ALU.mult)
                                else:
                                    last = dve.scalar_tensor_tensor(acc[:, t, :], y[:, t, :], w, acc[:, t, :],
                                                                    ALU.mult, ALU.add)
                        last.then_inc(out_drained, 1)
                        dve.wait_ge(out_drained, turn.drained)

                    product(0)
                    settle(top2(R, lg[:, 0:T * R], pr[:, 0:T * R], 1e-8 if name == "ffn1" else 0))
                    for e in range(1, E):
                        product(e)
                        gather(e - 1)
                    gather(E - 1)
                    settle(residual(name, hf, acc))

                if name == "att2":
                    turn = at["d", "gates"]
                    drained(dve.tensor_scalar(grow, take(turn)[0:64, :], sm("mgb", 64), None, ALU.add), turn)
                    fg, ig = grow[32:32 + MH, :], grow[0:MH, :]
                    settle(dve.tensor_scalar(row[4], fg, 0.0, None, ALU.min))
                    dve.wait_ge(flog_ready, seen(flog_ready))
                    settle(dve.tensor_tensor(row[4], row[4], row[1], ALU.subtract))
                    for b in range(NB):
                        bs = slice(b * S, (b + 1) * S)
                        last = dve.tensor_tensor_scan(row[0][:, bs], row[4][:, bs], row[4][:, bs], 0.0, ALU.add, ALU.bypass)
                    settle(last)
                    settle(dve.tensor_tensor(row[2], ig, row[0], ALU.subtract))
                    for b in range(NB):
                        bs = slice(b * S, (b + 1) * S)
                        last = dve.tensor_tensor_scan(row[3][:, bs], row[2][:, bs], row[2][:, bs], -3e38, ALU.max, ALU.max)
                    settle(last)
                    dve.tensor_tensor(row[0], row[0], row[3], ALU.add).then_inc(emarg_ready, 1)
                    dve.wait_ge(emarg_ready, seen(emarg_ready))
                    dve.tensor_scalar(row[3], row[3], -1.0, None, ALU.mult).then_inc(rows_ready, 1)
                    turn = at["d", "cols"]
                    b_ = take(turn)
                    dve.tensor_copy(ae[0][:, :, :], b_[:, 0:T * MH].rearrange("p (t h) -> p t h", t=T))
                    drained(dve.tensor_copy(ae[1][:, :, :], b_[:, T * MH:2 * T * MH].rearrange("p (t h) -> p t h", t=T)), turn)
                    for h in range(MH):
                        turn = at["d", "rows", h]
                        b_ = take(turn)
                        d_ = decay[h % 2]
                        for b in range(NB):
                            t0 = 2 * b
                            dve.scalar_tensor_tensor(d_[:, b, 0:S], b_[:, b * S:(b + 1) * S], ae[0][:, t0, h:h + 1],
                                                     addmask, ALU.add, ALU.min)
                            last = dve.scalar_tensor_tensor(d_[:, b, S:S + P], b_[:, b * S + P:(b + 1) * S],
                                                            ae[0][:, t0 + 1, h:h + 1], addmask[:, 0:P], ALU.add, ALU.min)
                        last.then_inc(dve_drained, 1)
                        dve.wait_ge(dve_drained, turn.drained)
                        dve.engine_nop().then_inc(dexp_in, 1)
                        dve.wait_ge(dexp_ready, seen(dexp_ready))
                        for b in range(NB):
                            turn = at["d", "scores", h, b]
                            dve.scalar_tensor_tensor(cmat[b], take(turn)[:, 0:3 * P], MD ** -0.5, d_[:, b, :],
                                                     ALU.mult, ALU.mult).then_inc(dve_drained, 1)
                    n_ = sums[:, 0:T * MH].rearrange("p (t h) -> p t h", t=T)
                    for b in range(NB):
                        turn = at["o", "out", b]
                        dve.wait_ge(out_filled, turn.filled)
                        o_ = BANK[turn.bank][:, 0:2 * MH * (MD + 1)].rearrange("p (a h e) -> p a h e", a=2, h=MH)
                        tb = slice(2 * b, 2 * b + 2)
                        settle(dve.tensor_tensor(n_[:, tb, :], o_[:, :, :, MD], ae[1][:, tb, :], ALU.max))
                        settle(dve.tensor_scalar(n_[:, tb, :], n_[:, tb, :], 1e-6, None, ALU.add))
                        settle(dve.reciprocal(n_[:, tb, :], n_[:, tb, :]))
                        dve.tensor_tensor(mout[:, tb, :, :], o_[:, :, :, 0:MD], bc(n_[:, tb, :], [P, 2, MH, MD], 3),
                                          ALU.mult).then_inc(out_drained, 1)
                        dve.wait_ge(out_drained, turn.drained)
                    settle(dve.tensor_tensor(msq, mout, mout, ALU.mult))
                    settle(dve.tensor_reduce(n_, msq, AX, ALU.add))
                    rsqrt(dve.tensor_scalar(VE[:, 0:T * MH], sums[:, 0:T * MH], 1.0 / MD, 1e-6, ALU.mult, ALU.add))
                    settle(dve.tensor_tensor(mout, mout, bc(RS[:, 0:T * MH].rearrange("p (t h) -> p t h", t=T),
                                                           [P, T, MH, MD], 3), ALU.mult))
                    settle(dve.tensor_scalar(rms1[:, :], sm("rms"), 1.0, None, ALU.add))
                    m3 = mout.rearrange("p t h e -> p (t h) e")
                    settle(dve.tensor_tensor(m3, m3, bc(rms1[:, :], [P, T * MH, MD], 1), ALU.mult))
                    settle(residual(name, hf, mout.rearrange("p t h e -> p t (h e)")))

                if name == "att3":
                    def xpos(w, ws, cos, sin):
                        shape = [P, NB, S]
                        turn = at["d", w]
                        drained(dve.tensor_tensor(fval.rearrange("p (b s) -> p b s", b=NB),
                                                  take(turn).rearrange("p (b s) -> p b s", b=NB),
                                                  bc(sm(cos), shape, 1), ALU.mult), turn)
                        turn = at["d", ws]
                        drained(dve.tensor_tensor(ftmp.rearrange("p (b s) -> p b s", b=NB),
                                                  take(turn).rearrange("p (b s) -> p b s", b=NB),
                                                  bc(sm(sin), shape, 1), ALU.mult), turn)
                        settle(dve.tensor_tensor(fval, fval, ftmp, ALU.add))
                        split(fval, parts_ready)

                    xpos("k", "ks", "kcos", "ksin")
                    xpos("q", "qs", "qcos", "qsin")
                    turn = at["d", "gate"]
                    dve.tensor_tensor(gate3, take(turn).rearrange("p (t d) -> p t d", t=T),
                                      bc(sm("rgb"), [P, T, D], 1), ALU.add).then_inc(dve_drained, 1)
                    dve.wait_ge(dve_drained, turn.drained)
                    dve.engine_nop().then_inc(gate3_in, 1)
                    for b in range(NB):
                        for p_ in range(H // 2):
                            turn = at["d", "diag", b, p_]
                            dve.tensor_tensor(diag[p_ % 2].rearrange("p a b i -> p (a b) i"),
                                              take(turn).rearrange("p (a i) -> p a i", a=4),
                                              bc(sm("keep"), [P, 4, P], 1), ALU.mult).then_inc(dve_drained, 1)
                        turn = at["o", "out", b]
                        dve.wait_ge(out_filled, turn.filled)
                        dve.tensor_copy(ret[:, 2 * b:2 * b + 2, :, :].rearrange("p t h e -> p t (h e)"),
                                        BANK[turn.bank][:, 0:2 * D].rearrange("p (t d) -> p t d", t=2)).then_inc(out_drained, 1)
                        dve.wait_ge(out_drained, turn.drained)
                    mu = sums[:, 0:T * H].rearrange("p (t h) -> p t h", t=T)
                    settle(dve.tensor_reduce(mu, ret, AX, ALU.add))
                    settle(dve.tensor_scalar(sums[:, 0:T * H], sums[:, 0:T * H], 1.0 / HD, None, ALU.mult))
                    settle(dve.tensor_tensor(ret, ret, bc(mu, [P, T, H, HD], 3), ALU.subtract))
                    settle(dve.tensor_tensor(retsq, ret, ret, ALU.mult))
                    settle(dve.tensor_reduce(mu, retsq, AX, ALU.add))
                    rsqrt(dve.tensor_scalar(VE[:, 0:T * H], sums[:, 0:T * H], 1.0 / HD, 1e-5, ALU.mult, ALU.add))
                    settle(dve.tensor_tensor(ret, ret, bc(RS[:, 0:T * H].rearrange("p (t h) -> p t h", t=T),
                                                         [P, T, H, HD], 3), ALU.mult))
                    dve.wait_ge(gate3_ready, seen(gate3_ready))
                    dve.tensor_tensor(fval, ret.rearrange("p t h e -> p (t h e)"), gate3.rearrange("p t d -> p (t d)"),
                                      ALU.mult).then_inc(y3_ready, 1)
                    turn = at["d", "proj"]
                    drained(dve.tensor_tensor(pad, take(turn).rearrange("p (t d) -> p t d", t=T),
                                              bc(sm("rob"), [P, T, D], 1), ALU.add), turn)
                    settle(residual(name, hf, pad))

                if name[:3] == "moe":
                    l = int(name[3])
                    z = XN[:, hf, :, :] if l == 0 else Z[l % 2][hf]
                    znew = Z[(l + 1) % 2][hf]

                    def expert_input(e):
                        if e >= 2:
                            dve.wait_ge(act_filled, at["a", "h", e - 2, F0 - 1].filled)
                        k = l * E3 + e
                        dve.tensor_scalar(xe[e % 2], turned[:, hf, :], sm("lng")[:, k:k + 1], sm("lnb")[:, k:k + 1],
                                          ALU.mult, ALU.add).then_inc(xe_ready, 1)

                    dve.wait_ge(act_drained, at["a", "xh"].drained)
                    expert_input(0)
                    expert_input(1)
                    turn = at["d", "logits"]
                    K = lg[:, 0:T * E3].rearrange("p (t e) -> p t e", t=T)
                    src = take(turn)[:, 0:T * E3].rearrange("p (t e) -> p t e", t=T)
                    rb = bc(sm("g3b")[:, l * E3:(l + 1) * E3], [P, T, E3], 1)
                    drained(dve.tensor_tensor(K, src, rb, ALU.add), turn)
                    softmax_keys(E3)
                    top2(E3, lg[:, 0:T * E3], pr[:, 0:T * E3], 0).then_inc(comb_ready, 1)
                    dve.wait_ge(comb_ready, seen(comb_ready))
                    C = comb[:, 0:T * E3].rearrange("p (t e) -> p t e", t=T)
                    settle(dve.tensor_reduce(rs4[:, 0:T], C, AX, ALU.add))
                    turn = at["d", "combT"]
                    drained(dve.tensor_copy(combT[:, :], take(turn)[0:E3, :]), turn)
                    turn = at["d", "bias"]
                    b_ = take(turn)
                    for t in range(T):
                        last = dve.scalar_tensor_tensor(znew[:, t, :], z[:, t, :], rs4[:, t:t + 1], b_[:, t * D:(t + 1) * D],
                                                        ALU.mult, ALU.add)
                    drained(last, turn)
                    for e in range(E3):
                        if e + 2 < E3:
                            expert_input(e + 2)
                        turn = at["o", "y", e]
                        dve.wait_ge(out_filled, turn.filled)
                        for t in range(T):
                            last = dve.scalar_tensor_tensor(znew[:, t, :], BANK[turn.bank][:, t * D:(t + 1) * D],
                                                            comb[:, t * E3 + e:t * E3 + e + 1], znew[:, t, :],
                                                            ALU.mult, ALU.add)
                        last.then_inc(out_drained, 1)
                        dve.wait_ge(out_drained, turn.drained)
                    if l == L3 - 1:
                        residual(name, hf, znew).then_inc(x_done[hf], 1)
                    else:
                        layernorm(znew, XH[:, hf, :, :]).then_inc(norm_done[hf], 1)

                if name == "att3":
                    settle(layernorm(X[:, hf, :, :], XN[:, hf, :, :]))
                    layernorm(XN[:, hf, :, :], XH[:, hf, :, :]).then_inc(norm_done[hf], 1)
                elif name[:3] != "moe":
                    layernorm(X[:, hf, :, :], XN[:, hf, :, :]).then_inc(norm_done[hf], 1)
            if debug_x:
                for hf in range(2):
                    dve.engine_nop().then_inc(x_done[hf], 1)


def tables():
    j, i = np.arange(P)[:, None], np.arange(P)[None, :]
    c = {"ident": np.eye(P), "ones": np.ones((P, P)), "keep": i >= j}
    c["addmask"] = np.concatenate([np.where(i >= j, 0.0, NEG), np.zeros((P, P))], 1)
    e = np.arange(8)
    c["low"] = np.broadcast_to((e[None, :] < e[:, None]).reshape(1, 64), (P, 64))
    sel = np.zeros((P, MH, P))
    for h in range(MH):
        sel[h, h] = 1
    c["sel"] = sel.reshape(P, MH * P)
    half = HD // 2
    f = np.float32
    base = (np.arange(0, HD, 2, dtype=f) + f(0.4 * HD)) / f(1.4 * HD)
    power = np.arange(-(S // 2), S - S // 2, dtype=f) / f(512.0)
    scale = base[None, :].astype(np.float64) ** power[:, None]
    freq = f(1.0) / f(10000.0) ** (np.arange(half, dtype=f) / f(half))
    ang = (np.arange(S, dtype=f)[:, None] * freq[None, :].astype(f)).astype(np.float64)
    gam = f(1.0) - np.exp(np.linspace(np.log(1.0 / 32.0), np.log(1.0 / 512.0), H)).astype(f)
    pos = np.arange(S)
    sign = np.where(np.arange(HD) % 2 == 0, -1.0, 1.0)
    for w, sc, g in (("q", scale, pos), ("k", 1 / scale, -pos)):
        decay = gam[:, None].astype(np.float64) ** g[None, :]
        cos = np.repeat((np.cos(ang) * sc).T, 2, axis=0)
        sin = np.repeat((np.sin(ang) * sc).T, 2, axis=0) * sign[:, None]
        c[w + "cos"] = (decay[:, None, :] * cos[None]).reshape(P, S)
        c[w + "sin"] = (decay[:, None, :] * sin[None]).reshape(P, S)
    return {k: np.asarray(v, np.float32) for k, v in c.items()}


def pack(columns, n, parts):
    a = np.zeros((P, n), np.float32)
    for name, v in parts.items():
        at, w = columns[name]
        v = v.reshape(v.shape[0], -1)
        assert v.shape[1] == w, (name, v.shape, w)
        a[:v.shape[0], at:at + w] = v
    return a


def layout(i):
    def rows(v):
        return np.broadcast_to(v.reshape(1, -1), (P, v.size))

    def swap(w):
        return np.ascontiguousarray(w.reshape(D, H, HD // 2, 2)[..., ::-1]).reshape(D, D)

    def heads(w):
        return w.transpose(1, 0, 2).reshape(D, D)

    s = dict(tables())
    s["wq"], s["wk"], s["wv"] = i["L0_xattn_Wq"].T, i["L0_xattn_Wk"].T, i["L0_xattn_Wv"].T
    s["bq"], s["bk"], s["bv"] = i["L0_xattn_bq"][:, None], i["L0_xattn_bk"][:, None], rows(i["L0_xattn_bv"])
    s["gates"] = rows(np.concatenate([i["g_xattn"], i["g_ffn"]]))
    er = np.zeros((HD, 384), np.float32)
    er[:, 0:S] = i["L0_xattn_Er"].T
    s["er"] = er
    s["g0w"], s["g1w"], s["g1b"], s["g2w"] = i["L0_ffn_gate_w"].T, i["L1_ffn_gate_w"].T, rows(i["L1_ffn_gate_b"]), i["L2_ffn_wg"].T
    s["g3w"], s["g3b"] = i["L3_ffn_router_w"].transpose(1, 0, 2), rows(i["L3_ffn_router_b"])
    s["s0b1"] = np.concatenate([i["L0_ffn_b1"], i["L0_ffn_sb1"][None]]).reshape(3, F0, P).transpose(2, 0, 1)
    s["b2s"] = np.concatenate([i["L0_ffn_b2"], i["L0_ffn_sb2"][None]])
    s["rms"] = rows(i["L2_xattn_rms_scale"])
    mg = np.zeros((D, 3, 64), np.float32)
    mg[:, :, 0:MH] = i["L2_xattn_igate_kernel"].reshape(3, D, MH).transpose(1, 0, 2)
    mg[:, :, 32:32 + MH] = i["L2_xattn_fgate_kernel"].reshape(3, D, MH).transpose(1, 0, 2)
    s["mgw"] = mg
    mb = np.zeros((P, 1), np.float32)
    mb[0:MH, 0], mb[32:32 + MH, 0] = i["L2_xattn_igate_bias"], i["L2_xattn_fgate_bias"]
    s["mgb"] = mb
    s["b2"] = i["L3_ffn_b2"].transpose(1, 0, 2)
    s["lng"], s["lnb"] = i["L3_ffn_ln_g"].reshape(L3 * E3, D).T, i["L3_ffn_ln_b"].reshape(L3 * E3, D).T
    s["b1"] = i["L3_ffn_b1"].reshape(L3 * E3 * F0, P).T
    wq, wk = heads(i["L3_xattn_W_Q"]), heads(i["L3_xattn_W_K"])
    s["rwq"], s["rwqs"], s["rwk"], s["rwks"], s["rwv"] = wq, swap(wq), wk, swap(wk), heads(i["L3_xattn_W_V"])
    s["rgw"], s["rgb"], s["row"], s["rob"] = i["L3_xattn_g_w"].T, rows(i["L3_xattn_g_b"]), i["L3_xattn_out_w"].T, rows(i["L3_xattn_out_b"])
    small = pack(SMALL, NSMALL, s)
    w0 = pack(W0, NW0, {
        "w1": np.concatenate([i["L0_ffn_w1"], i["L0_ffn_sw1"][None]]).transpose(1, 0, 2),
        "w2": np.concatenate([i["L0_ffn_w2"], i["L0_ffn_sw2"][None]]).reshape(3, F0, P, D).transpose(2, 0, 1, 3)})
    w1 = pack(W1, NW1, {
        "w1": np.concatenate([i["L1_ffn_ew1"], i["L1_ffn_fc1"][None]]).transpose(2, 0, 1),
        "w3": np.concatenate([i["L1_ffn_ew3"], i["L1_ffn_fc2"][None]]).transpose(2, 0, 1),
        "w2": np.concatenate([i["L1_ffn_ew2"], i["L1_ffn_fc3"][None]]).transpose(2, 0, 1)})
    w2 = pack(W2, NW2, {
        "w1": i["L2_ffn_w1"].transpose(2, 0, 1), "w3": i["L2_ffn_w3"].transpose(2, 0, 1),
        "w2": i["L2_ffn_w2"].transpose(2, 0, 1).reshape(I2, P, E2, D).transpose(1, 2, 0, 3)})
    w3 = np.stack([pack(W3, NW3, {
        "w1": i["L3_ffn_w1"][l].transpose(1, 0, 2),
        "w2": i["L3_ffn_w2"][l].reshape(E3, F0, P, D).transpose(2, 0, 1, 3)}) for l in range(L3)])
    return {"x": i["x"].reshape(2 * HALF, D), "ctx": i["ctx_1024"].reshape(2 * HALF, D),
            "ctxT": i["ctx_1024"].reshape(2 * HALF, D).T, "small": small, "w0": w0, "w1": w1, "w2": w2, "w3": w3}


def kernel(**inputs):
    import concourse.bacc as bacc
    from concourse.bass_utils import run_bass_kernel_spmd

    arrays = {k: np.ascontiguousarray(v) for k, v in layout({k: np.asarray(v) for k, v in inputs.items()}).items()}
    nc = bacc.Bacc("TRN2", target_bir_lowering=False, num_devices=1)
    args = [nc.dram_tensor(f"{k}_dram", v.shape, F32, kind="ExternalInput").ap() for k, v in arrays.items()]
    out = nc.dram_tensor("out_dram", (2 * HALF, D), F32, kind="ExternalOutput").ap()
    build(nc, *args, out)
    r = run_bass_kernel_spmd(nc, [{f"{k}_dram": v for k, v in arrays.items()}], core_ids=[0])
    return r.results[0]["out_dram"].reshape(4, S, D)
```

```python
from contextlib import ExitStack

import numpy as np

import concourse.bass as bass
from concourse import mybir

F32 = mybir.dt.float32
BF16 = mybir.dt.bfloat16
ALU = mybir.AluOpType
ACT = mybir.ActivationFunctionType
AX = mybir.AxisListType.X

P = 128
D = 128
S = 256
T = 4
HALF = T * P
NB = HALF // S
H = 16
HD = D // H
MH = 4
MD = D // MH
NEG = -1e30
F0 = 512 // P
E1, E2, E3, L3 = 6, 8, 4, 4
I2 = 256 // P
PARTS_A = (0, 0, 1, 0, 2, 1)
PARTS_B = (0, 1, 0, 2, 0, 1)
NSTACK = HD * len(PARTS_A)

SEGMENTS = [("att0", 0), ("att0", 1), ("ffn0", 0), ("ffn0", 1), ("att1", 0), ("ffn1", 0), ("att1", 1),
            ("ffn1", 1), ("att2", 0), ("att2", 1), ("ffn2", 0), ("ffn2", 1), ("att3", 0), ("att3", 1)]
SEGMENTS += [(f"moe{l}", hf) for l in range(L3) for hf in range(2)]


def steps_of(segments):
    out = [("head",) + segments[0]]
    for k, seg in enumerate(segments):
        before = segments[k - 1] if k else None
        after = segments[k + 1] if k + 1 < len(segments) else None
        if seg == ("att1", 0):
            out += [("body1",) + seg, ("body2",) + seg, ("tail", "ffn0", 1), ("tail",) + seg]
            if after:
                out += [("head",) + after]
            continue
        if seg == ("ffn1", 0):
            out += [("scores1", "att1", 1), ("body1",) + seg, ("scores2", "att1", 1), ("body2",) + seg]
            continue
        if seg == ("att1", 1):
            out += [("body1",) + seg, ("body2",) + seg, ("tail", "ffn1", 0), ("tail",) + seg]
            if after:
                out += [("head",) + after]
            continue
        early = before and before[0][:3] == "moe"
        if early:
            out += [("tail",) + before]
        out += [("body1",) + seg]
        if before and before[0] != "att1" and not early:
            out += [("tail",) + before]
        if after == ("att1", 0):
            out += [("scores1",) + after, ("scores2",) + after]
        elif after:
            out += [("head",) + after]
        out += [("body2",) + seg]
    if segments[-1][0] != "moe3" and segments[-1][0] != "att1":
        out += [("tail",) + segments[-1]]
    return out


ROWS = {"sel": (0, MH), "b2": (32, E3), "er": (64, HD)}


def _columns(parts):
    at, n = {}, 0
    for name, w in parts:
        at[name] = (n, w)
        n += w
    return at, n


SMALL, NSMALL = _columns([
    ("wq", D), ("wk", D), ("wv", D), ("bq", 1), ("bk", 1), ("gates", 8), ("bv", D),
    ("ident", P), ("addmask", 2 * P), ("ones", P),
    ("rows", MH * P),
    ("low", 64), ("g0w", 2), ("g1w", E1), ("g1b", E1), ("g2w", E2), ("g3w", L3 * E3), ("g3b", L3 * E3),
    ("s0b1", 3 * F0), ("b2s", D), ("rms", MD), ("mgw", 3 * 64), ("mgb", 1),
    ("lng", L3 * E3), ("lnb", L3 * E3), ("b1", L3 * E3 * F0),
    ("rwq", D), ("rwqs", D), ("rwk", D), ("rwks", D), ("rwv", D), ("rgw", D), ("rgb", D), ("row", D), ("rob", D),
    ("keep", P), 
    ("qcos", S), ("qsin", S), ("kcos", S), ("ksin", S)])
W0, NW0 = _columns([("w1", 3 * F0 * P), ("w2", 3 * F0 * D)])
W1, NW1 = _columns([("w1", 7 * P), ("w3", 7 * P), ("w2", 7 * D)])
W2, NW2 = _columns([("w1", E2 * I2 * P), ("w3", E2 * I2 * P), ("w2", E2 * I2 * D)])
W3, NW3 = _columns([("w1", E3 * F0 * P), ("w2", E3 * F0 * D)])


class Tally:

    def __init__(self):
        self.n = {}

    def __call__(self, sem, by=1):
        self.n[sem.name] = self.n.get(sem.name, 0) + by
        return self.n[sem.name]


class Turn:

    def __init__(self, bank, n, banks):
        self.bank, self.filled, self.drained, self.free = bank, n, n, max(n - banks, 0)


def plan(steps):
    rings = {"a": [0, 1], "d": [2, 3], "s": [4, 5], "o": [6, 7]}
    count = {r: 0 for r in rings}
    turns = {}

    def use(ring, *label):
        banks = rings[ring]
        turns[(name, hf, ring) + label] = Turn(banks[count[ring] % len(banks)], count[ring] + 1, len(banks))
        count[ring] += 1

    for part, name, hf in steps:
        kind = (name[:3] if name[:3] == "moe" else name, part)
        if kind == ("att0", "head"):
            use("d", "k"), use("d", "v"), use("a", "xt"), use("d", "q")
        if kind == ("att0", "body1"):
            for c in range(16):
                use("d", "rel", c)
                if c % 2:
                    use("a", "rel", c // 2)
        if kind == ("att0", "body2"):
            for n in range(NB * H):
                use("s", "scores", n)
                use("d", "probs", n)
                if n % 8 == 0:
                    use("a", "outT", n // 8)
                    use("o", "out", n // 8)
        if kind == ("ffn0", "head"):
            use("a", "xt"), use("d", "logits")
        if kind == ("ffn0", "body1"):
            use("o", "out")
            for c in range(F0):
                use("a", "h", FFN0_ORDER[0], c)
            use("a", "masked", 0), use("a", "masked", 1)
            for c in range(F0):
                use("a", "h", FFN0_ORDER[1], c)
        if kind == ("ffn0", "body2"):
            for c in range(F0):
                use("a", "h", FFN0_ORDER[2], c)
        if kind == ("att1", "body1"):
            use("o", "out")
        if name in ("ffn1", "ffn2"):
            if part == "head":
                use("a", "xt"), use("d", "logits")
            for e in body_experts(name, part):
                for c in range(CHUNKS[name]):
                    use("a", "gate", e, c), use("d", "up", e, c)
                use("o", "y", e)
        if kind == ("att2", "head"):
            use("a", "xt"), use("d", "gates")
        if kind == ("att2", "body1"):
            use("d", "cols")
            for b in range(NB):
                use("o", "out", b)
        if name == "att2" and part[:4] == "body":
            for h in body_heads(part):
                use("d", "rows", h)
                for b in range(NB):
                    use("d", "scores", h, b)
        if kind == ("att3", "head"):
            use("d", "k"), use("d", "ks"), use("a", "v"), use("a", "xt"), use("d", "q"), use("d", "qs"), use("d", "gate")
        if name == "att3" and part[:4] == "body":
            b = int(part == "body2")
            for p in range(H // 2):
                if p % 4 == 0:
                    use("s", "outT", b, p // 4)
                    use("o", "out", b, p // 4)
                if p % 2 == 0:
                    use("a", "off", b, p // 2)
                use("d", "diag", b, p)
        if kind == ("att3", "tail"):
            use("a", "yt"), use("d", "proj")
        if kind == ("moe", "head"):
            use("a", "xt"), use("a", "xh"), use("d", "logits")
        if kind == ("moe", "body1"):
            use("d", "combT"), use("d", "bias")
        if name[:3] == "moe":
            for e in body_experts(name, part):
                for c in range(F0):
                    use("a", "h", e, c)
                use("o", "y", e)
    return turns


def body_experts(name, part):
    n = EXPERTS.get(name, E3)
    return {"body1": range(0, (n + 1) // 2), "body2": range((n + 1) // 2, n)}.get(part, range(0))


FFN0_ORDER = (2, 0, 1)
EXPERTS = {"ffn1": E1 + 1, "ffn2": E2}
CHUNKS = {"ffn1": 1, "ffn2": I2}
FFN1_ORDER = (6, 0, 1, 2, 3, 4, 5)


def body_heads(part):
    return range(0, MH // 2) if part == "body1" else range(MH // 2, MH)


def build(nc, x_in, ctx_in, ctxT_in, small_in, w0_in, w1_in, w2_in, w3_in, out):
    with ExitStack() as stack:
        def sb(name, shape, dt=F32):
            return stack.enter_context(nc.sbuf_tensor(name, shape, dt))

        def sem(name):
            return stack.enter_context(nc.semaphore(name))

        X = sb("X", [P, 2, T, D])
        XN = sb("XN", [P, 2, T, D])
        XT = sb("XT", [P, 2, HALF])
        CT = sb("CT", [P, 2, HALF])
        CX = sb("CX", [P, 2, T, D])
        V9 = sb("V9", [P, 2, T, H, HD + 1])
        V33 = sb("V33", [P, 2, T, MH, MD + 1])
        V3 = [V9[:, hf, :, :, :].rearrange("p t h e -> p (t h e)")[:, 0:T * D].rearrange("p (t d) -> p t d", t=T)
              for hf in range(2)]
        XH = V33[:, :, :, :, :].rearrange("p a t h e -> p (a t h e)")[:, 0:2 * T * D]\
            .rearrange("p (a t d) -> p a t d", a=2, t=T)
        small = sb("small", [P, NSMALL])
        W = sb("W", [P, max(NW0 + NW1, NW2)])
        arena = sb("arena", [P, 3 * 32 * P])
        hidden = sb("hidden", [P, 2, F0, HALF])
        q6_all = sb("q6", [64 + NSTACK, H, HALF], BF16)
        k6_all = sb("k6", [64 + NSTACK, H, HALF], BF16)
        er6_all = sb("er6", [64 + NSTACK, 384], BF16)
        q6, k6, er6 = ([t_[64 * hf:64 * hf + NSTACK] for hf in range(2)] for t_ in (q6_all, k6_all, er6_all))
        erp = sb("erp", [64 + HD, 3, 384], BF16)[64:64 + HD]
        erf = sb("erf", [64 + HD, 384])[64:64 + HD]
        zeros = sb("zeros", [1, 512], BF16)
        gated = sb("gated", [P, 2, HALF])
        turned = sb("turned", [P, 2, HALF])
        scratch = sb("scratch", [P, 24 * 256])
        TG = sb("TG", [P, 8])
        st6 = sb("st6", [P, T, 6])
        mv = sb("mv", [P, T, 2])
        VE = sb("VE", [P, 64])
        RS = sb("RS", [P, 64])
        mhalf = sb("mhalf", [P, 64])
        negmax = sb("negmax", [P, 4, 2])
        sums = sb("sums", [P, 64])
        rms1 = sb("rms1", [P, MD])
        rt = sb("rt", [P, 2 * T * 64])
        lg = sb("lg", [P, T * 8])
        pr = sb("pr", [P, T * 8])
        combs = [sb(f"comb{hf}", [P, T * 8]) for hf in range(2)]
        rs4 = sb("rs4", [P, T * 2])
        csum = [sb(f"csum{hf}", [P, T]) for hf in range(2)]
        combT = rt[32:32 + E3, 0:HALF]
        ps = [stack.enter_context(nc.psum_tensor(f"bank{i}", [P, 512], F32)) for i in range(8)]

        def sm(name, rows=P):
            a, w = SMALL[name]
            return small[0:rows, a:a + w]

        def scr(at, *shape):
            return cut(scratch, at, *shape)

        def cut(memory, at, *shape):
            n = int(np.prod(shape))
            v = memory[:, at:at + n]
            if len(shape) == 1:
                return v
            names = "abcd"[:len(shape)]
            return v.rearrange(f"p ({' '.join(names)}) -> p {' '.join(names)}",
                               **{c: s for c, s in zip(names[1:], shape[1:])})

        def few(name, cols):
            at, n = ROWS[name]
            return small[at:at + n, SMALL["rows"][0]:SMALL["rows"][0] + cols]

        ident = sm("ident")
        addmask = sm("addmask")
        w0, w1, w2 = W[:, 0:NW0], W[:, NW0:NW0 + NW1], W[:, 0:NW2]
        relD = arena[:, 0:2 * 32 * P].rearrange("p (c i) -> p c i", i=P)
        relO = arena[:, 2 * 32 * P:3 * 32 * P].rearrange("p (c i) -> p c i", i=P)
        w3 = [arena[:, s * NW3:(s + 1) * NW3] for s in range(2)]

        def spare(at, *shape):
            return cut(arena, 2 * NW3 + at, *shape)

        flat = hidden[:, :, :, :].rearrange("p a b c -> p (a b c)")
        probs = [flat[:, 3 * P * s:3 * P * (s + 1)] for s in range(3)]
        probsT = [flat[:, 1152 + 3 * P * s:1152 + 3 * P * (s + 1)] for s in range(3)]
        outT = [flat[:, 2304 + 512 * s:2816 + 512 * s] for s in range(2)]

        fval = scr(0, HALF)
        ftmp = scr(512, HALF)
        parts = [scratch[:, 1024 + 768 * s:1024 + 768 * (s + 1)].bitcast(BF16).rearrange("p (c t) -> p c t", c=3)
                 for s in range(2)]
        pad = scr(2560, T, D)
        msk = [[scr(1024 * hf + 512 * s, T, D) for s in range(2)] for hf in range(2)]
        sc1_of = [spare(1024 * hf, T, H, H) for hf in range(2)]
        prod1 = [spare(2048 + 512 * s, T, D) for s in range(3)]
        acc = spare(3584, T, D)
        grow = scratch[0:64, 0:512]
        row = [scratch[0:MH, 512 * (1 + s):512 * (2 + s)] for s in range(4)]
        negrun = [scratch[0:MH, 2560 + 512 * hf:3072 + 512 * hf] for hf in range(2)]
        decay = [scr(3584 + 768 * s, NB, 3 * P) for s in range(2)]
        cmat = [scr(5120 + 384 * s, 3 * P) for s in range(2)]
        mout = scr(3584, T, MH, MD)
        msq = scr(4096, T, MH, MD)
        a_tok = [sb(f"a_tok{hf}", [P, T, MH]) for hf in range(2)]
        em_tok = [sb(f"em_tok{hf}", [P, T, MH]) for hf in range(2)]
        diag = [scr(2560 + 512 * s, 2, 2, P) for s in range(2)]
        gates3 = [scr(3584 + 512 * hf, T, D) for hf in range(2)]
        rets = [scr(4608 + 512 * hf, T, H, HD) for hf in range(2)]
        retsq = scr(5632, T, H, HD)
        y3 = spare(3584, T, D)
        Z = [[scr(512 * (2 * s + hf), T, D) for hf in range(2)] for s in range(2)]
        xe_of = [[spare(512 * (2 * hf + s), HALF) for s in range(2)] for hf in range(2)]

        stage = {(k, hf): nc.dram_tensor(f"parts_{k}_{hf}", (P, 3 * HALF), BF16, kind="Internal").ap()
                 for k in ("k0", "q0", "k3", "q3") for hf in range(2)}

        small_loaded, ctx_loaded = sem("small_loaded"), sem("ctx_loaded")
        ctxT_loaded = [sem(f"ctxT_loaded{h}") for h in range(2)]
        rest_loaded = sem("rest_loaded")
        x_loaded = [sem(f"x_loaded{h}") for h in range(2)]
        w0_loaded, w1_loaded, w2_loaded = sem("w0_loaded"), sem("w1_loaded"), sem("w2_loaded")
        w3_loaded = [sem(f"w3_loaded{s}") for s in range(2)]
        consts_done = sem("consts_done")
        v33_done = sem("v33_done")
        tanh_done = sem("tanh_done")
        er_parts = sem("er_parts")
        er_stacked = [sem(f"er_stacked{h}") for h in range(2)]
        parts_ready = sem("parts_ready")
        parts_out = [sem(f"parts_out{s}") for s in range(2)]
        stacked_k = [sem(f"stacked_k{h}") for h in range(2)]
        stacked_q = [sem(f"stacked_q{h}") for h in range(2)]
        norm_done = [sem(f"norm_done{h}") for h in range(2)]
        var_ready = sem("var_ready")
        rstd_ready = sem("rstd_ready")
        act_filled, act_drained = sem("act_filled"), sem("act_drained")
        dve_filled, dve_drained = sem("dve_filled"), sem("dve_drained")
        score_filled, score_drained = sem("score_filled"), sem("score_drained")
        out_filled, out_drained = sem("out_filled"), sem("out_drained")
        negmax_ready = sem("negmax_ready")
        masked_ready = sem("masked_ready")
        logits_ready = sem("logits_ready")
        weights_ready = sem("weights_ready")
        shifted1, expd1 = sem("shifted1"), sem("expd1")
        av1_ready, av1_used = sem("av1_ready"), sem("av1_used")
        flog_ready = sem("flog_ready")
        emarg_ready, em_ready = sem("emarg_ready"), sem("em_ready")
        rows_ready = sem("rows_ready")
        dexp_in, dexp_ready = sem("dexp_in"), sem("dexp_ready")
        gate3_in, gate3_ready = sem("gate3_in"), sem("gate3_ready")
        y3_ready = sem("y3_ready")
        comb_ready = sem("comb_ready")
        xe_ready = sem("xe_ready")
        step = sem("dve_step")
        astep = sem("act_step")
        x_done = [sem(f"x_done{h}") for h in range(2)]
        out_stored = sem("out_stored")

        NORM = {"att0": 1, "ffn0": 2, "att1": 3, "ffn1": 4, "att2": 5, "ffn2": 6, "att3": 7,
                "moe0": 8, "moe1": 9, "moe2": 10, "moe3": 11}
        GATE = {"att0": 0, "att1": 1, "att2": 2, "att3": 3, "ffn0": 4, "ffn1": 5, "ffn2": 6, "moe3": 7}
        steps = steps_of(SEGMENTS)
        turns = plan(steps)
        BANK = [p_[:, :] for p_ in ps]

        block = stack.enter_context(nc.Block())

        @block.sync
        def _(sp):
            seen = Tally()
            cut = SMALL["rms"][0]
            sp.dma_start(small[:, 0:cut], small_in[:, 0:cut]).then_inc(small_loaded, 16)
            xv = x_in.rearrange("(h t p) d -> h p t d", h=2, p=P)
            cv = ctx_in.rearrange("(h t p) d -> h p t d", h=2, p=P)
            for hf in range(2):
                sp.dma_start(CT[:, hf, :], ctxT_in[:, hf * HALF:(hf + 1) * HALF]).then_inc(ctxT_loaded[hf], 16)
                sp.dma_start(X[:, hf, :, :], xv[hf]).then_inc(x_loaded[hf], 16)
            sp.wait_ge(er_parts, 1)
            for hf in range(2):
                for r, c in enumerate(PARTS_B):
                    sp.dma_start(er6[hf][HD * r:HD * (r + 1), :], erp[:, c, :]).then_inc(er_stacked[hf], 16)
            n_parts = 0

            def restack(kind, hf, dst, rows, loaded):
                nonlocal n_parts
                buf = n_parts % 2
                n_parts += 1
                sp.wait_ge(parts_ready, n_parts)
                sp.dma_start(stage[kind, hf], parts[buf].rearrange("p c t -> p (c t)")).then_inc(parts_out[buf], 16)
                sp.wait_ge(parts_out[buf], seen(parts_out[buf], 16))
                src = stage[kind, hf].rearrange("(h e) (c t) -> e c h t", e=HD, c=3)
                for r, c in enumerate(rows):
                    sp.dma_start(dst[HD * r:HD * (r + 1), :, :], src[:, c, :, :]).then_inc(loaded, 16)

            for hf in range(2):
                restack("k0", hf, k6[hf], PARTS_B, stacked_k[hf])
                restack("q0", hf, q6[hf], PARTS_A, stacked_q[hf])
                if hf == 0:
                    sp.dma_start(small[:, cut:], small_in[:, cut:]).then_inc(rest_loaded, 16)
                    sp.dma_start(w0, w0_in).then_inc(w0_loaded, 16)
                    for h2 in range(2):
                        sp.dma_start(CX[:, h2, :, :], cv[h2]).then_inc(ctx_loaded, 16)
                    sp.dma_start(w1, w1_in).then_inc(w1_loaded, 16)
            sp.wait_ge(norm_done[1], NORM["att0"] + 1)
            for l in range(2):
                sp.dma_start(w3[l], w3_in[l]).then_inc(w3_loaded[l], 16)
            for hf in range(2):
                sp.wait_ge(norm_done[hf], NORM["ffn1"] + 1)
            sp.dma_start(w2, w2_in).then_inc(w2_loaded, 16)
            for hf in range(2):
                restack("k3", hf, k6[hf], PARTS_B, stacked_k[hf])
                restack("q3", hf, q6[hf], PARTS_A, stacked_q[hf])
            for l in range(L3 - 2):
                for hf in range(2):
                    sp.wait_ge(norm_done[hf], NORM[f"moe{l}"] + 1)
                sp.dma_start(w3[l], w3_in[l + 2]).then_inc(w3_loaded[l], 16)
            ov = out.rearrange("(h t p) d -> h p t d", h=2, p=P)
            for hf in range(2):
                sp.wait_ge(x_done[hf], 1)
                sp.dma_start(ov[hf], X[:, hf, :, :]).then_inc(out_stored, 16)
            sp.wait_ge(out_stored, 32)

        @block.gpsimd
        def _(pool):
            seen = Tally()
            pool.memset(mhalf[:, :], -0.5)
            pool.memset(zeros[:, :], 0.0)
            for hf in range(2):
                pool.memset(V9[:, hf, :, :, HD:HD + 1], 1.0)
            pool.memset(V33[:, :, :, :, MD:MD + 1], 1.0).then_inc(consts_done, 1)
            pool.wait_ge(consts_done, 1)

            def rsqrt(n):
                pool.wait_ge(var_ready, seen(var_ready))
                pool.tensor_tensor(RS[:, 0:n], VE[:, 0:n], mhalf[:, 0:n], ALU.pow).then_inc(rstd_ready, 1)

            for hf in range(2):
                rsqrt(T)
            for part, name, hf in steps:
                if (part, name) == ("body2", "att2"):
                    rsqrt(T * MH)
                if (part, name) == ("tail", "att3"):
                    rsqrt(T * H)
                    rsqrt(T)
                if part == "tail" and name != "moe3":
                    rsqrt(T)
                if (part, name, hf) == ("head", "ffn0", 0):
                    pool.wait_ge(ctx_loaded, 32)
                    for h2 in range(2):
                        for h in range(MH):
                            last = pool.tensor_copy(V33[:, h2, :, h, 0:MD], CX[:, h2, :, MD * h:MD * (h + 1)])
                    last.then_inc(v33_done, 1)

        @block.scalar
        def _(act):
            seen = Tally()
            act.wait_ge(small_loaded, 16)
            act.activation(TG[:, :], sm("gates"), ACT.Tanh).then_inc(tanh_done, 1)

            def drain(turn, dst, func=ACT.Copy, **kw):
                act.wait_ge(act_filled, turn.filled)
                src = BANK[turn.bank]
                if len(dst.shape) == 3:
                    src = src.rearrange("p (a b) -> p a b", a=dst.shape[1])
                act.activation(dst, src, func, **kw).then_inc(act_drained, 1)

            def weights(name):
                n = T * {"ffn1": E1, "ffn2": E2}.get(name, E3)
                act.wait_ge(logits_ready, seen(logits_ready))
                act.activation(pr[:, 0:n], lg[:, 0:n], ACT.Sigmoid if name == "ffn1" else ACT.Exp)\
                   .then_inc(weights_ready, 1)

            before = None
            for part, name, hf in steps:
                at = {k[2:]: v for k, v in turns.items() if k[:2] == (name, hf)}
                if part == "head":
                    if name == "att3":
                        drain(at["a", "v"], V3[hf])
                    drain(at["a", "xt"], XT[:, hf, :])
                    if name[:3] == "moe":
                        drain(at["a", "xh"], turned[:, hf, :])

                if name == "att0" and part == "body1":
                    for c in range(8):
                        turn = at["a", "rel", c]
                        act.wait_ge(act_filled, turn.filled)
                        act.activation(relO[:, :, 16 * c:16 * (c + 1)],
                                       BANK[turn.bank].rearrange("p (u c) -> p c u", c=NB * H), ACT.Copy)\
                           .then_inc(act_drained, 1)
                if name == "att0" and part == "body2":
                    for i in range(NB * H + 4):
                        if i < NB * H:
                            turn = at["s", "scores", i]
                            act.wait_ge(negmax_ready, seen(negmax_ready))
                            pr_ = probs[i % 3]
                            act.activation(pr_[:, 0:P], BANK[turn.bank][:, 0:P], ACT.Exp, bias=negmax[:, i % 4, 0:1])
                            act.activation(pr_[:, P:3 * P], BANK[turn.bank][:, P:3 * P], ACT.Exp,
                                           bias=negmax[:, i % 4, 1:2]).then_inc(score_drained, 1)
                        if i >= 11 and (i - 11) % 8 == 0:
                            g = (i - 11) // 8
                            drain(at["a", "outT", g], outT[g % 2])

                if name == "ffn0" and part[:4] == "body":
                    for k in ((0, 1) if part == "body1" else (2,)):
                        e = FFN0_ORDER[k]
                        for c in range(F0):
                            if hf == 0 and k == 0 and c == 0:
                                act.wait_ge(rest_loaded, 16)
                            drain(at["a", "h", e, c], hidden[:, k % 2, c, :], ACT.Relu,
                                  bias=sm("s0b1")[:, e * F0 + c:e * F0 + c + 1])
                        if k == 0:
                            for m in range(2):
                                drain(at["a", "masked", m], turned[:, m, :])

                if part == "scores2":
                    act.wait_ge(shifted1, seen(shifted1))
                    act.activation(sc1_of[hf], sc1_of[hf], ACT.Exp, scale=HD ** -0.5).then_inc(expd1, 1)

                if name in ("ffn1", "ffn2"):
                    if part == "head":
                        weights(name)
                    chunks = [(e, c) for e in range(EXPERTS[name]) for c in range(CHUNKS[name])]
                    for k, (e, c) in enumerate(chunks):
                        if e not in body_experts(name, part):
                            continue
                        if k >= 2:
                            act.wait_ge(dve_drained, at[("d", "up") + chunks[k - 2]].drained)
                        drain(at["a", "gate", e, c], gated[:, k % 2, :], ACT.Silu)

                if name == "att2" and part == "head":
                    act.wait_ge(dve_drained, at["d", "gates"].drained)
                    act.activation(row[1], grow[32:32 + MH, :], ACT.Abs).then_inc(astep, 1)
                    act.wait_ge(astep, seen(astep))
                    act.activation(row[1], row[1], ACT.Exp, scale=-1.0).then_inc(astep, 1)
                    act.wait_ge(astep, seen(astep))
                    act.activation(row[1], row[1], ACT.Ln, bias=sm("ones", MH)[:, 0:1]).then_inc(flog_ready, 1)
                    act.wait_ge(emarg_ready, seen(emarg_ready))
                    act.activation(row[0], row[0], ACT.Exp, scale=-1.0).then_inc(em_ready, 1)
                if name == "att2" and part[:4] == "body":
                    for h in body_heads(part):
                        act.wait_ge(dexp_in, seen(dexp_in))
                        act.activation(decay[h % 2], decay[h % 2], ACT.Exp).then_inc(dexp_ready, 1)

                if name == "att3" and part == "head":
                    act.wait_ge(gate3_in, seen(gate3_in))
                    act.activation(gates3[hf], gates3[hf], ACT.Silu).then_inc(gate3_ready, 1)
                if name == "att3" and part[:4] == "body":
                    b = int(part == "body2")
                    for g in range(H // 4):
                        drain(at["a", "off", b, g], gated[:, g % 2, :])
                        if g >= 2:
                            turn = at["s", "outT", b, g - 2]
                            act.wait_ge(score_filled, turn.filled)
                            act.activation(outT[g - 2], BANK[turn.bank], ACT.Copy).then_inc(score_drained, 1)
                if name == "att3" and part == "tail":
                    drain(at["a", "yt"], turned[:, hf, :])

                if name[:3] == "moe":
                    l = int(name[3])
                    if part == "head" and (before is None or l == 0 and hf == 0):
                        weights(name)
                    for e in body_experts(name, part):
                        for c in range(F0):
                            k = (l * E3 + e) * F0 + c
                            drain(at["a", "h", e, c], hidden[:, e % 2, c, :], ACT.Gelu, bias=sm("b1")[:, k:k + 1])
                            if part == "body2" and e == 2 and c == 1 and before[0] == "head":
                                weights(before[1])
                before = (part, name, hf)

        @block.tensor
        def _(pe):
            seen = Tally()

            def mm(dst, lhsT, rhs, start, stop=False, turn=False):
                return pe.matmul(dst, lhsT, rhs, start=start, stop=stop, is_transpose=turn or None,
                                 skip_group_check=True)

            def bank(turn, drained):
                if turn.free:
                    pe.wait_ge(drained, turn.free)
                return BANK[turn.bank]

            def turn_tiles(turn, src):
                b_ = bank(turn, act_drained)
                for t in range(T):
                    last = mm(b_[:, t * P:(t + 1) * P], src[:, t, :], ident, start=(t == 0), stop=True, turn=True)
                last.then_inc(act_filled, 1)

            def tokens(turn, lhsT, rhs, n, ring=(dve_drained, dve_filled)):
                b_ = bank(turn, ring[0])
                for t in range(T):
                    last = mm(b_[:, t * n:(t + 1) * n], lhsT[:, t * P:(t + 1) * P], rhs, start=True, stop=True)
                last.then_inc(ring[1], 1)

            def feats(turn, w, rhs, drained, filled):
                mm(bank(turn, drained), w, rhs, start=True, stop=True).then_inc(filled, 1)

            def inputs(name, hf, at):
                pe.wait_ge(norm_done[hf], NORM[name])
                turn_tiles(at["a", "xt"], XN[:, hf, :, :])

            def second(turn, n, w2_, slot, ready, count, first=True, close=True):
                b_ = BANK[turn.bank] if not first else bank(turn, out_drained)
                pe.wait_ge(ready, count)
                for t in range(T):
                    for c in range(n):
                        last = mm(b_[:, t * P:(t + 1) * P], hidden[:, slot, c, t * P:(t + 1) * P], w2_(c),
                                  start=(first and t == 0 and c == 0), stop=(c == n - 1))
                if close:
                    last.then_inc(out_filled, 1)

            def ffn_weights(name):
                cols, w_ = (W1, w1) if name == "ffn1" else (W2, w2)
                return [w_[:, cols[k][0]:cols[k][0] + cols[k][1]]
                        .rearrange("p (e c f) -> p e c f", e=EXPERTS[name], c=CHUNKS[name]) for k in ("w1", "w3", "w2")]

            def blocks_turned(turn, src, ring):
                b_ = bank(turn, out_drained)
                pe.wait_ge(*ring)
                for k in range(4):
                    last = mm(b_[:, k * P:(k + 1) * P], src[:, k * P:(k + 1) * P], ident, start=(k == 0), stop=True, turn=True)
                last.then_inc(out_filled, 1)

            def clear(turn, drained):
                mm(bank(turn, drained), zeros[:, 0:P], zeros[:, :], start=True)

            pe.wait_ge(small_loaded, 16)
            for part, name, hf in steps:
                at = {k[2:]: v for k, v in turns.items() if k[:2] == (name, hf)}

                if name == "att0" and part == "head":
                    pe.wait_ge(ctxT_loaded[hf], 16)
                    feats(at["d", "k"], sm("wk"), CT[:, hf, :], dve_drained, dve_filled)
                    tokens(at["d", "v"], CT[:, hf, :], sm("wv"), D)
                    inputs(name, hf, at)
                    pe.wait_ge(act_drained, at["a", "xt"].drained)
                    feats(at["d", "q"], sm("wq"), XT[:, hf, :], dve_drained, dve_filled)
                if name == "att0" and part == "body1":
                    pe.wait_ge(er_stacked[hf], 16 * len(PARTS_B))
                    pe.wait_ge(stacked_q[hf], 16 * len(PARTS_A))
                    qv = q6[hf].rearrange("k h (c i) -> k c h i", i=P)
                    for c in range(16):
                        b_ = bank(at["d", "rel", c], dve_drained)
                        for u in range(8):
                            i = 8 * c + u
                            last = mm(b_[:, u * 64:(u + 1) * 64], er6[hf][:, S - 1 - i:S - 1 - i + P], qv[:, :, :, i],
                                      start=True, stop=True)
                        last.then_inc(dve_filled, 1)
                        if c % 2:
                            b_ = bank(at["a", "rel", c // 2], act_drained)
                            for u in range(16):
                                i = 16 * (c // 2) + u
                                last = mm(b_[:, u * 32:(u + 1) * 32], er6[hf][:, P - 1 - i:2 * P - 1 - i],
                                          qv[:, 1::2, :, i], start=True, stop=True)
                            last.then_inc(act_filled, 1)
                if name == "att0" and part == "body2":
                    pe.wait_ge(stacked_k[hf], 16 * len(PARTS_B))
                    pe.wait_ge(dve_drained, at["d", "rel", 15].drained)
                    pe.wait_ge(act_drained, at["a", "rel", 7].drained)
                    for i in range(NB * H + 6):
                        if i < NB * H:
                            b, h = divmod(i, H)
                            s_ = bank(at["s", "scores", i], score_drained)
                            q0 = b * S
                            mm(s_[:, 0:P], relD[:, 2 * b * H + h, :], ident, start=True, turn=True)
                            mm(s_[:, P:2 * P], relO[:, b * H + h, :], ident, start=False, turn=True)
                            mm(s_[:, 2 * P:3 * P], relD[:, (2 * b + 1) * H + h, :], ident, start=False, turn=True)
                            mm(s_[:, 0:P], q6[hf][:, h, q0:q0 + P], k6[hf][:, h, q0:q0 + P], start=False)
                            mm(s_[:, P:3 * P], q6[hf][:, h, q0 + P:q0 + S], k6[hf][:, h, q0:q0 + S], start=False,
                               stop=True).then_inc(score_filled, 1)
                        if 2 <= i < NB * H + 2:
                            n = i - 2
                            pt = bank(at["d", "probs", n], dve_drained)
                            pe.wait_ge(score_drained, at["s", "scores", n].drained)
                            for k in range(3):
                                last = mm(pt[:, k * P:(k + 1) * P], probs[n % 3][:, k * P:(k + 1) * P], ident,
                                          start=(k == 0), stop=True, turn=True)
                            last.then_inc(dve_filled, 1)
                        if 3 <= i < NB * H + 3:
                            n = i - 3
                            b, h = divmod(n, H)
                            turn = at["a", "outT", n // 8]
                            if n == 0:
                                pe.wait_ge(dve_drained, at["d", "v"].drained)
                                pe.wait_ge(consts_done, 1)
                            if n % 8 == 0:
                                clear(turn, act_drained)
                            pe.wait_ge(dve_drained, at["d", "probs", n].drained)
                            pt = probsT[n % 3]
                            o_, c0 = BANK[turn.bank][32 * (h % 4):32 * (h % 4) + HD + 1, :], S * (h // 4 % 2)
                            v0, v1 = V9[:, hf, 2 * b, h, :], V9[:, hf, 2 * b + 1, h, :]
                            mm(o_[:, c0:c0 + S], v0, pt[:, 0:S], start=False)
                            last = mm(o_[:, c0 + P:c0 + S], v1, pt[:, S:S + P], start=False, stop=True)
                            if n % 8 == 7:
                                last.then_inc(act_filled, 1)
                        if i >= 13 and (i - 13) % 8 == 0:
                            g = (i - 13) // 8
                            blocks_turned(at["o", "out", g], outT[g % 2], (act_drained, at["a", "outT", g].drained))

                if name == "ffn0":
                    w1_ = w0[:, W0["w1"][0]:].rearrange("p (e c f) -> p e c f", e=6, c=F0)
                    w2_ = w0[:, W0["w2"][0]:].rearrange("p (e c d) -> p e c d", e=3, c=F0)

                    def first(e, rhs):
                        for c in range(F0):
                            feats(at["a", "h", e, c], w1_[:, e, c, :], rhs, act_drained, act_filled)

                    def then(k):
                        e = FFN0_ORDER[k]
                        second(at["o", "out"], F0, lambda c: w2_[:, e, c, :], k % 2, act_drained,
                               at["a", "h", e, F0 - 1].drained, first=False, close=(k == 2))

                    if part == "head":
                        inputs(name, hf, at)
                        if hf == 0:
                            pe.wait_ge(rest_loaded, 16)
                        pe.wait_ge(act_drained, at["a", "xt"].drained)
                        tokens(at["d", "logits"], XT[:, hf, :], sm("g0w"), 2)
                    if part == "body1":
                        o_ = bank(at["o", "out"], out_drained)
                        for t in range(T):
                            mm(o_[:, t * P:(t + 1) * P], sm("ones", 3), sm("b2s", 3), start=(t == 0))
                        if hf == 0:
                            pe.wait_ge(w0_loaded, 16)
                        first(2, XT[:, hf, :])
                        for m in range(2):
                            pe.wait_ge(masked_ready, seen(masked_ready))
                            turn_tiles(at["a", "masked", m], msk[hf][m])
                        pe.wait_ge(act_drained, at["a", "masked", 0].drained)
                        first(0, turned[:, 0, :])
                        then(0)
                    if part == "body2":
                        pe.wait_ge(act_drained, at["a", "masked", 1].drained)
                        first(1, turned[:, 1, :])
                        then(1)
                        then(2)

                if name == "att1" and part == "body1":
                    o_ = bank(at["o", "out"], out_drained).rearrange("p (t d) -> p t d", t=T)
                    for dl in range(H):
                        pe.wait_ge(av1_ready, seen(av1_ready))
                        w = D - HD * dl
                        last = mm(o_[:, :, HD * dl:D], ident, prod1[dl % 3][:, :, 0:w], start=(dl == 0), stop=(dl == H - 1))
                        last.then_inc(av1_used if dl < H - 1 else out_filled, 1)

                if name in ("ffn1", "ffn2"):
                    E, C = EXPERTS[name], CHUNKS[name]
                    wg, wu, wd = ffn_weights(name)

                    def down(e):
                        g = e if name == "ffn2" else FFN1_ORDER[e]
                        second(at["o", "y", e], C, lambda c: wd[:, g, c, :], e % 2, dve_drained,
                               at["d", "up", e, C - 1].drained)

                    if part == "head":
                        inputs(name, hf, at)
                        pe.wait_ge(act_drained, at["a", "xt"].drained)
                        if name == "ffn1":
                            tokens(at["d", "logits"], XT[:, hf, :], sm("g1w"), E1)
                        else:
                            tokens(at["d", "logits"], XT[:, hf, :], sm("g2w"), E2)
                    if part == "body1" and hf == 0:
                        pe.wait_ge(w1_loaded if name == "ffn1" else w2_loaded, 16)
                    for e in body_experts(name, part):
                        g = e if name == "ffn2" else FFN1_ORDER[e]
                        for c in range(C):
                            feats(at["a", "gate", e, c], wg[:, g, c, :], XT[:, hf, :], act_drained, act_filled)
                            feats(at["d", "up", e, c], wu[:, g, c, :], XT[:, hf, :], dve_drained, dve_filled)
                        if e:
                            down(e - 1)
                    if part == "body2":
                        down(E - 1)

                if name == "att2" and part == "head":
                    inputs(name, hf, at)
                    pe.wait_ge(act_drained, at["a", "xt"].drained)
                    gw = sm("mgw").rearrange("p (k m) -> p k m", k=3)
                    b_ = bank(at["d", "gates"], dve_drained)
                    mm(b_[0:64, :], gw[:, 0, :], XT[:, hf, :], start=True)
                    mm(b_[0:64, :], gw[:, 1, :], CT[:, hf, :], start=False)
                    mm(b_[0:64, :], gw[:, 2, :], CT[:, hf, :], start=False, stop=True).then_inc(dve_filled, 1)
                if name == "att2" and part[:4] == "body":
                    if part == "body1":
                        b_ = bank(at["d", "cols"], dve_drained)
                        pe.wait_ge(rows_ready, seen(rows_ready))
                        pe.wait_ge(em_ready, seen(em_ready))
                        for k, src in enumerate((row[2], row[0])):
                            for t in range(T):
                                last = mm(b_[:, (k * T + t) * MH:(k * T + t + 1) * MH], src[:, t * P:(t + 1) * P],
                                          ident[0:MH, 0:MH], start=True, stop=True)
                        last.then_inc(dve_filled, 1)
                        for b in range(NB):
                            bank(at["o", "out", b], out_drained)
                        if hf == 0:
                            pe.wait_ge(v33_done, 1)
                    outs = [BANK[at["o", "out", b].bank][:, 0:2 * MH * (MD + 1)]
                            .rearrange("p (a h e) -> p a h e", a=2, h=MH) for b in range(NB)]
                    sel = few("sel", MH * P).rearrange("p (h m) -> p h m", h=MH)

                    def values(k):
                        h, b = divmod(k, NB)
                        pe.wait_ge(dve_drained, at["d", "scores", h, b].drained)
                        c_ = cmat[k % 2]
                        o_ = outs[b]
                        mm(o_[:, 0, h, :], c_[:, 0:P], V33[:, hf, 2 * b, h, :], start=(h == 0))
                        mm(o_[:, 1, h, :], c_[:, P:2 * P], V33[:, hf, 2 * b, h, :], start=False)
                        last = mm(o_[:, 1, h, :], c_[:, 2 * P:3 * P], V33[:, hf, 2 * b + 1, h, :], start=False, stop=True)
                        if h == MH - 1:
                            last.then_inc(out_filled, 1)

                    for h in body_heads(part):
                        mm(bank(at["d", "rows", h], dve_drained), sel[:, h, :], negrun[hf], start=True, stop=True)\
                            .then_inc(dve_filled, 1)
                        hs = slice(MD * h, MD * (h + 1))
                        for b in range(NB):
                            b_ = bank(at["d", "scores", h, b], dve_drained)
                            k0, k1, k2 = b * S, b * S + P, (b + 1) * S
                            mm(b_[:, 0:S], CT[hs, hf, k0:k1], XT[hs, hf, k0:k2], start=True, stop=True)
                            mm(b_[:, S:S + P], CT[hs, hf, k1:k2], XT[hs, hf, k1:k2], start=True, stop=True)\
                                .then_inc(dve_filled, 1)
                            k = NB * h + b
                            if k:
                                values(k - 1)
                    if part == "body2":
                        values(NB * MH - 1)

                if name == "att3" and part == "head":
                    feats(at["d", "k"], sm("rwk"), CT[:, hf, :], dve_drained, dve_filled)
                    feats(at["d", "ks"], sm("rwks"), CT[:, hf, :], dve_drained, dve_filled)
                    tokens(at["a", "v"], CT[:, hf, :], sm("rwv"), D, (act_drained, act_filled))
                    inputs(name, hf, at)
                    pe.wait_ge(act_drained, at["a", "xt"].drained)
                    feats(at["d", "q"], sm("rwq"), XT[:, hf, :], dve_drained, dve_filled)
                    feats(at["d", "qs"], sm("rwqs"), XT[:, hf, :], dve_drained, dve_filled)
                    tokens(at["d", "gate"], XT[:, hf, :], sm("rgw"), D)
                if name == "att3" and part[:4] == "body":
                    if part == "body1":
                        pe.wait_ge(stacked_k[hf], 2 * 16 * len(PARTS_B))
                        pe.wait_ge(stacked_q[hf], 2 * 16 * len(PARTS_A))

                    def retained(b, p_):
                        turn = at["s", "outT", b, p_ // 4]
                        if p_ % 4 == 0:
                            clear(turn, score_drained)
                        pe.wait_ge(dve_drained, at["d", "diag", b, p_].drained)
                        pe.wait_ge(act_drained, at["a", "off", b, p_ // 2].drained)
                        for k in range(2):
                            h = 2 * p_ + k
                            off = gated[:, (p_ // 2) % 2, :].rearrange("p (h i) -> p h i", h=4)[:, h % 4, :]
                            d_ = diag[p_ % 2]
                            hs = slice(HD * h, HD * (h + 1))
                            o_, c0 = BANK[turn.bank][32 * (h % 4):32 * (h % 4) + HD, :], S * (h // 4 % 2)
                            mm(o_[:, c0:c0 + P], V3[hf][:, 2 * b, hs], d_[:, k, 0, :], start=False)
                            mm(o_[:, c0 + P:c0 + S], V3[hf][:, 2 * b, hs], off, start=False)
                            last = mm(o_[:, c0 + P:c0 + S], V3[hf][:, 2 * b + 1, hs], d_[:, k, 1, :], start=False, stop=True)
                        if p_ % 4 == 3:
                            last.then_inc(score_filled, 1)

                    def token_major(b, g):
                        turn = at["s", "outT", b, g]
                        blocks_turned(at["o", "out", b, g], outT[g], (score_drained, turn.drained))

                    b = int(part == "body2")
                    k0, k1, k2 = b * S, b * S + P, (b + 1) * S
                    for p_ in range(H // 2):
                        if p_ % 2 == 0:
                            b_ = bank(at["a", "off", b, p_ // 2], act_drained)
                            for k in range(4):
                                h = 2 * p_ + k
                                last = mm(b_[:, k * P:(k + 1) * P], k6[hf][:, h, k0:k1], q6[hf][:, h, k1:k2],
                                          start=True, stop=True)
                            last.then_inc(act_filled, 1)
                        b_ = bank(at["d", "diag", b, p_], dve_drained)
                        for k in range(2):
                            h = 2 * p_ + k
                            mm(b_[:, 2 * k * P:(2 * k + 1) * P], k6[hf][:, h, k0:k1], q6[hf][:, h, k0:k1],
                               start=True, stop=True)
                            last = mm(b_[:, (2 * k + 1) * P:(2 * k + 2) * P], k6[hf][:, h, k1:k2], q6[hf][:, h, k1:k2],
                                      start=True, stop=True)
                        last.then_inc(dve_filled, 1)
                        if p_:
                            retained(b, p_ - 1)
                        if p_ == 7:
                            token_major(b, 0)
                    retained(b, H // 2 - 1)
                    token_major(b, 1)
                if name == "att3" and part == "tail":
                    pe.wait_ge(y3_ready, seen(y3_ready))
                    turn_tiles(at["a", "yt"], y3)
                    pe.wait_ge(act_drained, at["a", "yt"].drained)
                    tokens(at["d", "proj"], turned[:, hf, :], sm("row"), D)

                if name[:3] == "moe":
                    l = int(name[3])
                    w_ = w3[l % 2]
                    wa = w_[:, 0:W3["w1"][1]].rearrange("p (e c f) -> p e c f", e=E3, c=F0)
                    wb = w_[:, W3["w2"][0]:].rearrange("p (e c d) -> p e c d", e=E3, c=F0)

                    def down(e):
                        second(at["o", "y", e], F0, lambda c: wb[:, e, c, :], e % 2, act_drained,
                               at["a", "h", e, F0 - 1].drained)

                    if part == "head":
                        pe.wait_ge(norm_done[hf], NORM[name])
                        turn_tiles(at["a", "xt"], XN[:, hf, :, :] if l == 0 else Z[l % 2][hf])
                        turn_tiles(at["a", "xh"], XH[:, hf, :, :])
                        pe.wait_ge(act_drained, at["a", "xt"].drained)
                        tokens(at["d", "logits"], XT[:, hf, :], sm("g3w")[:, l * E3:(l + 1) * E3], E3)
                    if part == "body1" and hf == 0:
                        pe.wait_ge(w3_loaded[l % 2], 16 * (l // 2 + 1))
                    for e in body_experts(name, part):
                        pe.wait_ge(xe_ready, seen(xe_ready))
                        for c in range(F0):
                            feats(at["a", "h", e, c], wa[:, e, c, :], xe_of[hf][e % 2], act_drained, act_filled)
                        if e == 0:
                            b_ = bank(at["d", "combT"], dve_drained)
                            pe.wait_ge(comb_ready, seen(comb_ready))
                            for t in range(T):
                                last = mm(b_[0:E3, t * P:(t + 1) * P], combs[hf][:, t * E3:(t + 1) * E3], ident,
                                          start=True, stop=True)
                            last.then_inc(dve_filled, 1)
                            pe.wait_ge(dve_drained, at["d", "combT"].drained)
                            tokens(at["d", "bias"], combT, few("b2", L3 * D)[:, l * D:(l + 1) * D], D)
                        else:
                            down(e - 1)
                    if part == "body2":
                        down(E3 - 1)

        @block.vector
        def _(dve):
            seen = Tally()

            def settle(last):
                last.then_inc(step, 1)
                dve.wait_ge(step, seen(step))

            def rsqrt(last):
                last.then_inc(var_ready, 1)
                dve.wait_ge(rstd_ready, seen(rstd_ready))

            def layernorm(src, dst):
                for t in range(T):
                    last = dve.bn_stats(st6[:, t, :], src[:, t, :])
                settle(last)
                for t in range(T):
                    last = dve.bn_aggr(mv[:, t, :], st6[:, t, :])
                settle(last)
                rsqrt(dve.tensor_scalar(VE[:, 0:T], mv[:, :, 1], 1e-5, None, ALU.add))
                for t in range(T):
                    last = dve.tensor_scalar(dst[:, t, :], src[:, t, :], mv[:, t, 0:1], RS[:, t:t + 1],
                                             ALU.subtract, ALU.mult)
                return last

            n_parts = 0

            def split(src, out_sem):
                nonlocal n_parts
                buf = n_parts % 2
                if n_parts >= 2:
                    dve.wait_ge(parts_out[buf], 16 * (n_parts // 2))
                n_parts += 1
                part = parts[buf]
                settle(dve.tensor_copy(part[:, 0, :], src))
                settle(dve.tensor_tensor(ftmp, src, part[:, 0, :], ALU.subtract))
                settle(dve.tensor_copy(part[:, 1, :], ftmp))
                dve.tensor_tensor(part[:, 2, :], ftmp, part[:, 1, :], ALU.subtract).then_inc(out_sem, 1)

            def bc(ap, shape, axis):
                return ap.unsqueeze(axis).broadcast_to(shape)

            def take(turn):
                dve.wait_ge(dve_filled, turn.filled)
                return BANK[turn.bank]

            def drained(last, turn):
                last.then_inc(dve_drained, 1)
                dve.wait_ge(dve_drained, turn.drained)

            def top2(comb, E, keys, vals, eps):
                K = keys.rearrange("p (t e) -> p t e", t=T)
                n = T * E * E
                gt = rt[:, 0:n].rearrange("p (t e f) -> p t e f", t=T, e=E)
                eq = rt[:, T * 64:T * 64 + n].rearrange("p (t e f) -> p t e f", t=T, e=E)
                mine = bc(K, [P, T, E, E], 3)
                other = bc(K, [P, T, E, E], 2)
                low = bc(sm("low").rearrange("p (e f) -> p e f", e=8)[:, 0:E, 0:E], [P, T, E, E], 1)
                dve.tensor_tensor(gt, other, mine, ALU.is_gt)
                settle(dve.tensor_tensor(eq, other, mine, ALU.is_equal))
                settle(dve.tensor_tensor(eq, eq, low, ALU.mult))
                settle(dve.tensor_tensor(gt, gt, eq, ALU.add))
                C = comb[:, 0:T * E].rearrange("p (t e) -> p t e", t=T)
                settle(dve.tensor_reduce(C, gt, AX, ALU.add))
                dve.wait_ge(weights_ready, seen(weights_ready))
                settle(dve.scalar_tensor_tensor(comb[:, 0:T * E], comb[:, 0:T * E], 1.5, vals, ALU.is_lt, ALU.mult))
                settle(dve.tensor_reduce(rs4[:, 0:T], C, AX, ALU.add))
                if eps:
                    settle(dve.tensor_scalar(rs4[:, 0:T], rs4[:, 0:T], eps, None, ALU.add))
                settle(dve.reciprocal(rs4[:, T:2 * T], rs4[:, 0:T]))
                return dve.tensor_tensor(C, C, bc(rs4[:, T:2 * T], [P, T, E], 2), ALU.mult)

            def softmax_keys(E):
                K = lg[:, 0:T * E].rearrange("p (t e) -> p t e", t=T)
                settle(dve.tensor_reduce(rs4[:, 0:T], K, AX, ALU.max))
                dve.tensor_tensor(K, K, bc(rs4[:, 0:T], [P, T, E], 2), ALU.subtract).then_inc(logits_ready, 1)
                dve.wait_ge(logits_ready, seen(logits_ready))

            def residual(name, hf, src, tiles=slice(0, T)):
                g = GATE[name]
                return dve.scalar_tensor_tensor(X[:, hf, tiles, :], src, TG[:, g:g + 1], X[:, hf, tiles, :],
                                                ALU.mult, ALU.add)

            dve.wait_ge(small_loaded, 16)
            er = few("er", 384)
            settle(dve.tensor_copy(erp[:, 0, :], er))
            settle(dve.tensor_tensor(erf[:, :], er, erp[:, 0, :], ALU.subtract))
            settle(dve.tensor_copy(erp[:, 1, :], erf[:, :]))
            dve.tensor_tensor(erp[:, 2, :], erf[:, :], erp[:, 1, :], ALU.subtract).then_inc(er_parts, 1)
            for hf in range(2):
                dve.wait_ge(x_loaded[hf], 16)
                layernorm(X[:, hf, :, :], XN[:, hf, :, :]).then_inc(norm_done[hf], 1)
            dve.wait_ge(tanh_done, 1)

            for part, name, hf in steps:
                at = {k[2:]: v for k, v in turns.items() if k[:2] == (name, hf)}

                if name == "att0" and part == "head":
                    turn = at["d", "k"]
                    drained(dve.tensor_scalar(fval, take(turn), sm("bk"), None, ALU.add), turn)
                    split(fval, parts_ready)
                    turn = at["d", "v"]
                    drained(dve.tensor_tensor(V9[:, hf, :, :, 0:HD],
                                              take(turn).rearrange("p (t h e) -> p t h e", t=T, h=H),
                                              bc(sm("bv").rearrange("p (h e) -> p h e", h=H), [P, T, H, HD], 1),
                                              ALU.add), turn)
                    turn = at["d", "q"]
                    drained(dve.tensor_scalar(fval, take(turn), sm("bq"), HD ** -0.5, ALU.add, ALU.mult), turn)
                    split(fval, parts_ready)
                if name == "att0" and part == "body1":
                    for c in range(16):
                        turn = at["d", "rel", c]
                        dve.tensor_tensor(relD[:, :, 8 * c:8 * (c + 1)],
                                          take(turn).rearrange("p (u c) -> p c u", c=64),
                                          bc(addmask[:, 8 * c:8 * (c + 1)], [P, 64, 8], 1), ALU.add)\
                           .then_inc(dve_drained, 1)
                if name == "att0" and part == "body2":
                    def finish(g):
                        b, g2 = divmod(g, 2)
                        turn = at["o", "out", g]
                        dve.wait_ge(out_filled, turn.filled)
                        o_ = BANK[turn.bank].rearrange("p (c t a e) -> p c t a e", c=2, t=2, a=4)
                        inv = sums[:, 0:16].rearrange("p (c t a) -> p c t a", c=2, t=2)
                        settle(dve.reciprocal(inv, o_[:, :, :, :, HD]))
                        for c in range(2):
                            h0 = 8 * g2 + 4 * c
                            dst = pad[:, 2 * b:2 * b + 2, HD * h0:HD * (h0 + 4)].rearrange("p t (a e) -> p t a e", a=4)
                            last = dve.tensor_tensor(dst, o_[:, c, :, :, 0:HD], bc(inv[:, c, :, :], [P, 2, 4, HD], 3),
                                                     ALU.mult)
                        last.then_inc(out_drained, 1)

                    for i in range(NB * H + 2):
                        if i < NB * H:
                            turn = at["s", "scores", i]
                            dve.wait_ge(score_filled, turn.filled)
                            dve.tensor_reduce(negmax[:, i % 4, 0:1], BANK[turn.bank][:, 0:P], AX, ALU.max, negate=True)
                            dve.tensor_reduce(negmax[:, i % 4, 1:2], BANK[turn.bank][:, P:3 * P], AX, ALU.max,
                                              negate=True).then_inc(negmax_ready, 1)
                        if i >= 2:
                            turn = at["d", "probs", i - 2]
                            dve.tensor_copy(probsT[(i - 2) % 3], take(turn)[:, 0:3 * P]).then_inc(dve_drained, 1)
                        if i >= 15 and (i - 15) % 8 == 0:
                            finish((i - 15) // 8)
                    finish(3)
                    dve.wait_ge(out_drained, at["o", "out", 3].drained)
                    settle(residual(name, hf, pad))

                if name == "ffn0" and part == "head":
                    comb = combs[hf]
                    turn = at["d", "logits"]
                    b_ = take(turn)[:, 0:2 * T].rearrange("p (t e) -> p t e", e=2)
                    settle(dve.tensor_copy(lg[:, 0:T], b_[:, :, 1]))
                    drained(dve.tensor_tensor(comb[:, 0:T], b_[:, :, 0], lg[:, 0:T], ALU.is_ge), turn)
                    for t in range(T):
                        last = dve.tensor_scalar(msk[hf][0][:, t, :], XN[:, hf, t, :], comb[:, t:t + 1], None, ALU.mult)
                    last.then_inc(masked_ready, 1)
                    dve.wait_ge(masked_ready, seen(masked_ready))
                    dve.tensor_tensor(msk[hf][1], XN[:, hf, :, :], msk[hf][0], ALU.subtract).then_inc(masked_ready, 1)
                    seen(masked_ready)
                if name == "ffn0" and part == "body2":
                    turn = at["o", "out"]
                    dve.wait_ge(out_filled, turn.filled)
                    residual(name, hf, BANK[turn.bank].rearrange("p (t d) -> p t d", t=T)).then_inc(out_drained, 1)
                    dve.wait_ge(out_drained, turn.drained)

                if name == "att1" and part[:6] == "scores":
                    xn, cx, sc1 = XN[:, hf, :, :], CX[:, hf, :, :], sc1_of[hf]
                    if hf == 0 and part == "scores1":
                        dve.wait_ge(ctx_loaded, 32)
                    if part == "scores1":
                        settle(dve.memset(sc1, NEG))
                    for dl in (range(0, 5) if part == "scores1" else range(5, H)):
                        w = D - HD * dl
                        pb = prod1[dl % 3][:, :, 0:w]
                        settle(dve.tensor_tensor(pb, xn[:, :, HD * dl:D], cx[:, :, 0:w], ALU.mult))
                        last = dve.tensor_reduce(sc1[:, :, dl:H, dl], pb.rearrange("p t (h e) -> p t h e", e=HD), AX, ALU.add)
                    settle(last)
                    if part == "scores2":
                        mx = sums[:, 0:T * H].rearrange("p (t h) -> p t h", t=T)
                        settle(dve.tensor_reduce(mx, sc1, AX, ALU.max))
                        dve.tensor_tensor(sc1, sc1, bc(mx, [P, T, H, H], 3), ALU.subtract).then_inc(shifted1, 1)
                        dve.wait_ge(expd1, seen(expd1))
                        settle(dve.tensor_reduce(mx, sc1, AX, ALU.add))
                        settle(dve.reciprocal(mx, mx))
                        settle(dve.tensor_tensor(sc1, sc1, bc(mx, [P, T, H, H], 3), ALU.mult))
                if name == "att1" and part == "body1":
                    cx, sc1 = CX[:, hf, :, :], sc1_of[hf]
                    for dl in range(H):
                        w = D - HD * dl
                        if dl >= 3:
                            dve.wait_ge(av1_used, (H - 1) * hf + dl - 2)
                        for t in range(T):
                            last = dve.tensor_tensor(prod1[dl % 3][:, t, 0:w].rearrange("p (h e) -> p h e", e=HD),
                                                     cx[:, t, 0:w].rearrange("p (h e) -> p h e", e=HD),
                                                     bc(sc1[:, t, dl:H, dl], [P, H - dl, HD], 2), ALU.mult)
                        last.then_inc(av1_ready, 1)
                if name == "att1" and part == "body2":
                    turn = at["o", "out"]
                    dve.wait_ge(out_filled, turn.filled)
                    residual(name, hf, BANK[turn.bank].rearrange("p (t d) -> p t d", t=T)).then_inc(out_drained, 1)
                    dve.wait_ge(out_drained, turn.drained)

                if name in ("ffn1", "ffn2"):
                    E, C = EXPERTS[name], CHUNKS[name]
                    R = E1 if name == "ffn1" else E2
                    comb = combs[hf]
                if name in ("ffn1", "ffn2") and part == "head":
                    turn = at["d", "logits"]
                    K = lg[:, 0:T * R].rearrange("p (t e) -> p t e", t=T)
                    src = take(turn)[:, 0:T * R].rearrange("p (t e) -> p t e", t=T)
                    if name == "ffn1":
                        dve.tensor_tensor(K, src, bc(sm("g1b"), [P, T, R], 1), ALU.add).then_inc(dve_drained, 1)
                        dve.wait_ge(dve_drained, turn.drained)
                        dve.tensor_scalar(K, K, 17.0, -87.0, ALU.min, ALU.max).then_inc(logits_ready, 1)
                        dve.wait_ge(logits_ready, seen(logits_ready))
                    else:
                        drained(dve.tensor_copy(K, src), turn)
                        softmax_keys(R)
                    settle(top2(comb, R, lg[:, 0:T * R], pr[:, 0:T * R], 1e-8 if name == "ffn1" else 0))

                if name in ("ffn1", "ffn2") and part[:4] == "body":
                    def product(e):
                        for c in range(C):
                            u, g = at["d", "up", e, c], at["a", "gate", e, c]
                            k = e * C + c
                            b_ = take(u)
                            dve.wait_ge(act_drained, g.drained)
                            dve.tensor_tensor(hidden[:, e % 2, c, :], b_, gated[:, k % 2, :], ALU.mult)\
                               .then_inc(dve_drained, 1)

                    def gather(e):
                        turn = at["o", "y", e]
                        dve.wait_ge(out_filled, turn.filled)
                        y = BANK[turn.bank].rearrange("p (t d) -> p t d", t=T)
                        g = e if name == "ffn2" else FFN1_ORDER[e]
                        if g == E1 and name == "ffn1":
                            last = dve.tensor_copy(acc, y)
                        else:
                            for t in range(T):
                                w = comb[:, t * R + g:t * R + g + 1]
                                if e == 0:
                                    last = dve.tensor_scalar(acc[:, t, :], y[:, t, :], w, None, ALU.mult)
                                else:
                                    last = dve.scalar_tensor_tensor(acc[:, t, :], y[:, t, :], w, acc[:, t, :],
                                                                    ALU.mult, ALU.add)
                        last.then_inc(out_drained, 1)
                        dve.wait_ge(out_drained, turn.drained)

                    for e in body_experts(name, part):
                        product(e)
                        if e:
                            gather(e - 1)
                    if part == "body2":
                        gather(E - 1)
                        settle(residual(name, hf, acc))

                if name == "att2" and part == "head":
                    turn = at["d", "gates"]
                    drained(dve.tensor_scalar(grow, take(turn)[0:64, :], sm("mgb", 64), None, ALU.add), turn)
                    fg, ig = grow[32:32 + MH, :], grow[0:MH, :]
                    settle(dve.tensor_scalar(row[3], fg, 0.0, None, ALU.min))
                    dve.wait_ge(flog_ready, seen(flog_ready))
                    settle(dve.tensor_tensor(row[3], row[3], row[1], ALU.subtract))
                    for b in range(NB):
                        bs = slice(b * S, (b + 1) * S)
                        last = dve.tensor_tensor_scan(row[0][:, bs], row[3][:, bs], row[3][:, bs], 0.0, ALU.add, ALU.bypass)
                    settle(last)
                    settle(dve.tensor_tensor(row[2], ig, row[0], ALU.subtract))
                    for b in range(NB):
                        bs = slice(b * S, (b + 1) * S)
                        last = dve.tensor_tensor_scan(row[3][:, bs], row[2][:, bs], row[2][:, bs], -3e38, ALU.max, ALU.max)
                    settle(last)
                    dve.tensor_tensor(row[0], row[0], row[3], ALU.add).then_inc(emarg_ready, 1)
                    dve.wait_ge(emarg_ready, seen(emarg_ready))
                    dve.tensor_scalar(negrun[hf], row[3], -1.0, None, ALU.mult).then_inc(rows_ready, 1)
                if name == "att2" and part == "body1":
                    turn = at["d", "cols"]
                    b_ = take(turn)
                    dve.tensor_copy(a_tok[hf][:, :, :], b_[:, 0:T * MH].rearrange("p (t h) -> p t h", t=T))
                    drained(dve.tensor_copy(em_tok[hf][:, :, :], b_[:, T * MH:2 * T * MH].rearrange("p (t h) -> p t h", t=T)), turn)
                if name == "att2" and part[:4] == "body":
                    for h in body_heads(part):
                        turn = at["d", "rows", h]
                        b_ = take(turn)
                        d_ = decay[h % 2]
                        for b in range(NB):
                            t0 = 2 * b
                            dve.scalar_tensor_tensor(d_[:, b, 0:S], b_[:, b * S:(b + 1) * S], a_tok[hf][:, t0, h:h + 1],
                                                     addmask, ALU.add, ALU.min)
                            last = dve.scalar_tensor_tensor(d_[:, b, S:S + P], b_[:, b * S + P:(b + 1) * S],
                                                            a_tok[hf][:, t0 + 1, h:h + 1], addmask[:, 0:P], ALU.add, ALU.min)
                        last.then_inc(dve_drained, 1)
                        dve.wait_ge(dve_drained, turn.drained)
                        dve.engine_nop().then_inc(dexp_in, 1)
                        dve.wait_ge(dexp_ready, seen(dexp_ready))
                        for b in range(NB):
                            turn = at["d", "scores", h, b]
                            dve.scalar_tensor_tensor(cmat[b], take(turn)[:, 0:3 * P], MD ** -0.5, d_[:, b, :],
                                                     ALU.mult, ALU.mult).then_inc(dve_drained, 1)
                if name == "att2" and part == "body2":
                    n_ = sums[:, 0:T * MH].rearrange("p (t h) -> p t h", t=T)
                    for b in range(NB):
                        turn = at["o", "out", b]
                        dve.wait_ge(out_filled, turn.filled)
                        o_ = BANK[turn.bank][:, 0:2 * MH * (MD + 1)].rearrange("p (a h e) -> p a h e", a=2, h=MH)
                        tb = slice(2 * b, 2 * b + 2)
                        settle(dve.tensor_tensor(n_[:, tb, :], o_[:, :, :, MD], em_tok[hf][:, tb, :], ALU.max))
                        settle(dve.tensor_scalar(n_[:, tb, :], n_[:, tb, :], 1e-6, None, ALU.add))
                        settle(dve.reciprocal(n_[:, tb, :], n_[:, tb, :]))
                        dve.tensor_tensor(mout[:, tb, :, :], o_[:, :, :, 0:MD], bc(n_[:, tb, :], [P, 2, MH, MD], 3),
                                          ALU.mult).then_inc(out_drained, 1)
                        dve.wait_ge(out_drained, turn.drained)
                    settle(dve.tensor_tensor(msq, mout, mout, ALU.mult))
                    settle(dve.tensor_reduce(n_, msq, AX, ALU.add))
                    rsqrt(dve.tensor_scalar(VE[:, 0:T * MH], sums[:, 0:T * MH], 1.0 / MD, 1e-6, ALU.mult, ALU.add))
                    settle(dve.tensor_tensor(mout, mout, bc(RS[:, 0:T * MH].rearrange("p (t h) -> p t h", t=T),
                                                           [P, T, MH, MD], 3), ALU.mult))
                    settle(dve.tensor_scalar(rms1[:, :], sm("rms"), 1.0, None, ALU.add))
                    m3 = mout.rearrange("p t h e -> p (t h) e")
                    settle(dve.tensor_tensor(m3, m3, bc(rms1[:, :], [P, T * MH, MD], 1), ALU.mult))
                    settle(residual(name, hf, mout.rearrange("p t h e -> p t (h e)")))

                if name == "att3" and part == "head":
                    def xpos(w, ws, cos, sin):
                        shape = [P, NB, S]
                        turn = at["d", w]
                        drained(dve.tensor_tensor(fval.rearrange("p (b s) -> p b s", b=NB),
                                                  take(turn).rearrange("p (b s) -> p b s", b=NB),
                                                  bc(sm(cos), shape, 1), ALU.mult), turn)
                        turn = at["d", ws]
                        drained(dve.tensor_tensor(ftmp.rearrange("p (b s) -> p b s", b=NB),
                                                  take(turn).rearrange("p (b s) -> p b s", b=NB),
                                                  bc(sm(sin), shape, 1), ALU.mult), turn)
                        settle(dve.tensor_tensor(fval, fval, ftmp, ALU.add))
                        split(fval, parts_ready)

                    xpos("k", "ks", "kcos", "ksin")
                    xpos("q", "qs", "qcos", "qsin")
                    turn = at["d", "gate"]
                    dve.tensor_tensor(gates3[hf], take(turn).rearrange("p (t d) -> p t d", t=T),
                                      bc(sm("rgb"), [P, T, D], 1), ALU.add).then_inc(dve_drained, 1)
                    dve.wait_ge(dve_drained, turn.drained)
                    dve.engine_nop().then_inc(gate3_in, 1)
                if name == "att3" and part[:4] == "body":
                    def collect(b, g):
                        turn = at["o", "out", b, g]
                        dve.wait_ge(out_filled, turn.filled)
                        o_ = BANK[turn.bank].rearrange("p (c t a e) -> p c t a e", c=2, t=2, a=4)
                        for c in range(2):
                            h0 = 8 * g + 4 * c
                            last = dve.tensor_copy(rets[hf][:, 2 * b:2 * b + 2, h0:h0 + 4, :], o_[:, c, :, :, 0:HD])
                        last.then_inc(out_drained, 1)

                    b = int(part == "body2")
                    for p_ in range(H // 2):
                        turn = at["d", "diag", b, p_]
                        dve.tensor_tensor(diag[p_ % 2].rearrange("p a b i -> p (a b) i"),
                                          take(turn).rearrange("p (a i) -> p a i", a=4),
                                          bc(sm("keep"), [P, 4, P], 1), ALU.mult).then_inc(dve_drained, 1)
                    collect(b, 0)
                    collect(b, 1)
                if name == "att3" and part == "tail":
                    ret = rets[hf]
                    dve.wait_ge(out_drained, at["o", "out", 1, 1].drained)
                    mu = sums[:, 0:T * H].rearrange("p (t h) -> p t h", t=T)
                    settle(dve.tensor_reduce(mu, ret, AX, ALU.add))
                    settle(dve.tensor_scalar(sums[:, 0:T * H], sums[:, 0:T * H], 1.0 / HD, None, ALU.mult))
                    settle(dve.tensor_tensor(ret, ret, bc(mu, [P, T, H, HD], 3), ALU.subtract))
                    settle(dve.tensor_tensor(retsq, ret, ret, ALU.mult))
                    settle(dve.tensor_reduce(mu, retsq, AX, ALU.add))
                    rsqrt(dve.tensor_scalar(VE[:, 0:T * H], sums[:, 0:T * H], 1.0 / HD, 1e-5, ALU.mult, ALU.add))
                    settle(dve.tensor_tensor(ret, ret, bc(RS[:, 0:T * H].rearrange("p (t h) -> p t h", t=T),
                                                         [P, T, H, HD], 3), ALU.mult))
                    dve.wait_ge(gate3_ready, seen(gate3_ready))
                    dve.tensor_tensor(y3, ret.rearrange("p t h e -> p t (h e)"), gates3[hf], ALU.mult).then_inc(y3_ready, 1)
                    dve.wait_ge(y3_ready, seen(y3_ready))
                    turn = at["d", "proj"]
                    drained(dve.tensor_tensor(gates3[hf], take(turn).rearrange("p (t d) -> p t d", t=T),
                                              bc(sm("rob"), [P, T, D], 1), ALU.add), turn)
                    settle(residual(name, hf, gates3[hf]))

                if name[:3] == "moe":
                    l = int(name[3])
                    z = XN[:, hf, :, :] if l == 0 else Z[l % 2][hf]
                    znew = Z[(l + 1) % 2][hf]
                    comb, xe = combs[hf], xe_of[hf]

                    def expert_input(e):
                        if e >= 2:
                            dve.wait_ge(act_filled, at["a", "h", e - 2, F0 - 1].filled)
                        k = l * E3 + e
                        dve.tensor_scalar(xe[e % 2], turned[:, hf, :], sm("lng")[:, k:k + 1], sm("lnb")[:, k:k + 1],
                                          ALU.mult, ALU.add).then_inc(xe_ready, 1)

                if name[:3] == "moe" and part == "head":
                    dve.wait_ge(act_drained, at["a", "xh"].drained)
                    expert_input(0)
                    expert_input(1)
                    turn = at["d", "logits"]
                    K = lg[:, 0:T * E3].rearrange("p (t e) -> p t e", t=T)
                    src = take(turn)[:, 0:T * E3].rearrange("p (t e) -> p t e", t=T)
                    rb = bc(sm("g3b")[:, l * E3:(l + 1) * E3], [P, T, E3], 1)
                    drained(dve.tensor_tensor(K, src, rb, ALU.add), turn)
                    softmax_keys(E3)
                    top2(comb, E3, lg[:, 0:T * E3], pr[:, 0:T * E3], 0).then_inc(comb_ready, 1)
                    dve.wait_ge(comb_ready, seen(comb_ready))
                    C = comb[:, 0:T * E3].rearrange("p (t e) -> p t e", t=T)
                    settle(dve.tensor_reduce(csum[hf][:, :], C, AX, ALU.add))
                if name[:3] == "moe" and part == "body1":
                    turn = at["d", "combT"]
                    drained(dve.tensor_copy(combT, take(turn)[0:E3, :]), turn)
                    turn = at["d", "bias"]
                    b_ = take(turn)
                    for t in range(T):
                        last = dve.scalar_tensor_tensor(znew[:, t, :], z[:, t, :], csum[hf][:, t:t + 1], b_[:, t * D:(t + 1) * D],
                                                        ALU.mult, ALU.add)
                    drained(last, turn)
                if name[:3] == "moe" and part[:4] == "body":
                    def gather(e):
                        turn = at["o", "y", e]
                        dve.wait_ge(out_filled, turn.filled)
                        for t in range(T):
                            last = dve.scalar_tensor_tensor(znew[:, t, :], BANK[turn.bank][:, t * D:(t + 1) * D],
                                                            comb[:, t * E3 + e:t * E3 + e + 1], znew[:, t, :],
                                                            ALU.mult, ALU.add)
                        last.then_inc(out_drained, 1)
                        dve.wait_ge(out_drained, turn.drained)

                    for e in body_experts(name, part):
                        if e + 2 < E3:
                            expert_input(e + 2)
                        if e:
                            gather(e - 1)
                    if part == "body2":
                        gather(E3 - 1)
                        if l == L3 - 1:
                            residual(name, hf, znew).then_inc(x_done[hf], 1)

                if part == "tail":
                    if name == "att3":
                        settle(layernorm(X[:, hf, :, :], XN[:, hf, :, :]))
                        layernorm(XN[:, hf, :, :], XH[:, hf, :, :]).then_inc(norm_done[hf], 1)
                    elif name[:3] != "moe":
                        layernorm(X[:, hf, :, :], XN[:, hf, :, :]).then_inc(norm_done[hf], 1)
                    elif name != "moe3":
                        layernorm(znew, XH[:, hf, :, :]).then_inc(norm_done[hf], 1)



def tables():
    j, i = np.arange(P)[:, None], np.arange(P)[None, :]
    c = {"ident": np.eye(P), "ones": np.ones((P, P)), "keep": i >= j}
    c["addmask"] = np.concatenate([np.where(i >= j, 0.0, NEG), np.zeros((P, P))], 1)
    e = np.arange(8)
    c["low"] = np.broadcast_to((e[None, :] < e[:, None]).reshape(1, 64), (P, 64))
    sel = np.zeros((P, MH, P))
    for h in range(MH):
        sel[h, h] = 1
    c["rows"] = sel.reshape(P, MH * P)
    half = HD // 2
    f = np.float32
    base = (np.arange(0, HD, 2, dtype=f) + f(0.4 * HD)) / f(1.4 * HD)
    power = np.arange(-(S // 2), S - S // 2, dtype=f) / f(512.0)
    scale = base[None, :].astype(np.float64) ** power[:, None]
    freq = f(1.0) / f(10000.0) ** (np.arange(half, dtype=f) / f(half))
    ang = (np.arange(S, dtype=f)[:, None] * freq[None, :].astype(f)).astype(np.float64)
    gam = f(1.0) - np.exp(np.linspace(np.log(1.0 / 32.0), np.log(1.0 / 512.0), H)).astype(f)
    pos = np.arange(S)
    sign = np.where(np.arange(HD) % 2 == 0, -1.0, 1.0)
    for w, sc, g in (("q", scale, pos), ("k", 1 / scale, -pos)):
        decay = gam[:, None].astype(np.float64) ** g[None, :]
        cos = np.repeat((np.cos(ang) * sc).T, 2, axis=0)
        sin = np.repeat((np.sin(ang) * sc).T, 2, axis=0) * sign[:, None]
        c[w + "cos"] = (decay[:, None, :] * cos[None]).reshape(P, S)
        c[w + "sin"] = (decay[:, None, :] * sin[None]).reshape(P, S)
    return {k: np.asarray(v, np.float32) for k, v in c.items()}


def pack(columns, n, parts):
    a = np.zeros((P, n), np.float32)
    for name, v in parts.items():
        at, w = columns[name]
        v = v.reshape(v.shape[0], -1)
        assert v.shape[1] == w, (name, v.shape, w)
        a[:v.shape[0], at:at + w] = v
    return a


def layout(i):
    def rows(v):
        return np.broadcast_to(v.reshape(1, -1), (P, v.size))

    def swap(w):
        return np.ascontiguousarray(w.reshape(D, H, HD // 2, 2)[..., ::-1]).reshape(D, D)

    def heads(w):
        return w.transpose(1, 0, 2).reshape(D, D)

    s = dict(tables())
    s["wq"], s["wk"], s["wv"] = i["L0_xattn_Wq"].T, i["L0_xattn_Wk"].T, i["L0_xattn_Wv"].T
    s["bq"], s["bk"], s["bv"] = i["L0_xattn_bq"][:, None], i["L0_xattn_bk"][:, None], rows(i["L0_xattn_bv"])
    s["gates"] = rows(np.concatenate([i["g_xattn"], i["g_ffn"]]))
    s["rows"][ROWS["er"][0]:ROWS["er"][0] + HD, 0:S] = i["L0_xattn_Er"].T
    s["rows"][ROWS["b2"][0]:ROWS["b2"][0] + E3, :] = i["L3_ffn_b2"].transpose(1, 0, 2).reshape(E3, L3 * D)
    s["g0w"], s["g1w"], s["g1b"], s["g2w"] = i["L0_ffn_gate_w"].T, i["L1_ffn_gate_w"].T, rows(i["L1_ffn_gate_b"]), i["L2_ffn_wg"].T
    s["g3w"], s["g3b"] = i["L3_ffn_router_w"].transpose(1, 0, 2), rows(i["L3_ffn_router_b"])
    s["s0b1"] = np.concatenate([i["L0_ffn_b1"], i["L0_ffn_sb1"][None]]).reshape(3, F0, P).transpose(2, 0, 1)
    s["b2s"] = np.concatenate([i["L0_ffn_b2"], i["L0_ffn_sb2"][None]])
    s["rms"] = rows(i["L2_xattn_rms_scale"])
    mg = np.zeros((D, 3, 64), np.float32)
    mg[:, :, 0:MH] = i["L2_xattn_igate_kernel"].reshape(3, D, MH).transpose(1, 0, 2)
    mg[:, :, 32:32 + MH] = i["L2_xattn_fgate_kernel"].reshape(3, D, MH).transpose(1, 0, 2)
    s["mgw"] = mg
    mb = np.zeros((P, 1), np.float32)
    mb[0:MH, 0], mb[32:32 + MH, 0] = i["L2_xattn_igate_bias"], i["L2_xattn_fgate_bias"]
    s["mgb"] = mb
    s["lng"], s["lnb"] = i["L3_ffn_ln_g"].reshape(L3 * E3, D).T, i["L3_ffn_ln_b"].reshape(L3 * E3, D).T
    s["b1"] = i["L3_ffn_b1"].reshape(L3 * E3 * F0, P).T
    wq, wk = heads(i["L3_xattn_W_Q"]), heads(i["L3_xattn_W_K"])
    s["rwq"], s["rwqs"], s["rwk"], s["rwks"], s["rwv"] = wq, swap(wq), wk, swap(wk), heads(i["L3_xattn_W_V"])
    s["rgw"], s["rgb"], s["row"], s["rob"] = i["L3_xattn_g_w"].T, rows(i["L3_xattn_g_b"]), i["L3_xattn_out_w"].T, rows(i["L3_xattn_out_b"])
    small = pack(SMALL, NSMALL, s)
    w0 = pack(W0, NW0, {
        "w1": np.concatenate([i["L0_ffn_w1"], i["L0_ffn_sw1"][None]]).transpose(1, 0, 2),
        "w2": np.concatenate([i["L0_ffn_w2"], i["L0_ffn_sw2"][None]]).reshape(3, F0, P, D).transpose(2, 0, 1, 3)})
    w1 = pack(W1, NW1, {
        "w1": np.concatenate([i["L1_ffn_ew1"], i["L1_ffn_fc1"][None]]).transpose(2, 0, 1),
        "w3": np.concatenate([i["L1_ffn_ew3"], i["L1_ffn_fc2"][None]]).transpose(2, 0, 1),
        "w2": np.concatenate([i["L1_ffn_ew2"], i["L1_ffn_fc3"][None]]).transpose(2, 0, 1)})
    w2 = pack(W2, NW2, {
        "w1": i["L2_ffn_w1"].transpose(2, 0, 1), "w3": i["L2_ffn_w3"].transpose(2, 0, 1),
        "w2": i["L2_ffn_w2"].transpose(2, 0, 1).reshape(I2, P, E2, D).transpose(1, 2, 0, 3)})
    w3 = np.stack([pack(W3, NW3, {
        "w1": i["L3_ffn_w1"][l].transpose(1, 0, 2),
        "w2": i["L3_ffn_w2"][l].reshape(E3, F0, P, D).transpose(2, 0, 1, 3)}) for l in range(L3)])
    return {"x": i["x"].reshape(2 * HALF, D), "ctx": i["ctx_1024"].reshape(2 * HALF, D),
            "ctxT": i["ctx_1024"].reshape(2 * HALF, D).T, "small": small, "w0": w0, "w1": w1, "w2": w2, "w3": w3}


def kernel(**inputs):
    import concourse.bacc as bacc
    from concourse.bass_utils import run_bass_kernel_spmd

    arrays = {k: np.ascontiguousarray(v) for k, v in layout({k: np.asarray(v) for k, v in inputs.items()}).items()}
    nc = bacc.Bacc("TRN2", target_bir_lowering=False, num_devices=1)
    args = [nc.dram_tensor(f"{k}_dram", v.shape, F32, kind="ExternalInput").ap() for k, v in arrays.items()]
    out = nc.dram_tensor("out_dram", (2 * HALF, D), F32, kind="ExternalOutput").ap()
    build(nc, *args, out)
    r = run_bass_kernel_spmd(nc, [{f"{k}_dram": v for k, v in arrays.items()}], core_ids=[0])
    return r.results[0]["out_dram"].reshape(4, S, D)
```

```python
from contextlib import ExitStack

import numpy as np

import concourse.bass as bass
from concourse import mybir

F32 = mybir.dt.float32
BF16 = mybir.dt.bfloat16
ALU = mybir.AluOpType
ACT = mybir.ActivationFunctionType
AX = mybir.AxisListType.X

P = 128
D = 128
S = 256
T = 4
HALF = T * P
NB = HALF // S
H = 16
HD = D // H
MH = 4
MD = D // MH
NEG = -1e30
F0 = 512 // P
E1, E2, E3, L3 = 6, 8, 4, 4
I2 = 256 // P
PARTS_A = (0, 0, 0, 1, 1, 2)
PARTS_B = (0, 1, 2, 0, 1, 0)
RUNS_A = ((0, 1), (0, 1), (0, 2), (1, 2))
RUNS_B = ((0, 3), (0, 2), (0, 1))
NSTACK = HD * len(PARTS_A)

SEGMENTS = [("att0", 0), ("att0", 1), ("ffn0", 0), ("ffn0", 1), ("att1", 0), ("ffn1", 0), ("att1", 1),
            ("ffn1", 1), ("att2", 0), ("att2", 1), ("ffn2", 0), ("ffn2", 1), ("att3", 0), ("att3", 1)]
SEGMENTS += [(f"moe{l}", hf) for l in range(L3) for hf in range(2)]


def steps_of(segments):
    special = {
        ("att0", 0): [("head", "att0", 1), ("body1", "att0", 0), ("body2", "att0", 0)],
        ("ffn0", 1): [("body1", "ffn0", 1), ("tail", "ffn0", 0), ("scores", "att1", 0), ("body2", "ffn0", 1)],
        ("att1", 0): [("body1", "att1", 0), ("body2", "att1", 0), ("tail", "att1", 0), ("head", "ffn1", 0),
                      ("tail", "ffn0", 1)],
        ("ffn1", 0): [("body1", "ffn1", 0), ("scores", "att1", 1), ("body2", "ffn1", 0)],
        ("att1", 1): [("body2", "att1", 1), ("tail", "att1", 1), ("head", "ffn1", 1),
                      ("tail", "ffn1", 0)],
        ("att2", 1): [("body1", "att2", 1), ("body2", "att2", 1), ("tail", "att2", 0), ("head", "ffn2", 0)],
        ("ffn2", 0): [("body1", "ffn2", 0), ("body2", "ffn2", 0), ("tail", "att2", 1), ("head", "ffn2", 1)],
        ("att3", 1): [("body1", "att3", 1), ("body2", "att3", 1), ("head", "moe0", 0)],
        ("moe0", 0): [("body1", "moe0", 0), ("tail", "att3", 1), ("body2", "moe0", 0), ("head", "moe0", 1)],
    }
    out = [("head",) + segments[0]]
    for k, seg in enumerate(segments):
        before = segments[k - 1] if k else None
        after = segments[k + 1] if k + 1 < len(segments) else None
        if seg in special:
            out += special[seg]
            continue
        early = before and before[0][:3] == "moe"
        if early:
            out += [("tail",) + before]
        out += [("body1",) + seg]
        if before and before[0] != "att1" and not early:
            out += [("tail",) + before]
        if after:
            out += [("head",) + after]
        out += [("body2",) + seg]
    return out


ROWS = {"sel": (0, MH), "b2": (32, E3), "er": (64, HD)}


def _columns(parts):
    at, n = {}, 0
    for name, w in parts:
        at[name] = (n, w)
        n += w
    return at, n


SMALL, NSMALL = _columns([
    ("wq", D), ("wk", D), ("wv", D), ("bq", 1), ("bk", 1), ("gates", 8), ("bv", D),
    ("ident", P),
    ("rows", MH * P),
    ("addmask", 2 * P), ("ones", P),
    ("low", 64), ("g0w", 2), ("g1w", E1), ("g1b", E1), ("g2w", E2), ("g3w", L3 * E3), ("g3b", L3 * E3),
    ("s0b1", 3 * F0), ("b2s", D), ("rms", MD), ("mgw", 3 * 64), ("mgb", 1),
    ("lng", L3 * E3), ("lnb", L3 * E3), ("b1", L3 * E3 * F0),
    ("rwq", D), ("rwqs", D), ("rwk", D), ("rwks", D), ("rwv", D), ("rgw", D), ("rgb", D), ("row", D), ("rob", D),
    ("keep", P), 
    ("qcos", S), ("qsin", S), ("kcos", S), ("ksin", S)])
W0, NW0 = _columns([("w1", 3 * F0 * P), ("w2", 3 * F0 * D)])
W1, NW1 = _columns([("w1", 7 * P), ("w3", 7 * P), ("w2", 7 * D)])
W2, NW2 = _columns([("w1", E2 * I2 * P), ("w3", E2 * I2 * P), ("w2", E2 * I2 * D)])
W3, NW3 = _columns([("w1", E3 * F0 * P), ("w2", E3 * F0 * D)])


class Tally:

    def __init__(self):
        self.n = {}

    def __call__(self, sem, by=1):
        self.n[sem.name] = self.n.get(sem.name, 0) + by
        return self.n[sem.name]

    def last(self, sem):
        return self.n[sem.name]


class Turn:

    def __init__(self, bank, n, free):
        self.bank, self.filled, self.drained, self.free = bank, n, n, free


def plan(steps):
    rings = {"a": [0, 1], "d": [2, 3], "s": [4, 5, 7], "o": [6]}
    count = {r: 0 for r in rings}
    turns = {}
    last = {}

    def use(ring, *label, half=None):
        bank = rings[ring][count[ring] % len(rings[ring])]
        count[ring] += 1
        turns[(name, hf if half is None else half, ring) + label] = Turn(bank, count[ring], last.get((ring, bank), 0))
        last[ring, bank] = count[ring]
        return turns[(name, hf if half is None else half, ring) + label]

    for part, name, hf in steps:
        kind = (name[:3] if name[:3] == "moe" else name, part)
        if kind == ("att0", "head"):
            use("a", "xt"), use("d", "q"), use("d", "k"), use("d", "v")
        if kind == ("att0", "body1"):
            for c in range(16):
                use("d", "rel", c)
                if c % 2:
                    use("a", "rel", c // 2)
        if kind == ("att0", "body2"):
            for n in range(NB * H):
                use("s", "scores", n)
                use("d", "probs", n)
                if n % 8 == 0:
                    use("a", "outT", n // 8)
                    use("o", "out", n // 8)
        if kind == ("ffn0", "head"):
            use("a", "xt"), use("d", "logits")
        if kind == ("ffn0", "body1"):
            use("o", "out")
            for c in range(F0):
                use("a", "h", FFN0_ORDER[0], c)
            use("a", "masked", 0), use("a", "masked", 1)
            for c in range(F0):
                use("a", "h", FFN0_ORDER[1], c)
        if kind == ("ffn0", "body2"):
            for c in range(F0):
                use("a", "h", FFN0_ORDER[2], c)
        if kind == ("att1", "body1"):
            use("s", "out")
        if (part, name, hf) == ("body2", "ffn1", 0):
            turns["att1", 1, "s", "out"] = use("s", "beside")
        if name in ("ffn1", "ffn2"):
            if part == "head":
                use("a", "xt"), use("d", "logits")
            for e in body_experts(name, part):
                for c in range(CHUNKS[name]):
                    use("a", "gate", e, c), use("d", "up", e, c)
                use("o", "y", e)
        if kind == ("att2", "head"):
            use("a", "xt"), use("d", "gates")
        if kind == ("att2", "body1"):
            use("d", "cols")
        if name == "att2" and part[:4] == "body":
            for h in range(2 * (part == "body1")):
                use("d", "rows", h)
            for h in body_heads(part):
                for b in range(NB):
                    use("d", "scores", h, b)
            for h in range(2, 2 + 2 * (part == "body1")):
                use("d", "rows", h)
            use("s", "outT", int(part == "body2"))
            use("o", "out", int(part == "body2"))
        if kind == ("att3", "head"):
            use("d", "k"), use("d", "ks"), use("a", "v"), use("a", "xt"), use("d", "q"), use("d", "qs"), use("d", "gate")
        if name == "att3" and part[:4] == "body":
            b = int(part == "body2")
            for p in range(H // 2):
                if (part, hf, p) == PROJECT_0:
                    use("a", "yt", half=0), use("d", "proj", half=0)
                if p % 4 == 0:
                    use("s", "outT", b, p // 4)
                    use("o", "out", b, p // 4)
                if p % 2 == 0:
                    use("a", "off", b, p // 2)
                use("d", "diag", b, p)
        if kind == ("att3", "tail") and hf == 1:
            use("a", "yt"), use("d", "proj")
        if (part, name, hf) == ("body1", "ffn0", 0):
            rings["s"], rings["o"] = [4, 5], [6, 7]
        if (part, name, hf) == ("head", "moe0", 0):
            rings["a"] = rings["a"] + rings["s"]
            turns["scores drained"] = count["s"]
        if kind == ("moe", "head"):
            use("a", "xt"), use("a", "xh"), use("d", "logits")
        if kind == ("moe", "body1"):
            use("d", "combT"), use("d", "bias")
        if name[:3] == "moe":
            for e in body_experts(name, part):
                for c in range(F0):
                    use("a", "h", e, c)
                use("o", "y", e)
    return turns


def body_experts(name, part):
    n = EXPERTS.get(name, E3)
    return {"body1": range(0, (n + 1) // 2), "body2": range((n + 1) // 2, n)}.get(part, range(0))


DISTANCES = {0: range(1, 4), 1: range(4, 7), 2: range(7, 11), 3: range(11, H)}
VALUE_DISTANCES = {4: range(0, 5), 5: range(5, 10), 6: range(10, H)}
OWN_DISTANCES = (range(2, H, 3), ())
NORM_BESIDE = {("body1", "att0", 1): ("att0", 0), ("body1", "ffn1", 1): ("ffn1", 0), ("body1", "att2", 0): ("ffn1", 1),
               ("body2", "att2", 1): ("att2", 0), ("body2", "ffn2", 0): ("att2", 1),
               ("body1", "ffn2", 1): ("ffn2", 0), ("body1", "att3", 0): ("ffn2", 1)}
PROJECT_0 = ("body2", 1, 2)
FFN0_ORDER = (2, 0, 1)
EXPERTS = {"ffn1": E1 + 1, "ffn2": E2}
CHUNKS = {"ffn1": 1, "ffn2": I2}
FFN1_ORDER = (6, 0, 1, 2, 3, 4, 5)


def shared(hf):
    return [dl for dl in range(H) if dl not in OWN_DISTANCES[hf]]


def body_heads(part):
    return range(0, MH // 2) if part == "body1" else range(MH // 2, MH)


def build(nc, x_in, ctx_in, ctxT_in, small_in, w0_in, w1_in, w2_in, w3_in, out):
    with ExitStack() as stack:
        def sb(name, shape, dt=F32):
            return stack.enter_context(nc.sbuf_tensor(name, shape, dt))

        def sem(name):
            return stack.enter_context(nc.semaphore(name))

        X = sb("X", [P, 2, T, D])
        XN = sb("XN", [P, 2, T, D])
        XT = sb("XT", [P, 2, HALF])
        CT = sb("CT", [P, 2, HALF])
        CX = sb("CX", [P, 2, T, D])
        V9 = sb("V9", [P, 2, T, H, HD + 1])
        V33 = sb("V33", [P, 2, T, MH, MD + 1])
        V3 = [V9[:, hf, :, :, :].rearrange("p t h e -> p (t h e)")[:, 0:T * D].rearrange("p (t d) -> p t d", t=T)
              for hf in range(2)]
        XH = V33[:, :, :, :, :].rearrange("p a t h e -> p (a t h e)")[:, 0:2 * T * D]\
            .rearrange("p (a t d) -> p a t d", a=2, t=T)
        small = sb("small", [P, NSMALL])
        W = sb("W", [P, max(NW0 + NW1, NW2)])
        arena = sb("arena", [P, 3 * 32 * P])
        hidden = sb("hidden", [P, 2, F0, HALF])
        q6_all = sb("q6", [64 + NSTACK, H, HALF], BF16)
        k6_all = sb("k6", [64 + NSTACK, H, HALF], BF16)
        er6_all = sb("er6", [64 + NSTACK, 384], BF16)
        q6, k6, er6 = ([t_[64 * hf:64 * hf + NSTACK] for hf in range(2)] for t_ in (q6_all, k6_all, er6_all))
        erp = sb("erp", [64 + HD, 3, 384], BF16)[64:64 + HD]
        erf = sb("erf", [64 + HD, 384])[64:64 + HD]
        zeros = sb("zeros", [1, 512], BF16)
        gated = sb("gated", [P, 2, HALF])
        turned = sb("turned", [P, 2, HALF])
        scratch = sb("scratch", [P, 24 * 256])
        TG = sb("TG", [P, 8])
        st6 = sb("st6", [P, T, 6])
        mv = sb("mv", [P, T, 2])
        VE = sb("VE", [P, 64])
        RS = sb("RS", [P, 64])
        mhalf = sb("mhalf", [P, 64])
        negmax = sb("negmax", [P, 4, 2])
        sums = sb("sums", [P, 64])
        rms1 = sb("rms1", [P, MD])
        rt = sb("rt", [P, 2 * T * 64])
        lg = sb("lg", [P, T * 8])
        pr = sb("pr", [P, T * 8])
        combs = [sb(f"comb{hf}", [P, T * 8]) for hf in range(2)]
        rs4 = sb("rs4", [P, T * 2])
        csum = [sb(f"csum{hf}", [P, T]) for hf in range(2)]
        combT = rt[32:32 + E3, 0:HALF]
        ps = [stack.enter_context(nc.psum_tensor(f"bank{i}", [P, 512], F32)) for i in range(8)]

        def sm(name, rows=P):
            a, w = SMALL[name]
            return small[0:rows, a:a + w]

        def scr(at, *shape):
            return cut(scratch, at, *shape)

        def cut(memory, at, *shape):
            n = int(np.prod(shape))
            v = memory[:, at:at + n]
            if len(shape) == 1:
                return v
            names = "abcd"[:len(shape)]
            return v.rearrange(f"p ({' '.join(names)}) -> p {' '.join(names)}",
                               **{c: s for c, s in zip(names[1:], shape[1:])})

        def few(name, cols):
            at, n = ROWS[name]
            return small[at:at + n, SMALL["rows"][0]:SMALL["rows"][0] + cols]

        ident = sm("ident")
        addmask = sm("addmask")
        w0, w1, w2 = W[:, 0:NW0], W[:, NW0:NW0 + NW1], W[:, 0:NW2]
        relD = arena[:, 0:2 * 32 * P].rearrange("p (c i) -> p c i", i=P)
        relO = arena[:, 2 * 32 * P:3 * 32 * P].rearrange("p (c i) -> p c i", i=P)
        w3 = [arena[:, s * NW3:(s + 1) * NW3] for s in range(2)]

        def spare(at, *shape):
            return cut(arena, 2 * NW3 + at, *shape)

        flat = hidden[:, :, :, :].rearrange("p a b c -> p (a b c)")
        probs = [flat[:, 3 * P * s:3 * P * (s + 1)] for s in range(4)]
        probsT = [flat[:, 3 * P * s:3 * P * (s + 1)] for s in range(4, 8)]
        outT = [flat[:, 3072 + 512 * s:3584 + 512 * s] for s in range(2)]

        fval = scr(0, HALF)
        ftmp = scr(512, HALF)
        parts = [scratch[:, 1024 + 768 * s:1024 + 768 * (s + 1)].bitcast(BF16).rearrange("p (c t) -> p c t", c=3)
                 for s in range(2)]
        pad = scr(2560, T, D)
        msk = [[scr(1024 * hf + 512 * s, T, D) for s in range(2)] for hf in range(2)]
        sc1_of = [spare(1024 * hf, T, H, H) for hf in range(2)]
        sprod = [scr(2560 + 512 * s, T, D) for s in range(4)]
        own = scr(4608, T, D)
        prod1 = [spare(2048 + 512 * s, T, D) for s in range(3)] + sprod
        acc = spare(3584, T, D)
        grow = scratch[0:64, 0:512]
        row = [scratch[0:MH, 512 * (1 + s):512 * (2 + s)] for s in range(4)]
        negrun = [scratch[0:MH, 2560 + 512 * hf:3072 + 512 * hf] for hf in range(2)]
        decay = [scr(3584 + 768 * s, NB, 3 * P) for s in range(2)] + \
                [spare(1024 + 768 * s, NB, 3 * P) for s in range(2)]
        cmat = [scr(5120 + 384 * s, 3 * P) for s in range(2)]
        mout = spare(0, T, MH, MD)
        msq = spare(512, T, MH, MD)
        a_tok = [sb(f"a_tok{hf}", [P, T, MH]) for hf in range(2)]
        em_tok = [sb(f"em_tok{hf}", [P, T, MH]) for hf in range(2)]
        diag = [scr(2560 + 512 * s, 2, 2, P) for s in range(2)] + [spare(2048, 2, 2, P)]
        gates3 = [scr(3584 + 512 * hf, T, D) for hf in range(2)]
        rets = [scr(4608 + 512 * hf, T, H, HD) for hf in range(2)]
        retsq = scr(5632, T, H, HD)
        y3 = spare(3584, T, D)
        Z = [[scr(512 * (2 * s + hf), T, D) for hf in range(2)] for s in range(2)]
        xe_of = [[spare(512 * (2 * hf + s), HALF) for s in range(2)] for hf in range(2)]

        stage = {(k, hf): nc.dram_tensor(f"parts_{k}_{hf}", (3, P, HALF), BF16, kind="Internal").ap()
                 for k in ("k0", "q0", "k3", "q3") for hf in range(2)}

        small_loaded, ctx_loaded = sem("small_loaded"), sem("ctx_loaded")
        ctxT_loaded = [sem(f"ctxT_loaded{h}") for h in range(2)]
        mask_loaded = sem("mask_loaded")
        rest_loaded = sem("rest_loaded")
        x_loaded = [sem(f"x_loaded{h}") for h in range(2)]
        w0_loaded, w1_loaded, w2_loaded = sem("w0_loaded"), sem("w1_loaded"), sem("w2_loaded")
        w3_loaded = [sem(f"w3_loaded{s}") for s in range(2)]
        consts_done = sem("consts_done")
        v33_done = sem("v33_done")
        tanh_done = sem("tanh_done")
        er_parts = sem("er_parts")
        er_stacked = [sem(f"er_stacked{h}") for h in range(2)]
        parts_ready = sem("parts_ready")
        parts_out = [sem(f"parts_out{s}") for s in range(2)]
        stacked_k = [sem(f"stacked_k{h}") for h in range(2)]
        stacked_q = [sem(f"stacked_q{h}") for h in range(2)]
        norm_done = [sem(f"norm_done{h}") for h in range(2)]
        var_ready = sem("var_ready")
        rstd_ready = sem("rstd_ready")
        act_filled, act_drained = sem("act_filled"), sem("act_drained")
        dve_filled, dve_drained = sem("dve_filled"), sem("dve_drained")
        score_filled, score_drained = sem("score_filled"), sem("score_drained")
        out_filled, out_drained = sem("out_filled"), sem("out_drained")
        negmax_ready = sem("negmax_ready")
        masked_ready = sem("masked_ready")
        logits_ready = sem("logits_ready")
        weights_ready = sem("weights_ready")
        prod_ready, prod_used = sem("prod_ready"), sem("prod_used")
        headvar_ready, headsqrt_ready = sem("headvar_ready"), sem("headsqrt_ready")
        shifted1, expd1 = sem("shifted1"), sem("expd1")
        av1_ready, av1_used = sem("av1_ready"), sem("av1_used")
        flog_ready = sem("flog_ready")
        emarg_ready, em_ready = sem("emarg_ready"), sem("em_ready")
        rows_ready = sem("rows_ready")
        dexp_in, dexp_ready = sem("dexp_in"), sem("dexp_ready")
        gate3_in, gate3_ready = sem("gate3_in"), sem("gate3_ready")
        y3_ready = sem("y3_ready")
        comb_ready = sem("comb_ready")
        xe_ready = sem("xe_ready")
        step = sem("dve_step")
        astep = sem("act_step")
        x_done = [sem(f"x_done{h}") for h in range(2)]
        out_stored = sem("out_stored")

        NORM = {"att0": 1, "ffn0": 2, "att1": 3, "ffn1": 4, "att2": 5, "ffn2": 6, "att3": 7,
                "moe0": 8, "moe1": 9, "moe2": 10, "moe3": 11}
        GATE = {"att0": 0, "att1": 1, "att2": 2, "att3": 3, "ffn0": 4, "ffn1": 5, "ffn2": 6, "moe3": 7}
        steps = steps_of(SEGMENTS)
        turns = plan(steps)
        BANK = [p_[:, :] for p_ in ps]

        block = stack.enter_context(nc.Block())

        @block.sync
        def _(sp):
            seen = Tally()
            cut = SMALL["rms"][0]
            mask = SMALL["addmask"][0]
            xv = x_in.rearrange("(h t p) d -> h p t d", h=2, p=P)
            cv = ctx_in.rearrange("(h t p) d -> h p t d", h=2, p=P)
            for hf in range(2):
                sp.dma_start(X[:, hf, :, :], xv[hf]).then_inc(x_loaded[hf], 16)
                if hf == 0:
                    sp.dma_start(small[:, 0:mask], small_in[:, 0:mask]).then_inc(small_loaded, 16)
                sp.dma_start(CT[:, hf, :], ctxT_in[:, hf * HALF:(hf + 1) * HALF]).then_inc(ctxT_loaded[hf], 16)
            sp.dma_start(small[:, mask:cut], small_in[:, mask:cut]).then_inc(mask_loaded, 16)
            n_parts = 0

            def restack(kind, hf, dst, runs, loaded):
                nonlocal n_parts
                buf = n_parts % 2
                n_parts += 1
                sp.wait_ge(parts_ready, n_parts)
                sp.dma_start(stage[kind, hf].rearrange("c p t -> p c t"), parts[buf]).then_inc(parts_out[buf], 16)
                sp.wait_ge(parts_out[buf], seen(parts_out[buf], 16))
                src = stage[kind, hf].rearrange("c (e h) t -> (c e) h t", e=HD)
                at = 0
                for first, n in runs:
                    sp.dma_start(dst[at:at + HD * n, :, :], src[HD * first:HD * (first + n), :, :]).then_inc(loaded, 16)
                    at += HD * n

            for hf in range(2):
                if hf == 0:
                    sp.wait_ge(er_parts, 1)
                for r, c in enumerate(PARTS_B):
                    sp.dma_start(er6[hf][HD * r:HD * (r + 1), :], erp[:, c, :]).then_inc(er_stacked[hf], 16)
                restack("q0", hf, q6[hf], RUNS_A, stacked_q[hf])
                restack("k0", hf, k6[hf], RUNS_B, stacked_k[hf])
                if hf == 0:
                    sp.dma_start(small[:, cut:], small_in[:, cut:]).then_inc(rest_loaded, 16)
                    sp.dma_start(w0, w0_in).then_inc(w0_loaded, 16)
                    for h2 in range(2):
                        sp.dma_start(CX[:, h2, :, :], cv[h2]).then_inc(ctx_loaded, 16)
                    sp.dma_start(w1, w1_in).then_inc(w1_loaded, 16)
            sp.wait_ge(norm_done[1], NORM["att0"] + 1)
            for l in range(2):
                sp.dma_start(w3[l], w3_in[l]).then_inc(w3_loaded[l], 16)
            for hf in range(2):
                sp.wait_ge(norm_done[hf], NORM["ffn1"] + 1)
            sp.dma_start(w2, w2_in).then_inc(w2_loaded, 16)
            for hf in range(2):
                restack("k3", hf, k6[hf], RUNS_B, stacked_k[hf])
                restack("q3", hf, q6[hf], RUNS_A, stacked_q[hf])
            for l in range(L3 - 2):
                for hf in range(2):
                    sp.wait_ge(norm_done[hf], NORM[f"moe{l}"] + 1)
                sp.dma_start(w3[l], w3_in[l + 2]).then_inc(w3_loaded[l], 16)
            ov = out.rearrange("(h t p) d -> h p t d", h=2, p=P)
            for hf in range(2):
                sp.wait_ge(x_done[hf], 1)
                sp.dma_start(ov[hf], X[:, hf, :, :]).then_inc(out_stored, 16)
            sp.wait_ge(out_stored, 32)

        @block.gpsimd
        def _(pool):
            seen = Tally()
            pool.memset(mhalf[:, :], -0.5)
            pool.memset(zeros[:, :], 0.0)
            for hf in range(2):
                pool.memset(V9[:, hf, :, :, HD:HD + 1], 1.0)
            pool.memset(V33[:, :, :, :, MD:MD + 1], 1.0).then_inc(consts_done, 1)
            pool.wait_ge(consts_done, 1)

            def rsqrt(n):
                pool.wait_ge(var_ready, seen(var_ready))
                pool.tensor_tensor(RS[:, 0:n], VE[:, 0:n], mhalf[:, 0:n], ALU.pow).then_inc(rstd_ready, 1)

            for hf in range(2):
                rsqrt(T)
            for part, name, hf in steps:
                if (part, name, hf) in (("scores", "att1", 0), ("body1", "ffn1", 0)):
                    hq = int(name == "ffn1")
                    pool.wait_ge(ctx_loaded, 32)
                    pool.wait_ge(norm_done[hq], NORM["att1"])
                    for k, dl in enumerate(shared(hq)):
                        n, w = hq * len(shared(0)) + k, D - HD * dl
                        if n >= 4:
                            pool.wait_ge(prod_used, n - 3)
                        pool.tensor_tensor(sprod[k % 4][:, :, 0:w], XN[:, hq, :, HD * dl:D], CX[:, hq, :, 0:w],
                                           ALU.mult).then_inc(prod_ready, 1)
                if (part, name, hf) in (("body1", "att2", 1), ("body1", "ffn2", 0)):
                    rsqrt(T * MH)
                if (part, name, hf) == ("body2", "att3", 1):
                    rsqrt(T)
                    rsqrt(T)
                if (part, name, hf) == ("tail", "att3", 0):
                    continue
                if (part, name) == ("tail", "att3"):
                    rsqrt(T)
                if part == "tail" and name != "moe3":
                    rsqrt(T)
                if (part, name, hf) == ("head", "ffn0", 0):
                    pool.wait_ge(ctx_loaded, 32)
                    for h2 in range(2):
                        for h in range(MH):
                            last = pool.tensor_copy(V33[:, h2, :, h, 0:MD], CX[:, h2, :, MD * h:MD * (h + 1)])
                    last.then_inc(v33_done, 1)

        @block.scalar
        def _(act):
            seen = Tally()
            act.wait_ge(small_loaded, 16)
            act.activation(TG[:, :], sm("gates"), ACT.Tanh).then_inc(tanh_done, 1)

            def drain(turn, dst, func=ACT.Copy, **kw):
                act.wait_ge(act_filled, turn.filled)
                src = BANK[turn.bank]
                if len(dst.shape) == 3:
                    src = src.rearrange("p (a b) -> p a b", a=dst.shape[1])
                act.activation(dst, src, func, **kw).then_inc(act_drained, 1)

            def head_sqrt(hf):
                act.wait_ge(headvar_ready, hf + 1)
                act.activation(RS[:, 0:T * H], VE[:, 0:T * H], ACT.Sqrt).then_inc(headsqrt_ready, 1)

            def weights(name):
                n = T * {"ffn1": E1, "ffn2": E2}.get(name, E3)
                act.wait_ge(logits_ready, seen(logits_ready))
                act.activation(pr[:, 0:n], lg[:, 0:n], ACT.Sigmoid if name == "ffn1" else ACT.Tanh)\
                   .then_inc(weights_ready, 1)

            before = None
            for part, name, hf in steps:
                at = {k[2:]: v for k, v in turns.items() if k[:2] == (name, hf)}
                if part == "head":
                    if name == "att3":
                        drain(at["a", "v"], V3[hf])
                    drain(at["a", "xt"], XT[:, hf, :])
                    if name[:3] == "moe":
                        drain(at["a", "xh"], turned[:, hf, :])

                if name == "att0" and part == "body1":
                    for c in range(8):
                        turn = at["a", "rel", c]
                        act.wait_ge(act_filled, turn.filled)
                        act.activation(relO[:, :, 16 * c:16 * (c + 1)],
                                       BANK[turn.bank].rearrange("p (u c) -> p c u", c=NB * H), ACT.Copy)\
                           .then_inc(act_drained, 1)
                if name == "att0" and part == "body2":
                    for i in range(NB * H + 6):
                        if i < NB * H:
                            turn = at["s", "scores", i]
                            act.wait_ge(negmax_ready, seen(negmax_ready))
                            pr_ = probs[i % 4]
                            act.activation(pr_[:, 0:P], BANK[turn.bank][:, 0:P], ACT.Exp, bias=negmax[:, i % 4, 0:1])
                            act.activation(pr_[:, P:3 * P], BANK[turn.bank][:, P:3 * P], ACT.Exp,
                                           bias=negmax[:, i % 4, 1:2]).then_inc(score_drained, 1)
                        if i >= 13 and (i - 13) % 8 == 0:
                            g = (i - 13) // 8
                            drain(at["a", "outT", g], outT[g % 2])

                if name == "ffn0" and part[:4] == "body":
                    for k in ((0, 1) if part == "body1" else (2,)):
                        e = FFN0_ORDER[k]
                        for c in range(F0):
                            if hf == 0 and k == 0 and c == 0:
                                act.wait_ge(mask_loaded, 16)
                                act.wait_ge(rest_loaded, 16)
                            drain(at["a", "h", e, c], hidden[:, k % 2, c, :], ACT.Relu,
                                  bias=sm("s0b1")[:, e * F0 + c:e * F0 + c + 1])
                        if k == 0:
                            for m in range(2):
                                drain(at["a", "masked", m], turned[:, m, :])

                if (part, name, hf) in (("body2", "ffn0", 1), ("scores", "att1", 1)):
                    sc1 = sc1_of[int(name == "att1")]
                    act.wait_ge(shifted1, seen(shifted1))
                    act.activation(sc1, sc1, ACT.Exp, scale=HD ** -0.5).then_inc(expd1, 1)

                if name in ("ffn1", "ffn2"):
                    if (part, name) == ("head", "ffn1"):
                        weights(name)
                    chunks = [(e, c) for e in range(EXPERTS[name]) for c in range(CHUNKS[name])]
                    for k, (e, c) in enumerate(chunks):
                        if e not in body_experts(name, part):
                            continue
                        if k >= 2:
                            act.wait_ge(dve_drained, at[("d", "up") + chunks[k - 2]].drained)
                        drain(at["a", "gate", e, c], gated[:, k % 2, :], ACT.Silu)
                        if (name, k) == ("ffn2", 0):
                            weights(name)

                if name == "att2" and part == "head":
                    act.wait_ge(dve_drained, at["d", "gates"].drained)
                    act.activation(row[1], grow[32:32 + MH, :], ACT.Abs).then_inc(astep, 1)
                    act.wait_ge(astep, seen(astep))
                    act.activation(row[1], row[1], ACT.Exp, scale=-1.0).then_inc(astep, 1)
                    act.wait_ge(astep, seen(astep))
                    act.activation(row[1], row[1], ACT.Ln, bias=sm("ones", MH)[:, 0:1]).then_inc(flog_ready, 1)
                if name == "att2" and part[:4] == "body":
                    def decays(h):
                        act.wait_ge(dexp_in, seen(dexp_in))
                        act.activation(decay[h], decay[h], ACT.Exp).then_inc(dexp_ready, 1)

                    if part == "body1":
                        decays(0)
                        decays(1)
                    g = int(part == "body2")
                    turn = at["s", "outT", g]
                    act.wait_ge(score_filled, turn.filled)
                    act.activation(outT[g], BANK[turn.bank], ACT.Copy).then_inc(score_drained, 1)
                    if part == "body1":
                        decays(2)
                        decays(3)

                if name == "att3" and part == "head":
                    act.wait_ge(gate3_in, seen(gate3_in))
                    act.activation(gates3[hf], gates3[hf], ACT.Silu).then_inc(gate3_ready, 1)
                if name == "att3" and part[:4] == "body":
                    b = int(part == "body2")
                    for g in range(H // 4):
                        if (part, hf, 2 * g) == PROJECT_0:
                            drain(turns["att3", 0, "a", "yt"], turned[:, 0, :])
                        drain(at["a", "off", b, g], gated[:, g % 2, :])
                        if (hf, part, g) == (1, "body1", 3):
                            head_sqrt(0)
                        if g >= 2:
                            turn = at["s", "outT", b, g - 2]
                            act.wait_ge(score_filled, turn.filled)
                            act.activation(outT[g - 2], BANK[turn.bank], ACT.Copy).then_inc(score_drained, 1)
                if name == "att3" and part == "tail" and hf == 1:
                    drain(at["a", "yt"], turned[:, hf, :])

                if name[:3] == "moe":
                    l = int(name[3])
                    if part == "head" and l == 0:
                        weights(name)
                    for e in body_experts(name, part):
                        for c in range(F0):
                            k = (l * E3 + e) * F0 + c
                            drain(at["a", "h", e, c], hidden[:, e % 2, c, :], ACT.Gelu, bias=sm("b1")[:, k:k + 1])
                            if part == "body2" and e == 2 and c == 3 and before[0] == "head":
                                weights(before[1])
                            if (part, name, hf, e, c) == ("body1", "moe0", 0, 0, F0 - 1):
                                head_sqrt(1)
                if (part, name, hf) in (("body2", "ffn1", 1), ("body2", "att2", 0)):
                    act.wait_ge(emarg_ready, seen(emarg_ready))
                    act.activation(row[0], row[0], ACT.Exp, scale=-1.0).then_inc(em_ready, 1)
                before = (part, name, hf)

        @block.tensor
        def _(pe):
            seen = Tally()

            def mm(dst, lhsT, rhs, start, stop=False, turn=False):
                return pe.matmul(dst, lhsT, rhs, start=start, stop=stop, is_transpose=turn or None,
                                 skip_group_check=True)

            def bank(turn, drained):
                if turn.free:
                    pe.wait_ge(drained, turn.free)
                return BANK[turn.bank]

            def turn_tiles(turn, src):
                b_ = bank(turn, act_drained)
                for t in range(T):
                    last = mm(b_[:, t * P:(t + 1) * P], src[:, t, :], ident, start=(t == 0), stop=True, turn=True)
                last.then_inc(act_filled, 1)

            def tokens(turn, lhsT, rhs, n, ring=(dve_drained, dve_filled)):
                b_ = bank(turn, ring[0])
                for t in range(T):
                    last = mm(b_[:, t * n:(t + 1) * n], lhsT[:, t * P:(t + 1) * P], rhs, start=True, stop=True)
                last.then_inc(ring[1], 1)

            def feats(turn, w, rhs, drained, filled):
                mm(bank(turn, drained), w, rhs, start=True, stop=True).then_inc(filled, 1)

            def inputs(name, hf, at):
                pe.wait_ge(norm_done[hf], NORM[name])
                turn_tiles(at["a", "xt"], XN[:, hf, :, :])

            def second(turn, n, w2_, slot, ready, count, first=True, close=True):
                b_ = BANK[turn.bank] if not first else bank(turn, out_drained)
                pe.wait_ge(ready, count)
                for t in range(T):
                    for c in range(n):
                        last = mm(b_[:, t * P:(t + 1) * P], hidden[:, slot, c, t * P:(t + 1) * P], w2_(c),
                                  start=(first and t == 0 and c == 0), stop=(c == n - 1))
                if close:
                    last.then_inc(out_filled, 1)

            def ffn_weights(name):
                cols, w_ = (W1, w1) if name == "ffn1" else (W2, w2)
                return [w_[:, cols[k][0]:cols[k][0] + cols[k][1]]
                        .rearrange("p (e c f) -> p e c f", e=EXPERTS[name], c=CHUNKS[name]) for k in ("w1", "w3", "w2")]

            def weighted(hf, distances):
                turn = turns["att1", hf, "s", "out"]
                o_ = BANK[turn.bank].rearrange("p (t d) -> p t d", t=T)
                for dl in distances:
                    if dl == 0:
                        bank(turn, score_drained)
                    pe.wait_ge(av1_ready, seen(av1_ready))
                    w = D - HD * dl
                    last = mm(o_[:, :, HD * dl:D], ident, prod1[dl % len(prod1)][:, :, 0:w], start=(dl == 0), stop=(dl == H - 1))
                    last.then_inc(av1_used if dl < H - 1 else score_filled, 1)

            def moe_logits(name, hf):
                l = int(name[3])
                pe.wait_ge(act_drained, turns[name, hf, "a", "xt"].drained)
                tokens(turns[name, hf, "d", "logits"], XT[:, hf, :], sm("g3w")[:, l * E3:(l + 1) * E3], E3)

            def project(hf):
                yt = turns["att3", hf, "a", "yt"]
                pe.wait_ge(y3_ready, seen(y3_ready))
                turn_tiles(yt, y3)
                pe.wait_ge(act_drained, yt.drained)
                tokens(turns["att3", hf, "d", "proj"], turned[:, hf, :], sm("row"), D)

            def blocks_turned(turn, src, ring):
                b_ = bank(turn, out_drained)
                pe.wait_ge(*ring)
                for k in range(4):
                    last = mm(b_[:, k * P:(k + 1) * P], src[:, k * P:(k + 1) * P], ident, start=(k == 0), stop=True, turn=True)
                last.then_inc(out_filled, 1)

            def clear(turn, drained):
                mm(bank(turn, drained), zeros[:, 0:P], zeros[:, :], start=True)

            pe.wait_ge(small_loaded, 16)
            for part, name, hf in steps:
                at = {k[2:]: v for k, v in turns.items() if k[:2] == (name, hf)}

                if name == "att0" and part == "head":
                    inputs(name, hf, at)
                    pe.wait_ge(act_drained, at["a", "xt"].drained)
                    feats(at["d", "q"], sm("wq"), XT[:, hf, :], dve_drained, dve_filled)
                    pe.wait_ge(ctxT_loaded[hf], 16)
                    feats(at["d", "k"], sm("wk"), CT[:, hf, :], dve_drained, dve_filled)
                    tokens(at["d", "v"], CT[:, hf, :], sm("wv"), D)
                if name == "att0" and part == "body1":
                    pe.wait_ge(er_stacked[hf], 16 * len(PARTS_B))
                    pe.wait_ge(stacked_q[hf], 16 * len(RUNS_A))
                    qv = q6[hf].rearrange("k h (c i) -> k c h i", i=P)
                    for c in range(16):
                        b_ = bank(at["d", "rel", c], dve_drained)
                        for u in range(8):
                            i = 8 * c + u
                            last = mm(b_[:, u * 64:(u + 1) * 64], er6[hf][:, S - 1 - i:S - 1 - i + P], qv[:, :, :, i],
                                      start=True, stop=True)
                        last.then_inc(dve_filled, 1)
                        if c % 2:
                            b_ = bank(at["a", "rel", c // 2], act_drained)
                            for u in range(16):
                                i = 16 * (c // 2) + u
                                last = mm(b_[:, u * 32:(u + 1) * 32], er6[hf][:, P - 1 - i:2 * P - 1 - i],
                                          qv[:, 1::2, :, i], start=True, stop=True)
                            last.then_inc(act_filled, 1)
                if name == "att0" and part == "body2":
                    pe.wait_ge(stacked_k[hf], 16 * len(RUNS_B))
                    pe.wait_ge(dve_drained, at["d", "rel", 15].drained)
                    pe.wait_ge(act_drained, at["a", "rel", 7].drained)
                    for i in range(NB * H + 8):
                        if i < NB * H:
                            b, h = divmod(i, H)
                            s_ = bank(at["s", "scores", i], score_drained)
                            q0 = b * S
                            mm(s_[:, 0:P], relD[:, 2 * b * H + h, :], ident, start=True, turn=True)
                            mm(s_[:, P:2 * P], relO[:, b * H + h, :], ident, start=False, turn=True)
                            mm(s_[:, 2 * P:3 * P], relD[:, (2 * b + 1) * H + h, :], ident, start=False, turn=True)
                            mm(s_[:, 0:P], q6[hf][:, h, q0:q0 + P], k6[hf][:, h, q0:q0 + P], start=False)
                            mm(s_[:, P:3 * P], q6[hf][:, h, q0 + P:q0 + S], k6[hf][:, h, q0:q0 + S], start=False,
                               stop=True).then_inc(score_filled, 1)
                        if 3 <= i < NB * H + 3:
                            n = i - 3
                            pt = bank(at["d", "probs", n], dve_drained)
                            pe.wait_ge(score_drained, at["s", "scores", n].drained)
                            for k in range(3):
                                last = mm(pt[:, k * P:(k + 1) * P], probs[n % 4][:, k * P:(k + 1) * P], ident,
                                          start=(k == 0), stop=True, turn=True)
                            last.then_inc(dve_filled, 1)
                        if 5 <= i < NB * H + 5:
                            n = i - 5
                            b, h = divmod(n, H)
                            turn = at["a", "outT", n // 8]
                            if n == 0:
                                pe.wait_ge(dve_drained, at["d", "v"].drained)
                                pe.wait_ge(consts_done, 1)
                            if n % 8 == 0:
                                clear(turn, act_drained)
                            pe.wait_ge(dve_drained, at["d", "probs", n].drained)
                            pt = probsT[n % 4]
                            o_, c0 = BANK[turn.bank][32 * (h % 4):32 * (h % 4) + HD + 1, :], S * (h // 4 % 2)
                            v0, v1 = V9[:, hf, 2 * b, h, :], V9[:, hf, 2 * b + 1, h, :]
                            mm(o_[:, c0:c0 + S], v0, pt[:, 0:S], start=False)
                            last = mm(o_[:, c0 + P:c0 + S], v1, pt[:, S:S + P], start=False, stop=True)
                            if n % 8 == 7:
                                last.then_inc(act_filled, 1)
                        if i >= 15 and (i - 15) % 8 == 0:
                            g = (i - 15) // 8
                            blocks_turned(at["o", "out", g], outT[g % 2], (act_drained, at["a", "outT", g].drained))

                if name == "ffn0":
                    w1_ = w0[:, W0["w1"][0]:].rearrange("p (e c f) -> p e c f", e=6, c=F0)
                    w2_ = w0[:, W0["w2"][0]:].rearrange("p (e c d) -> p e c d", e=3, c=F0)

                    def first(e, rhs):
                        for c in range(F0):
                            feats(at["a", "h", e, c], w1_[:, e, c, :], rhs, act_drained, act_filled)

                    def then(k):
                        e = FFN0_ORDER[k]
                        second(at["o", "out"], F0, lambda c: w2_[:, e, c, :], k % 2, act_drained,
                               at["a", "h", e, F0 - 1].drained, first=False, close=(k == 2))

                    if part == "head":
                        inputs(name, hf, at)
                        if hf == 0:
                            pe.wait_ge(mask_loaded, 16)
                            pe.wait_ge(rest_loaded, 16)
                        pe.wait_ge(act_drained, at["a", "xt"].drained)
                        tokens(at["d", "logits"], XT[:, hf, :], sm("g0w"), 2)
                    if part == "body1":
                        o_ = bank(at["o", "out"], out_drained)
                        for t in range(T):
                            mm(o_[:, t * P:(t + 1) * P], sm("ones", 3), sm("b2s", 3), start=(t == 0))
                        if hf == 0:
                            pe.wait_ge(w0_loaded, 16)
                        first(2, XT[:, hf, :])
                        for m in range(2):
                            pe.wait_ge(masked_ready, seen(masked_ready))
                            turn_tiles(at["a", "masked", m], msk[hf][m])
                        pe.wait_ge(act_drained, at["a", "masked", 0].drained)
                        first(0, turned[:, 0, :])
                        then(0)
                    if part == "body2":
                        pe.wait_ge(act_drained, at["a", "masked", 1].drained)
                        first(1, turned[:, 1, :])
                        then(1)
                        then(2)

                if name == "att1" and part == "body1":
                    weighted(hf, range(H))

                if name in ("ffn1", "ffn2"):
                    E, C = EXPERTS[name], CHUNKS[name]
                    wg, wu, wd = ffn_weights(name)

                    def down(e):
                        g = e if name == "ffn2" else FFN1_ORDER[e]
                        second(at["o", "y", e], C, lambda c: wd[:, g, c, :], e % 2, dve_drained,
                               at["d", "up", e, C - 1].drained)

                    if part == "head":
                        inputs(name, hf, at)
                        pe.wait_ge(act_drained, at["a", "xt"].drained)
                        if name == "ffn1":
                            tokens(at["d", "logits"], XT[:, hf, :], sm("g1w"), E1)
                        else:
                            tokens(at["d", "logits"], XT[:, hf, :], sm("g2w"), E2)
                    if part == "body1" and hf == 0:
                        pe.wait_ge(w1_loaded if name == "ffn1" else w2_loaded, 16)
                    for e in body_experts(name, part):
                        g = e if name == "ffn2" else FFN1_ORDER[e]
                        for c in range(C):
                            feats(at["a", "gate", e, c], wg[:, g, c, :], XT[:, hf, :], act_drained, act_filled)
                            feats(at["d", "up", e, c], wu[:, g, c, :], XT[:, hf, :], dve_drained, dve_filled)
                        if (name, hf) == ("ffn1", 0) and e - 1 in VALUE_DISTANCES:
                            weighted(1, VALUE_DISTANCES[e - 1])
                        if e:
                            down(e - 1)
                    if part == "body2":
                        if (name, hf) == ("ffn1", 0):
                            weighted(1, VALUE_DISTANCES[E - 1])
                        down(E - 1)

                if name == "att2" and part == "head":
                    inputs(name, hf, at)
                    pe.wait_ge(act_drained, at["a", "xt"].drained)
                    gw = sm("mgw").rearrange("p (k m) -> p k m", k=3)
                    b_ = bank(at["d", "gates"], dve_drained)
                    mm(b_[0:64, :], gw[:, 0, :], XT[:, hf, :], start=True)
                    mm(b_[0:64, :], gw[:, 1, :], CT[:, hf, :], start=False)
                    mm(b_[0:64, :], gw[:, 2, :], CT[:, hf, :], start=False, stop=True).then_inc(dve_filled, 1)
                if name == "att2" and part[:4] == "body":
                    if part == "body1":
                        b_ = bank(at["d", "cols"], dve_drained)
                        pe.wait_ge(rows_ready, seen(rows_ready))
                        pe.wait_ge(em_ready, seen(em_ready))
                        for k, src in enumerate((row[2], row[0])):
                            for t in range(T):
                                last = mm(b_[:, (k * T + t) * MH:(k * T + t + 1) * MH], src[:, t * P:(t + 1) * P],
                                          ident[0:MH, 0:MH], start=True, stop=True)
                        last.then_inc(dve_filled, 1)
                        if hf == 0:
                            pe.wait_ge(v33_done, 1)
                    g = int(part == "body2")
                    sel = few("sel", MH * P).rearrange("p (h m) -> p h m", h=MH)

                    def values(h, b):
                        turn = at["s", "outT", g]
                        if (h, b) == (2 * g, 0):
                            clear(turn, score_drained)
                        pe.wait_ge(dve_drained, at["d", "scores", h, b].drained)
                        c_ = cmat[b]
                        o_, c0 = BANK[turn.bank][64 * (h % 2):64 * (h % 2) + MD + 1, :], S * b
                        mm(o_[:, c0:c0 + S], V33[:, hf, 2 * b, h, :], c_[:, 0:S], start=False)
                        last = mm(o_[:, c0 + P:c0 + S], V33[:, hf, 2 * b + 1, h, :], c_[:, S:S + P], start=False, stop=True)
                        if (h, b) == (2 * g + 1, NB - 1):
                            last.then_inc(score_filled, 1)

                    def rows(h):
                        mm(bank(at["d", "rows", h], dve_drained), sel[:, h, :], negrun[hf], start=True, stop=True)\
                            .then_inc(dve_filled, 1)

                    if part == "body1":
                        rows(0)
                        rows(1)
                    for h in body_heads(part):
                        hs = slice(MD * h, MD * (h + 1))
                        for b in range(NB):
                            b_ = bank(at["d", "scores", h, b], dve_drained)
                            k0, k1, k2 = b * S, b * S + P, (b + 1) * S
                            mm(b_[:, 0:S], CT[hs, hf, k0:k1], XT[hs, hf, k0:k2], start=True, stop=True)
                            mm(b_[:, S:S + P], CT[hs, hf, k1:k2], XT[hs, hf, k1:k2], start=True, stop=True)\
                                .then_inc(dve_filled, 1)
                            if b:
                                values(h, b - 1)
                            elif h % 2:
                                values(h - 1, NB - 1)
                    if part == "body1":
                        rows(2)
                    values(2 * g + 1, NB - 1)
                    if part == "body1":
                        rows(3)
                    turn = at["s", "outT", g]
                    blocks_turned(at["o", "out", g], outT[g], (score_drained, turn.drained))

                if name == "att3" and part == "head":
                    feats(at["d", "k"], sm("rwk"), CT[:, hf, :], dve_drained, dve_filled)
                    feats(at["d", "ks"], sm("rwks"), CT[:, hf, :], dve_drained, dve_filled)
                    tokens(at["a", "v"], CT[:, hf, :], sm("rwv"), D, (act_drained, act_filled))
                    inputs(name, hf, at)
                    pe.wait_ge(act_drained, at["a", "xt"].drained)
                    feats(at["d", "q"], sm("rwq"), XT[:, hf, :], dve_drained, dve_filled)
                    feats(at["d", "qs"], sm("rwqs"), XT[:, hf, :], dve_drained, dve_filled)
                    tokens(at["d", "gate"], XT[:, hf, :], sm("rgw"), D)
                if name == "att3" and part[:4] == "body":
                    if part == "body1":
                        pe.wait_ge(stacked_k[hf], 2 * 16 * len(RUNS_B))
                        pe.wait_ge(stacked_q[hf], 2 * 16 * len(RUNS_A))

                    def retained(b, p_):
                        turn = at["s", "outT", b, p_ // 4]
                        if p_ % 4 == 0:
                            clear(turn, score_drained)
                        pe.wait_ge(dve_drained, at["d", "diag", b, p_].drained)
                        pe.wait_ge(act_drained, at["a", "off", b, p_ // 2].drained)
                        for k in range(2):
                            h = 2 * p_ + k
                            off = gated[:, (p_ // 2) % 2, :].rearrange("p (h i) -> p h i", h=4)[:, h % 4, :]
                            d_ = diag[p_ % 3]
                            hs = slice(HD * h, HD * (h + 1))
                            o_, c0 = BANK[turn.bank][32 * (h % 4):32 * (h % 4) + HD, :], S * (h // 4 % 2)
                            mm(o_[:, c0:c0 + P], V3[hf][:, 2 * b, hs], d_[:, k, 0, :], start=False)
                            mm(o_[:, c0 + P:c0 + S], V3[hf][:, 2 * b, hs], off, start=False)
                            last = mm(o_[:, c0 + P:c0 + S], V3[hf][:, 2 * b + 1, hs], d_[:, k, 1, :], start=False, stop=True)
                        if p_ % 4 == 3:
                            last.then_inc(score_filled, 1)

                    def token_major(b, g):
                        turn = at["s", "outT", b, g]
                        blocks_turned(at["o", "out", b, g], outT[g], (score_drained, turn.drained))

                    b = int(part == "body2")
                    k0, k1, k2 = b * S, b * S + P, (b + 1) * S
                    for p_ in range(H // 2 + 2):
                        if (part, hf, p_) == PROJECT_0:
                            project(0)
                        if p_ < H // 2 and p_ % 2 == 0:
                            b_ = bank(at["a", "off", b, p_ // 2], act_drained)
                            for k in range(4):
                                h = 2 * p_ + k
                                last = mm(b_[:, k * P:(k + 1) * P], k6[hf][:, h, k0:k1], q6[hf][:, h, k1:k2],
                                          start=True, stop=True)
                            last.then_inc(act_filled, 1)
                        if p_ < H // 2:
                            b_ = bank(at["d", "diag", b, p_], dve_drained)
                            for k in range(2):
                                h = 2 * p_ + k
                                mm(b_[:, 2 * k * P:(2 * k + 1) * P], k6[hf][:, h, k0:k1], q6[hf][:, h, k0:k1],
                                   start=True, stop=True)
                                last = mm(b_[:, (2 * k + 1) * P:(2 * k + 2) * P], k6[hf][:, h, k1:k2],
                                          q6[hf][:, h, k1:k2], start=True, stop=True)
                            last.then_inc(dve_filled, 1)
                        if p_ >= 2:
                            retained(b, p_ - 2)
                        if p_ == 7:
                            token_major(b, 0)
                    token_major(b, 1)
                if name == "att3" and part == "tail" and hf == 1:
                    project(1)

                if name[:3] == "moe":
                    l = int(name[3])
                    w_ = w3[l % 2]
                    wa = w_[:, 0:W3["w1"][1]].rearrange("p (e c f) -> p e c f", e=E3, c=F0)
                    wb = w_[:, W3["w2"][0]:].rearrange("p (e c d) -> p e c d", e=E3, c=F0)

                    def down(e):
                        second(at["o", "y", e], F0, lambda c: wb[:, e, c, :], e % 2, act_drained,
                               at["a", "h", e, F0 - 1].drained)

                    if part == "head":
                        if l == 0 and hf == 0:
                            pe.wait_ge(score_drained, turns["scores drained"])
                        pe.wait_ge(norm_done[hf], NORM[name])
                        turn_tiles(at["a", "xt"], XN[:, hf, :, :] if l == 0 else Z[l % 2][hf])
                        turn_tiles(at["a", "xh"], XH[:, hf, :, :])
                        if l == 0:
                            moe_logits(name, hf)
                    if part == "body1" and hf == 0:
                        pe.wait_ge(w3_loaded[l % 2], 16 * (l // 2 + 1))
                    for e in body_experts(name, part):
                        pe.wait_ge(xe_ready, seen(xe_ready))
                        for c in range(F0):
                            feats(at["a", "h", e, c], wa[:, e, c, :], xe_of[hf][e % 2], act_drained, act_filled)
                            if part == "body2" and (e, c) == (2, 0) and before[0] == "head":
                                moe_logits(*before[1:])
                            if (e, c) == (1, 1):
                                pe.wait_ge(dve_drained, at["d", "combT"].drained)
                                tokens(at["d", "bias"], combT, few("b2", L3 * D)[:, l * D:(l + 1) * D], D)
                        if e == 0:
                            b_ = bank(at["d", "combT"], dve_drained)
                            pe.wait_ge(comb_ready, seen(comb_ready))
                            for t in range(T):
                                last = mm(b_[0:E3, t * P:(t + 1) * P], combs[hf][:, t * E3:(t + 1) * E3], ident,
                                          start=True, stop=True)
                            last.then_inc(dve_filled, 1)
                        else:
                            down(e - 1)
                    if part == "body2":
                        down(E3 - 1)
                before = (part, name, hf)

        @block.vector
        def _(dve):
            seen = Tally()

            def settle(last):
                last.then_inc(step, 1)
                dve.wait_ge(step, seen(step))

            def rsqrt(last):
                last.then_inc(var_ready, 1)
                dve.wait_ge(rstd_ready, seen(rstd_ready))

            def layernorm(src, dst):
                for t in range(T):
                    last = dve.bn_stats(st6[:, t, :], src[:, t, :])
                settle(last)
                for t in range(T):
                    last = dve.bn_aggr(mv[:, t, :], st6[:, t, :])
                settle(last)
                rsqrt(dve.tensor_scalar(VE[:, 0:T], mv[:, :, 1], 1e-5, None, ALU.add))
                for t in range(T):
                    last = dve.tensor_scalar(dst[:, t, :], src[:, t, :], mv[:, t, 0:1], RS[:, t:t + 1],
                                             ALU.subtract, ALU.mult)
                return last

            n_parts = 0

            def split(src, out_sem):
                nonlocal n_parts
                buf = n_parts % 2
                if n_parts >= 2:
                    dve.wait_ge(parts_out[buf], 16 * (n_parts // 2))
                n_parts += 1
                part = parts[buf]
                settle(dve.tensor_copy(part[:, 0, :], src))
                settle(dve.tensor_tensor(ftmp, src, part[:, 0, :], ALU.subtract))
                settle(dve.tensor_copy(part[:, 1, :], ftmp))
                dve.tensor_tensor(part[:, 2, :], ftmp, part[:, 1, :], ALU.subtract).then_inc(out_sem, 1)

            def bc(ap, shape, axis):
                return ap.unsqueeze(axis).broadcast_to(shape)

            def take(turn):
                dve.wait_ge(dve_filled, turn.filled)
                return BANK[turn.bank]

            def drained(last, turn):
                last.then_inc(dve_drained, 1)
                dve.wait_ge(dve_drained, turn.drained)

            def beaten(comb, E):
                K = lg[:, 0:T * E].rearrange("p (t e) -> p t e", t=T)
                n = T * E * E
                gt = rt[:, 0:n].rearrange("p (t e f) -> p t e f", t=T, e=E)
                eq = rt[:, T * 64:T * 64 + n].rearrange("p (t e f) -> p t e f", t=T, e=E)
                mine = bc(K, [P, T, E, E], 3)
                other = bc(K, [P, T, E, E], 2)
                low = bc(sm("low").rearrange("p (e f) -> p e f", e=8)[:, 0:E, 0:E], [P, T, E, E], 1)
                dve.tensor_tensor(gt, other, mine, ALU.is_gt)
                settle(dve.tensor_tensor(eq, other, mine, ALU.is_equal))
                settle(dve.tensor_tensor(eq, eq, low, ALU.mult))
                settle(dve.tensor_tensor(gt, gt, eq, ALU.add))
                settle(dve.tensor_reduce(comb[:, 0:T * E].rearrange("p (t e) -> p t e", t=T), gt, AX, ALU.add))

            def top2_of_sigmoids(comb, E):
                beaten(comb, E)
                C = comb[:, 0:T * E].rearrange("p (t e) -> p t e", t=T)
                dve.wait_ge(weights_ready, seen(weights_ready))
                settle(dve.scalar_tensor_tensor(comb[:, 0:T * E], comb[:, 0:T * E], 1.5, pr[:, 0:T * E], ALU.is_lt, ALU.mult))
                settle(dve.tensor_reduce(rs4[:, 0:T], C, AX, ALU.add))
                settle(dve.tensor_scalar(rs4[:, 0:T], rs4[:, 0:T], 1e-8, None, ALU.add))
                settle(dve.reciprocal(rs4[:, T:2 * T], rs4[:, 0:T]))
                settle(dve.tensor_tensor(C, C, bc(rs4[:, T:2 * T], [P, T, E], 2), ALU.mult))

            def top2_of_softmax(comb, E):
                n = T * E
                K = lg[:, 0:n].rearrange("p (t e) -> p t e", t=T)
                settle(dve.tensor_reduce(rs4[:, 0:T], K, AX, ALU.max))
                settle(dve.tensor_tensor(K, K, bc(rs4[:, 0:T], [P, T, E], 2), ALU.subtract))
                beaten(comb, E)
                settle(dve.tensor_scalar(comb[:, 0:n], comb[:, 0:n], 1.5, None, ALU.is_lt))
                settle(dve.tensor_tensor(rt[:, 0:n], comb[:, 0:n], lg[:, 0:n], ALU.mult))
                settle(dve.tensor_reduce(rs4[:, 0:T], rt[:, 0:n].rearrange("p (t e) -> p t e", t=T), AX, ALU.add))
                settle(dve.tensor_scalar(rs4[:, 0:T], rs4[:, 0:T], 0.5, None, ALU.mult))
                dve.tensor_tensor(K, K, bc(rs4[:, 0:T], [P, T, E], 2), ALU.subtract).then_inc(logits_ready, 1)

            def softmax_weights(comb, E):
                n = T * E
                dve.wait_ge(weights_ready, seen(weights_ready))
                settle(dve.tensor_scalar(pr[:, 0:n], pr[:, 0:n], 0.5, 0.5, ALU.mult, ALU.add))
                return dve.tensor_tensor(comb[:, 0:n], comb[:, 0:n], pr[:, 0:n], ALU.mult)

            def residual(name, hf, src, tiles=slice(0, T)):
                g = GATE[name]
                return dve.scalar_tensor_tensor(X[:, hf, tiles, :], src, TG[:, g:g + 1], X[:, hf, tiles, :],
                                                ALU.mult, ALU.add)

            def distance_scores(hf, distances):
                sc1 = sc1_of[hf]
                if distances[0] == 0:
                    settle(dve.memset(sc1, NEG))
                for dl in distances:
                    if dl in OWN_DISTANCES[hf]:
                        w = D - HD * dl
                        settle(dve.tensor_tensor(own[:, :, 0:w], XN[:, hf, :, HD * dl:D], CX[:, hf, :, 0:w], ALU.mult))
                        settle(dve.tensor_reduce(sc1[:, :, dl:H, dl], own[:, :, 0:w].rearrange("p t (h e) -> p t h e", e=HD),
                                                 AX, ALU.add))
                        continue
                    dve.wait_ge(prod_ready, seen(prod_ready))
                    pb = sprod[shared(hf).index(dl) % 4][:, :, 0:D - HD * dl].rearrange("p t (h e) -> p t h e", e=HD)
                    dve.tensor_reduce(sc1[:, :, dl:H, dl], pb, AX, ALU.add).then_inc(prod_used, 1)
                dve.wait_ge(prod_used, seen(prod_used, sum(dl not in OWN_DISTANCES[hf] for dl in distances)))

            def weighted(hf, distances):
                cx, sc1 = CX[:, hf, :, :], sc1_of[hf]
                for dl in distances:
                    w = D - HD * dl
                    if dl >= len(prod1):
                        dve.wait_ge(av1_used, (H - 1) * hf + dl - len(prod1) + 1)
                    dve.tensor_tensor(prod1[dl % len(prod1)][:, :, 0:w].rearrange("p t (h e) -> p t h e", e=HD),
                                      cx[:, :, 0:w].rearrange("p t (h e) -> p t h e", e=HD),
                                      bc(sc1[:, :, dl:H, dl], [P, T, H - dl, HD], 3), ALU.mult).then_inc(av1_ready, 1)

            def mlstm_gates(stage, hf):
                fg, ig = grow[32:32 + MH, :], grow[0:MH, :]
                batches = [slice(b * S, (b + 1) * S) for b in range(NB)]
                if stage == 0:
                    last = dve.tensor_scalar(row[3], fg, 0.0, None, ALU.min)
                elif stage == 1:
                    begin()
                    dve.wait_ge(flog_ready, hf + 1)
                    last = dve.tensor_tensor(row[3], row[3], row[1], ALU.subtract)
                elif stage == 2:
                    begin()
                    for bs in batches:
                        last = dve.tensor_tensor_scan(row[0][:, bs], row[3][:, bs], row[3][:, bs], 0.0, ALU.add, ALU.bypass)
                elif stage == 3:
                    begin()
                    last = dve.tensor_tensor(row[2], ig, row[0], ALU.subtract)
                elif stage == 4:
                    begin()
                    for bs in batches:
                        last = dve.tensor_tensor_scan(row[3][:, bs], row[2][:, bs], row[2][:, bs], -3e38, ALU.max, ALU.max)
                else:
                    begin()
                    dve.tensor_tensor(row[0], row[0], row[3], ALU.add).then_inc(emarg_ready, 1)
                    dve.tensor_scalar(negrun[hf], row[3], -1.0, None, ALU.mult).then_inc(rows_ready, 1)
                    return
                last.then_inc(step, 1)
                seen(step)

            def mlstm_values(g, hf):
                n_ = sums[:, 0:T * MH].rearrange("p (t h) -> p t h", t=T)[:, :, 2 * g:2 * g + 2]
                turn = turns["att2", hf, "o", "out", g]
                dve.wait_ge(out_filled, turn.filled)
                o_ = BANK[turn.bank].rearrange("p (t k e) -> p t k e", t=T, k=2)
                settle(dve.tensor_tensor(n_, o_[:, :, :, MD], em_tok[hf][:, :, 2 * g:2 * g + 2], ALU.max))
                settle(dve.tensor_scalar(n_, n_, 1e-6, None, ALU.add))
                settle(dve.reciprocal(n_, n_))
                dve.tensor_tensor(mout[:, :, 2 * g:2 * g + 2, :], o_[:, :, :, 0:MD], bc(n_, [P, T, 2, MD], 3),
                                  ALU.mult).then_inc(out_drained, 1)
                dve.wait_ge(out_drained, turn.drained)

            def begin():
                dve.wait_ge(step, seen.last(step))

            def mlstm_norm(stage, hf):
                flat_n = sums[:, 0:T * MH]
                n_ = flat_n.rearrange("p (t h) -> p t h", t=T)
                m3 = mout.rearrange("p t h e -> p (t h) e")
                if stage == 0:
                    mlstm_values(1, hf)
                    last = dve.tensor_tensor(msq, mout, mout, ALU.mult)
                elif stage == 1:
                    begin()
                    last = dve.tensor_reduce(n_, msq, AX, ALU.add)
                elif stage == 2:
                    begin()
                    dve.tensor_scalar(VE[:, 0:T * MH], flat_n, 1.0 / MD, 1e-6, ALU.mult, ALU.add).then_inc(var_ready, 1)
                    last = dve.tensor_scalar(rms1[:, :], sm("rms"), 1.0, None, ALU.add)
                elif stage == 3:
                    begin()
                    dve.wait_ge(rstd_ready, seen(rstd_ready))
                    last = dve.tensor_tensor(mout, mout, bc(RS[:, 0:T * MH].rearrange("p (t h) -> p t h", t=T),
                                                            [P, T, MH, MD], 3), ALU.mult)
                elif stage == 4:
                    begin()
                    last = dve.tensor_tensor(m3, m3, bc(rms1[:, :], [P, T * MH, MD], 1), ALU.mult)
                else:
                    begin()
                    last = residual("att2", hf, mout.rearrange("p t h e -> p t (h e)"))
                last.then_inc(step, 1)
                seen(step)

            def retention_norm(stage, hf):
                ret = rets[hf]
                flat_mu = sums[:, 0:T * H]
                mu = flat_mu.rearrange("p (t h) -> p t h", t=T)
                if stage == 0:
                    dve.wait_ge(out_drained, turns["att3", hf, "o", "out", 1, 1].drained)
                else:
                    begin()
                if stage == 0:
                    last = dve.tensor_reduce(mu, ret, AX, ALU.add)
                elif stage == 1:
                    last = dve.tensor_scalar(flat_mu, flat_mu, 1.0 / HD, None, ALU.mult)
                elif stage == 2:
                    last = dve.tensor_tensor(ret, ret, bc(mu, [P, T, H, HD], 3), ALU.subtract)
                elif stage == 3:
                    last = dve.tensor_tensor(retsq, ret, ret, ALU.mult)
                elif stage == 4:
                    last = dve.tensor_reduce(mu, retsq, AX, ALU.add)
                elif stage == 5:
                    dve.tensor_scalar(VE[:, 0:T * H], flat_mu, 1.0 / HD, 1e-5, ALU.mult, ALU.add)\
                       .then_inc(headvar_ready, 1)
                    return
                elif stage == 6:
                    v, r, c = VE[:, 0:T * H], RS[:, 0:T * H], flat_mu
                    dve.wait_ge(headsqrt_ready, hf + 1)
                    settle(dve.reciprocal(r, r))
                    settle(dve.tensor_tensor(c, v, r, ALU.mult))
                    settle(dve.tensor_tensor(c, c, r, ALU.mult))
                    settle(dve.tensor_scalar(c, c, -0.5, 1.5, ALU.mult, ALU.add))
                    settle(dve.tensor_tensor(r, r, c, ALU.mult))
                    last = dve.tensor_tensor(ret, ret, bc(RS[:, 0:T * H].rearrange("p (t h) -> p t h", t=T),
                                                          [P, T, H, HD], 3), ALU.mult)
                else:
                    dve.wait_ge(gate3_ready, hf + 1)
                    dve.tensor_tensor(y3, ret.rearrange("p t h e -> p (t h e)"), gates3[hf], ALU.mult)\
                       .then_inc(y3_ready, 1)
                    return
                last.then_inc(step, 1)
                seen(step)

            def projected(stage, hf):
                x, xn, xh = X[:, hf, :, :], XN[:, hf, :, :], XH[:, hf, :, :]
                turn = turns["att3", hf, "d", "proj"]
                if stage == 0:
                    dve.wait_ge(y3_ready, hf + 1)
                    dve.tensor_tensor(gates3[hf], take(turn).rearrange("p (t d) -> p t d", t=T),
                                      bc(sm("rob"), [P, T, D], 1), ALU.add).then_inc(dve_drained, 1)
                    return
                if stage == 1:
                    dve.wait_ge(dve_drained, turn.drained)
                    last = residual("att3", hf, gates3[hf])
                else:
                    begin()
                    last = norm_stage((stage - 2) % 4, *((x, xn) if stage < 6 else (xn, xh)))
                if stage in (4, 8):
                    last.then_inc(var_ready, 1)
                    return
                if stage == 9:
                    last.then_inc(norm_done[hf], 1)
                    return
                last.then_inc(step, 1)
                seen(step)

            def norm_beside(stage, *work):
                if work not in NORM_BESIDE:
                    return
                h2 = NORM_BESIDE[work][1]
                begin()
                last = norm_stage(stage, X[:, h2, :, :], XN[:, h2, :, :])
                if stage == 2:
                    last.then_inc(var_ready, 1)
                elif stage == 3:
                    last.then_inc(norm_done[h2], 1)
                else:
                    last.then_inc(step, 1)
                    seen(step)

            def norm_stage(stage, src, dst):
                if stage == 0:
                    for t in range(T):
                        last = dve.bn_stats(st6[:, t, :], src[:, t, :])
                elif stage == 1:
                    for t in range(T):
                        last = dve.bn_aggr(mv[:, t, :], st6[:, t, :])
                elif stage == 2:
                    last = dve.tensor_scalar(VE[:, 0:T], mv[:, :, 1], 1e-5, None, ALU.add)
                else:
                    dve.wait_ge(rstd_ready, seen(rstd_ready))
                    for t in range(T):
                        last = dve.tensor_scalar(dst[:, t, :], src[:, t, :], mv[:, t, 0:1], RS[:, t:t + 1],
                                                 ALU.subtract, ALU.mult)
                return last

            for hf in range(2):
                dve.wait_ge(x_loaded[hf], 16)
                layernorm(X[:, hf, :, :], XN[:, hf, :, :]).then_inc(norm_done[hf], 1)
                if hf == 0:
                    dve.wait_ge(small_loaded, 16)
                    er = few("er", 384)
                    settle(dve.tensor_copy(erp[:, 0, :], er))
                    settle(dve.tensor_tensor(erf[:, :], er, erp[:, 0, :], ALU.subtract))
                    settle(dve.tensor_copy(erp[:, 1, :], erf[:, :]))
                    dve.tensor_tensor(erp[:, 2, :], erf[:, :], erp[:, 1, :], ALU.subtract).then_inc(er_parts, 1)
            dve.wait_ge(tanh_done, 1)

            for part, name, hf in steps:
                at = {k[2:]: v for k, v in turns.items() if k[:2] == (name, hf)}

                if name == "att0" and part == "head":
                    turn = at["d", "q"]
                    drained(dve.tensor_scalar(fval, take(turn), sm("bq"), HD ** -0.5, ALU.add, ALU.mult), turn)
                    split(fval, parts_ready)
                    turn = at["d", "k"]
                    drained(dve.tensor_scalar(fval, take(turn), sm("bk"), None, ALU.add), turn)
                    split(fval, parts_ready)
                    turn = at["d", "v"]
                    drained(dve.tensor_tensor(V9[:, hf, :, :, 0:HD],
                                              take(turn).rearrange("p (t h e) -> p t h e", t=T, h=H),
                                              bc(sm("bv").rearrange("p (h e) -> p h e", h=H), [P, T, H, HD], 1),
                                              ALU.add), turn)
                if name == "att0" and part == "body1":
                    if hf == 0:
                        dve.wait_ge(mask_loaded, 16)
                    for c in range(16):
                        turn = at["d", "rel", c]
                        dve.tensor_tensor(relD[:, :, 8 * c:8 * (c + 1)],
                                          take(turn).rearrange("p (u c) -> p c u", c=64),
                                          bc(addmask[:, 8 * c:8 * (c + 1)], [P, 64, 8], 1), ALU.add)\
                           .then_inc(dve_drained, 1)
                        if c % 4 == 3:
                            norm_beside(c // 4, part, name, hf)
                if name == "att0" and part == "body2":
                    def finish(g):
                        b, g2 = divmod(g, 2)
                        turn = at["o", "out", g]
                        dve.wait_ge(out_filled, turn.filled)
                        o_ = BANK[turn.bank].rearrange("p (c t a e) -> p c t a e", c=2, t=2, a=4)
                        inv = sums[:, 0:16].rearrange("p (c t a) -> p c t a", c=2, t=2)
                        settle(dve.reciprocal(inv, o_[:, :, :, :, HD]))
                        for c in range(2):
                            h0 = 8 * g2 + 4 * c
                            dst = pad[:, 2 * b:2 * b + 2, HD * h0:HD * (h0 + 4)].rearrange("p t (a e) -> p t a e", a=4)
                            last = dve.tensor_tensor(dst, o_[:, c, :, :, 0:HD], bc(inv[:, c, :, :], [P, 2, 4, HD], 3),
                                                     ALU.mult)
                        last.then_inc(out_drained, 1)

                    for i in range(NB * H + 3):
                        if i < NB * H:
                            turn = at["s", "scores", i]
                            dve.wait_ge(score_filled, turn.filled)
                            dve.tensor_reduce(negmax[:, i % 4, 0:1], BANK[turn.bank][:, 0:P], AX, ALU.max, negate=True)
                            dve.tensor_reduce(negmax[:, i % 4, 1:2], BANK[turn.bank][:, P:3 * P], AX, ALU.max,
                                              negate=True).then_inc(negmax_ready, 1)
                        if i >= 3:
                            turn = at["d", "probs", i - 3]
                            dve.tensor_copy(probsT[(i - 3) % 4], take(turn)[:, 0:3 * P]).then_inc(dve_drained, 1)
                        if i >= 17 and (i - 17) % 8 == 0:
                            finish((i - 17) // 8)
                    finish(3)
                    dve.wait_ge(out_drained, at["o", "out", 3].drained)
                    settle(residual(name, hf, pad))

                if name == "ffn0" and part == "head":
                    comb = combs[hf]
                    turn = at["d", "logits"]
                    b_ = take(turn)[:, 0:2 * T].rearrange("p (t e) -> p t e", e=2)
                    settle(dve.tensor_copy(lg[:, 0:T], b_[:, :, 1]))
                    drained(dve.tensor_tensor(comb[:, 0:T], b_[:, :, 0], lg[:, 0:T], ALU.is_ge), turn)
                    for t in range(T):
                        last = dve.tensor_scalar(msk[hf][0][:, t, :], XN[:, hf, t, :], comb[:, t:t + 1], None, ALU.mult)
                    last.then_inc(masked_ready, 1)
                    dve.wait_ge(masked_ready, seen(masked_ready))
                    dve.tensor_tensor(msk[hf][1], XN[:, hf, :, :], msk[hf][0], ALU.subtract).then_inc(masked_ready, 1)
                    seen(masked_ready)
                if name == "ffn0" and part == "body2":
                    turn = at["o", "out"]
                    dve.wait_ge(out_filled, turn.filled)
                    residual(name, hf, BANK[turn.bank].rearrange("p (t d) -> p t d", t=T)).then_inc(out_drained, 1)
                    dve.wait_ge(out_drained, turn.drained)

                if part == "scores":
                    if hf == 0:
                        dve.wait_ge(ctx_loaded, 32)
                        distance_scores(hf, range(H))
                    sc1 = sc1_of[hf]
                    mx = sums[:, 0:T * H].rearrange("p (t h) -> p t h", t=T)
                    settle(dve.tensor_reduce(mx, sc1, AX, ALU.max))
                    dve.tensor_tensor(sc1, sc1, bc(mx, [P, T, H, H], 3), ALU.subtract).then_inc(shifted1, 1)
                    dve.wait_ge(expd1, seen(expd1))
                    settle(dve.tensor_reduce(mx, sc1, AX, ALU.add))
                    settle(dve.reciprocal(mx, mx))
                    settle(dve.tensor_tensor(sc1, sc1, bc(mx, [P, T, H, H], 3), ALU.mult))
                if name == "att1" and part == "body1":
                    weighted(hf, range(H))
                if name == "att1" and part == "body2":
                    turn = at["s", "out"]
                    dve.wait_ge(score_filled, turn.filled)
                    residual(name, hf, BANK[turn.bank].rearrange("p (t d) -> p t d", t=T)).then_inc(score_drained, 1)
                    dve.wait_ge(score_drained, turn.drained)

                if name in ("ffn1", "ffn2"):
                    E, C = EXPERTS[name], CHUNKS[name]
                    R = E1 if name == "ffn1" else E2
                    comb = combs[hf]
                if name in ("ffn1", "ffn2") and part == "head":
                    turn = at["d", "logits"]
                    K = lg[:, 0:T * R].rearrange("p (t e) -> p t e", t=T)
                    src = take(turn)[:, 0:T * R].rearrange("p (t e) -> p t e", t=T)
                    if name == "ffn1":
                        dve.tensor_tensor(K, src, bc(sm("g1b"), [P, T, R], 1), ALU.add).then_inc(dve_drained, 1)
                        dve.wait_ge(dve_drained, turn.drained)
                        dve.tensor_scalar(K, K, 17.0, -87.0, ALU.min, ALU.max).then_inc(logits_ready, 1)
                        dve.wait_ge(logits_ready, hf + 1)
                        top2_of_sigmoids(comb, R)
                    else:
                        drained(dve.tensor_copy(K, src), turn)
                        top2_of_softmax(comb, R)

                if name in ("ffn1", "ffn2") and part[:4] == "body":
                    def product(e):
                        for c in range(C):
                            u, g = at["d", "up", e, c], at["a", "gate", e, c]
                            k = e * C + c
                            b_ = take(u)
                            dve.wait_ge(act_drained, g.drained)
                            dve.tensor_tensor(hidden[:, e % 2, c, :], b_, gated[:, k % 2, :], ALU.mult)\
                               .then_inc(dve_drained, 1)

                    def gather(e):
                        turn = at["o", "y", e]
                        dve.wait_ge(out_filled, turn.filled)
                        y = BANK[turn.bank].rearrange("p (t d) -> p t d", t=T)
                        g = e if name == "ffn2" else FFN1_ORDER[e]
                        if g == E1 and name == "ffn1":
                            last = dve.tensor_copy(acc, y)
                        else:
                            for t in range(T):
                                w = comb[:, t * R + g:t * R + g + 1]
                                if e == 0:
                                    last = dve.tensor_scalar(acc[:, t, :], y[:, t, :], w, None, ALU.mult)
                                else:
                                    last = dve.scalar_tensor_tensor(acc[:, t, :], y[:, t, :], w, acc[:, t, :],
                                                                    ALU.mult, ALU.add)
                        last.then_inc(out_drained, 1)
                        dve.wait_ge(out_drained, turn.drained)

                    if (name, hf, part) == ("ffn1", 0, "body1"):
                        distance_scores(1, range(0, 1))
                    for e in body_experts(name, part):
                        product(e)
                        if (name, e) == ("ffn2", 0):
                            settle(softmax_weights(comb, R))
                        norm_beside(e % 4, part, name, hf)
                        if (name, hf) == ("ffn1", 0):
                            if e in DISTANCES:
                                distance_scores(1, DISTANCES[e])
                        if (name, hf, part) == ("ffn1", 1, "body2"):
                            mlstm_gates(2 * (e - 4), 0)
                            mlstm_gates(2 * (e - 4) + 1, 0)
                        if (name, hf, part) == ("ffn2", 0, "body1"):
                            if e == 0:
                                mlstm_norm(0, 1)
                            mlstm_norm(e + 1, 1)
                        if (name, hf) == ("ffn1", 0) and e in VALUE_DISTANCES:
                            weighted(1, VALUE_DISTANCES[e])
                        if e:
                            gather(e - 1)
                    if (name, hf, part) == ("ffn2", 0, "body1"):
                        mlstm_norm(5, 1)
                    if part == "body2":
                        gather(E - 1)
                        settle(residual(name, hf, acc))

                if name == "att2" and part == "head":
                    turn = at["d", "gates"]
                    drained(dve.tensor_scalar(grow, take(turn)[0:64, :], sm("mgb", 64), None, ALU.add), turn)
                if name == "att2" and part == "body1":
                    turn = at["d", "cols"]
                    b_ = take(turn)
                    dve.tensor_copy(a_tok[hf][:, :, :], b_[:, 0:T * MH].rearrange("p (t h) -> p t h", t=T))
                    drained(dve.tensor_copy(em_tok[hf][:, :, :], b_[:, T * MH:2 * T * MH].rearrange("p (t h) -> p t h", t=T)), turn)
                if name == "att2" and part[:4] == "body":
                    def exponents(h):
                        turn = at["d", "rows", h]
                        b_ = take(turn)
                        d_ = decay[h]
                        for b in range(NB):
                            t0 = 2 * b
                            dve.scalar_tensor_tensor(d_[:, b, 0:S], b_[:, b * S:(b + 1) * S], a_tok[hf][:, t0, h:h + 1],
                                                     addmask, ALU.add, ALU.min)
                            last = dve.scalar_tensor_tensor(d_[:, b, S:S + P], b_[:, b * S + P:(b + 1) * S],
                                                            a_tok[hf][:, t0 + 1, h:h + 1], addmask[:, 0:P], ALU.add, ALU.min)
                        drained(last, turn)
                        dve.engine_nop().then_inc(dexp_in, 1)

                    if part == "body1":
                        for h in range(2):
                            exponents(h)
                            if hf == 1:
                                mlstm_norm(h, 0)
                    for h in body_heads(part):
                        dve.wait_ge(dexp_ready, seen(dexp_ready))
                        d_ = decay[h]
                        for b in range(NB):
                            turn = at["d", "scores", h, b]
                            dve.scalar_tensor_tensor(cmat[b], take(turn)[:, 0:3 * P], MD ** -0.5, d_[:, b, :],
                                                     ALU.mult, ALU.mult).then_inc(dve_drained, 1)
                            norm_beside(NB * (h % 2) + b, part, name, hf)
                            if (hf, part) == (1, "body1"):
                                mlstm_norm(2 + NB * h + b, 0)
                            if (hf, part) == (0, "body2"):
                                for stage in ((0,), (1,), (2, 3), (4, 5))[NB * (h - 2) + b]:
                                    mlstm_gates(stage, 1)
                    if part == "body1":
                        exponents(2)
                        exponents(3)
                    else:
                        mlstm_values(0, hf)

                if name == "att3" and part == "head":
                    def xpos(w, ws, cos, sin):
                        shape = [P, NB, S]
                        turn = at["d", w]
                        drained(dve.tensor_tensor(fval.rearrange("p (b s) -> p b s", b=NB),
                                                  take(turn).rearrange("p (b s) -> p b s", b=NB),
                                                  bc(sm(cos), shape, 1), ALU.mult), turn)
                        turn = at["d", ws]
                        drained(dve.tensor_tensor(ftmp.rearrange("p (b s) -> p b s", b=NB),
                                                  take(turn).rearrange("p (b s) -> p b s", b=NB),
                                                  bc(sm(sin), shape, 1), ALU.mult), turn)
                        settle(dve.tensor_tensor(fval, fval, ftmp, ALU.add))
                        split(fval, parts_ready)

                    xpos("k", "ks", "kcos", "ksin")
                    xpos("q", "qs", "qcos", "qsin")
                    turn = at["d", "gate"]
                    dve.tensor_tensor(gates3[hf], take(turn).rearrange("p (t d) -> p t d", t=T),
                                      bc(sm("rgb"), [P, T, D], 1), ALU.add).then_inc(dve_drained, 1)
                    dve.wait_ge(dve_drained, turn.drained)
                    dve.engine_nop().then_inc(gate3_in, 1)
                if name == "att3" and part[:4] == "body":
                    def collect(b, g):
                        turn = at["o", "out", b, g]
                        dve.wait_ge(out_filled, turn.filled)
                        o_ = BANK[turn.bank].rearrange("p (c t a e) -> p c t a e", c=2, t=2, a=4)
                        for c in range(2):
                            h0 = 8 * g + 4 * c
                            last = dve.tensor_copy(rets[hf][:, 2 * b:2 * b + 2, h0:h0 + 4, :], o_[:, c, :, :, 0:HD])
                        last.then_inc(out_drained, 1)

                    b = int(part == "body2")
                    for p_ in range(H // 2):
                        turn = at["d", "diag", b, p_]
                        dve.tensor_tensor(diag[p_ % 3].rearrange("p a b i -> p (a b) i"),
                                          take(turn).rearrange("p (a i) -> p a i", a=4),
                                          bc(sm("keep"), [P, 4, P], 1), ALU.mult).then_inc(dve_drained, 1)
                        if p_ % 2:
                            norm_beside(p_ // 2, part, name, hf)
                        if (hf, part) == (1, "body1"):
                            retention_norm(p_, 0)
                        if (part, hf, p_ + 1) == PROJECT_0:
                            projected(0, 0)
                        if (part, hf) == PROJECT_0[0:2] and p_ >= PROJECT_0[2]:
                            k = p_ - PROJECT_0[2]
                            for stage in range(1 + 2 * k, min(3 + 2 * k, 10)):
                                projected(stage, 0)
                    collect(b, 0)
                    collect(b, 1)
                if name[:3] == "moe":
                    l = int(name[3])
                    z = XN[:, hf, :, :] if l == 0 else Z[l % 2][hf]
                    znew = Z[(l + 1) % 2][hf]
                    comb, xe = combs[hf], xe_of[hf]

                    def expert_input(e):
                        if e >= 2:
                            dve.wait_ge(act_filled, at["a", "h", e - 2, F0 - 1].filled)
                        k = l * E3 + e
                        dve.tensor_scalar(xe[e % 2], turned[:, hf, :], sm("lng")[:, k:k + 1], sm("lnb")[:, k:k + 1],
                                          ALU.mult, ALU.add).then_inc(xe_ready, 1)

                if name[:3] == "moe" and part == "head":
                    if (name, hf) == ("moe0", 0):
                        retention_norm(0, 1)
                        retention_norm(1, 1)
                    dve.wait_ge(act_drained, at["a", "xh"].drained)
                    expert_input(0)
                    expert_input(1)
                    turn = at["d", "logits"]
                    K = lg[:, 0:T * E3].rearrange("p (t e) -> p t e", t=T)
                    src = take(turn)[:, 0:T * E3].rearrange("p (t e) -> p t e", t=T)
                    rb = bc(sm("g3b")[:, l * E3:(l + 1) * E3], [P, T, E3], 1)
                    drained(dve.tensor_tensor(K, src, rb, ALU.add), turn)
                    top2_of_softmax(comb, E3)
                    if (name, hf) == ("moe0", 0):
                        for stage in range(2, 6):
                            retention_norm(stage, 1)
                    softmax_weights(comb, E3).then_inc(comb_ready, 1)
                    dve.wait_ge(comb_ready, seen(comb_ready))
                    C = comb[:, 0:T * E3].rearrange("p (t e) -> p t e", t=T)
                    settle(dve.tensor_reduce(csum[hf][:, :], C, AX, ALU.add))
                if name[:3] == "moe" and part == "body1":
                    turn = at["d", "combT"]
                    drained(dve.tensor_copy(combT, take(turn)[0:E3, :]), turn)
                    turn = at["d", "bias"]
                    b_ = take(turn)
                    for t in range(T):
                        last = dve.scalar_tensor_tensor(znew[:, t, :], z[:, t, :], csum[hf][:, t:t + 1], b_[:, t * D:(t + 1) * D],
                                                        ALU.mult, ALU.add)
                    drained(last, turn)
                if name[:3] == "moe" and part[:4] == "body":
                    def gather(e):
                        turn = at["o", "y", e]
                        dve.wait_ge(out_filled, turn.filled)
                        for t in range(T):
                            last = dve.scalar_tensor_tensor(znew[:, t, :], BANK[turn.bank][:, t * D:(t + 1) * D],
                                                            comb[:, t * E3 + e:t * E3 + e + 1], znew[:, t, :],
                                                            ALU.mult, ALU.add)
                        last.then_inc(out_drained, 1)
                        dve.wait_ge(out_drained, turn.drained)

                    for e in body_experts(name, part):
                        if (name, hf, e) == ("moe0", 0, 1):
                            retention_norm(6, 1)
                            retention_norm(7, 1)
                        if e + 2 < E3:
                            expert_input(e + 2)
                        if e:
                            gather(e - 1)
                    if part == "body2":
                        gather(E3 - 1)
                        if l == L3 - 1:
                            residual(name, hf, znew).then_inc(x_done[hf], 1)

                if part == "tail" and (name, hf) not in NORM_BESIDE.values():
                    if name == "att3":
                        if hf == 1:
                            for stage in range(10):
                                projected(stage, 1)
                    elif name[:3] != "moe":
                        if name == "att2":
                            begin()
                        layernorm(X[:, hf, :, :], XN[:, hf, :, :]).then_inc(norm_done[hf], 1)
                    elif name != "moe3":
                        layernorm(znew, XH[:, hf, :, :]).then_inc(norm_done[hf], 1)



def tables():
    j, i = np.arange(P)[:, None], np.arange(P)[None, :]
    c = {"ident": np.eye(P), "ones": np.ones((P, P)), "keep": i >= j}
    c["addmask"] = np.concatenate([np.where(i >= j, 0.0, NEG), np.zeros((P, P))], 1)
    e = np.arange(8)
    c["low"] = np.broadcast_to((e[None, :] < e[:, None]).reshape(1, 64), (P, 64))
    sel = np.zeros((P, MH, P))
    for h in range(MH):
        sel[h, h] = 1
    c["rows"] = sel.reshape(P, MH * P)
    half = HD // 2
    f = np.float32
    base = (np.arange(0, HD, 2, dtype=f) + f(0.4 * HD)) / f(1.4 * HD)
    power = np.arange(-(S // 2), S - S // 2, dtype=f) / f(512.0)
    scale = base[None, :].astype(np.float64) ** power[:, None]
    freq = f(1.0) / f(10000.0) ** (np.arange(half, dtype=f) / f(half))
    ang = (np.arange(S, dtype=f)[:, None] * freq[None, :].astype(f)).astype(np.float64)
    gam = f(1.0) - np.exp(np.linspace(np.log(1.0 / 32.0), np.log(1.0 / 512.0), H)).astype(f)
    pos = np.arange(S)
    sign = np.where(np.arange(HD) % 2 == 0, -1.0, 1.0)
    for w, sc, g in (("q", scale, pos), ("k", 1 / scale, -pos)):
        decay = gam[:, None].astype(np.float64) ** g[None, :]
        cos = np.repeat((np.cos(ang) * sc).T, 2, axis=0)
        sin = np.repeat((np.sin(ang) * sc).T, 2, axis=0) * sign[:, None]
        c[w + "cos"] = (decay[None] * cos[:, None, :]).reshape(P, S)
        c[w + "sin"] = (decay[None] * sin[:, None, :]).reshape(P, S)
    return {k: np.asarray(v, np.float32) for k, v in c.items()}


def pack(columns, n, parts):
    a = np.zeros((P, n), np.float32)
    for name, v in parts.items():
        at, w = columns[name]
        v = v.reshape(v.shape[0], -1)
        assert v.shape[1] == w, (name, v.shape, w)
        a[:v.shape[0], at:at + w] = v
    return a


def layout(i):
    def rows(v):
        return np.broadcast_to(v.reshape(1, -1), (P, v.size))

    def swap(w):
        return np.ascontiguousarray(w.reshape(D, H, HD // 2, 2)[..., ::-1]).reshape(D, D)

    def by_feature(w):
        return w.reshape(-1, H, HD).transpose(0, 2, 1).reshape(-1, D)

    def heads(w):
        return w.transpose(1, 0, 2).reshape(D, D)

    s = dict(tables())
    s["wq"], s["wk"], s["wv"] = by_feature(i["L0_xattn_Wq"].T), by_feature(i["L0_xattn_Wk"].T), i["L0_xattn_Wv"].T
    s["bq"], s["bk"] = by_feature(i["L0_xattn_bq"][None]).T, by_feature(i["L0_xattn_bk"][None]).T
    s["bv"] = rows(i["L0_xattn_bv"])
    s["gates"] = rows(np.concatenate([i["g_xattn"], i["g_ffn"]]))
    s["rows"][ROWS["er"][0]:ROWS["er"][0] + HD, 0:S] = i["L0_xattn_Er"].T
    s["rows"][ROWS["b2"][0]:ROWS["b2"][0] + E3, :] = i["L3_ffn_b2"].transpose(1, 0, 2).reshape(E3, L3 * D)
    s["g0w"], s["g1w"], s["g1b"], s["g2w"] = i["L0_ffn_gate_w"].T, i["L1_ffn_gate_w"].T, rows(i["L1_ffn_gate_b"]), i["L2_ffn_wg"].T
    s["g3w"], s["g3b"] = i["L3_ffn_router_w"].transpose(1, 0, 2), rows(i["L3_ffn_router_b"])
    s["s0b1"] = np.concatenate([i["L0_ffn_b1"], i["L0_ffn_sb1"][None]]).reshape(3, F0, P).transpose(2, 0, 1)
    s["b2s"] = np.concatenate([i["L0_ffn_b2"], i["L0_ffn_sb2"][None]])
    s["rms"] = rows(i["L2_xattn_rms_scale"])
    mg = np.zeros((D, 3, 64), np.float32)
    mg[:, :, 0:MH] = i["L2_xattn_igate_kernel"].reshape(3, D, MH).transpose(1, 0, 2)
    mg[:, :, 32:32 + MH] = i["L2_xattn_fgate_kernel"].reshape(3, D, MH).transpose(1, 0, 2)
    s["mgw"] = mg
    mb = np.zeros((P, 1), np.float32)
    mb[0:MH, 0], mb[32:32 + MH, 0] = i["L2_xattn_igate_bias"], i["L2_xattn_fgate_bias"]
    s["mgb"] = mb
    s["lng"], s["lnb"] = i["L3_ffn_ln_g"].reshape(L3 * E3, D).T, i["L3_ffn_ln_b"].reshape(L3 * E3, D).T
    s["b1"] = i["L3_ffn_b1"].reshape(L3 * E3 * F0, P).T
    wq, wk = heads(i["L3_xattn_W_Q"]), heads(i["L3_xattn_W_K"])
    s["rwq"], s["rwqs"], s["rwk"], s["rwks"] = (by_feature(w) for w in (wq, swap(wq), wk, swap(wk)))
    s["rwv"] = heads(i["L3_xattn_W_V"])
    s["rgw"], s["rgb"], s["row"], s["rob"] = i["L3_xattn_g_w"].T, rows(i["L3_xattn_g_b"]), i["L3_xattn_out_w"].T, rows(i["L3_xattn_out_b"])
    small = pack(SMALL, NSMALL, s)
    w0 = pack(W0, NW0, {
        "w1": np.concatenate([i["L0_ffn_w1"], i["L0_ffn_sw1"][None]]).transpose(1, 0, 2),
        "w2": np.concatenate([i["L0_ffn_w2"], i["L0_ffn_sw2"][None]]).reshape(3, F0, P, D).transpose(2, 0, 1, 3)})
    w1 = pack(W1, NW1, {
        "w1": np.concatenate([i["L1_ffn_ew1"], i["L1_ffn_fc1"][None]]).transpose(2, 0, 1),
        "w3": np.concatenate([i["L1_ffn_ew3"], i["L1_ffn_fc2"][None]]).transpose(2, 0, 1),
        "w2": np.concatenate([i["L1_ffn_ew2"], i["L1_ffn_fc3"][None]]).transpose(2, 0, 1)})
    w2 = pack(W2, NW2, {
        "w1": i["L2_ffn_w1"].transpose(2, 0, 1), "w3": i["L2_ffn_w3"].transpose(2, 0, 1),
        "w2": i["L2_ffn_w2"].transpose(2, 0, 1).reshape(I2, P, E2, D).transpose(1, 2, 0, 3)})
    w3 = np.stack([pack(W3, NW3, {
        "w1": i["L3_ffn_w1"][l].transpose(1, 0, 2),
        "w2": i["L3_ffn_w2"][l].reshape(E3, F0, P, D).transpose(2, 0, 1, 3)}) for l in range(L3)])
    return {"x": i["x"].reshape(2 * HALF, D), "ctx": i["ctx_1024"].reshape(2 * HALF, D),
            "ctxT": i["ctx_1024"].reshape(2 * HALF, D).T, "small": small, "w0": w0, "w1": w1, "w2": w2, "w3": w3}


def kernel(**inputs):
    import concourse.bacc as bacc
    from concourse.bass_utils import run_bass_kernel_spmd

    arrays = {k: np.ascontiguousarray(v) for k, v in layout({k: np.asarray(v) for k, v in inputs.items()}).items()}
    nc = bacc.Bacc("TRN2", target_bir_lowering=False, num_devices=1)
    args = [nc.dram_tensor(f"{k}_dram", v.shape, F32, kind="ExternalInput").ap() for k, v in arrays.items()]
    out = nc.dram_tensor("out_dram", (2 * HALF, D), F32, kind="ExternalOutput").ap()
    build(nc, *args, out)
    r = run_bass_kernel_spmd(nc, [{f"{k}_dram": v for k, v in arrays.items()}], core_ids=[0])
    return r.results[0]["out_dram"].reshape(4, S, D)
```
